# Optimizing a Trainium2 kernel written in Bass

```python
import numpy as np
import jax
import jax.numpy as jnp

def _softmax(x, axis=-1):
    return jax.nn.softmax(x, axis=axis)

def _gelu(x):
    return jax.nn.gelu(x, approximate=True)

def _silu(x):
    return jax.nn.silu(x)

def _sigmoid(x):
    return jax.nn.sigmoid(x)

def _layernorm(x, axis=-1, eps=1e-05):
    m = jnp.mean(x, axis=axis, keepdims=True)
    v = jnp.var(x, axis=axis, keepdims=True)
    return (x - m) / jnp.sqrt(v + eps)

def _scatter_add(tgt, idx, src, axis=0):
    return tgt.at[idx].add(src)

def _segment_sum(src, seg, n):
    return jax.ops.segment_sum(src, seg, n)
kernel_name = 'mk_perceiver_d2_seqx_r4_09e98b'

def setup_inputs(seed: int=0):
    np.random.seed(seed)
    _w = jnp.asarray

    def _rec_inputs():
        import jax
        import jax.numpy as jnp
        _rk = jax.random.key(seed)
        x = -0.0002928 + 1 * jax.random.normal(jax.random.fold_in(_rk, 1), (8, 64, 256), jnp.float32)
        _lenS = 64 - jax.random.randint(jax.random.fold_in(_rk, 7), (8,), 0, max(1, 64 // 4) + 1, jnp.int32)
        _lenS2 = 1024 - jax.random.randint(jax.random.fold_in(_rk, 8), (8,), 0, max(1, 1024 // 4) + 1, jnp.int32)
        _ctx_1024P = jax.random.normal(jax.random.fold_in(_rk, 11), (8, 16, 256), jnp.float32)
        _ctx_1024c = jax.random.dirichlet(jax.random.fold_in(_rk, 511), 0.3 * jnp.ones((16,), jnp.float32), (8, 1024))
        _ctx_1024t = jnp.einsum('bsk,bkd->bsd', _ctx_1024c, _ctx_1024P)
        _ctx_1024t = _ctx_1024t * jax.lax.rsqrt(jnp.mean(jnp.square(_ctx_1024t)) + 1e-12) * 0.953939
        ctx_1024 = -1.39393e-06 + 0.999914 * (_ctx_1024t + 0.3 * jax.random.normal(jax.random.fold_in(_rk, 611), (8, 1024, 256), jnp.float32))
        fside_Bx16xSxS2_0 = -6.00028e-06 + 0.100001 * jax.random.normal(jax.random.fold_in(_rk, 12), (8, 16, 64, 1024), jnp.float32)
        return (x, ctx_1024, fside_Bx16xSxS2_0)
    x, ctx_1024, fside_Bx16xSxS2_0 = _rec_inputs()

    def _L0_xattn_setup():
        import jax, jax.numpy as jnp
        import numpy as np
        import math
        H = 16
        D = 256
        FF = 1024
        DK = D // H
        EPS = 1e-05

        def layer_norm(x, g, b):
            mu = jnp.mean(x, axis=-1, keepdims=True)
            var = jnp.var(x, axis=-1, keepdims=True)
            return (x - mu) * jax.lax.rsqrt(var + EPS) * g + b
        key = jax.random.key(seed)
        ks = jax.random.split(key, 16)
        B, S = (2, 512)
        s = 1.0 / math.sqrt(D)
        return {'x_q': jax.random.normal(ks[0], (B, S, D), jnp.float32), 'x_kv': jax.random.normal(ks[1], (B, S, D), jnp.float32), 'bias': jax.random.normal(ks[2], (B, H, S, S), jnp.float32) * 0.1, 'Wq': jax.random.normal(ks[3], (D, D), jnp.float32) * s, 'Wk': jax.random.normal(ks[4], (D, D), jnp.float32) * s, 'Wv': jax.random.normal(ks[5], (D, D), jnp.float32) * s, 'Wo': jax.random.normal(ks[6], (D, D), jnp.float32) * s, 'W1': jax.random.normal(ks[7], (FF, D), jnp.float32) * s, 'b1': jnp.zeros((FF,), jnp.float32), 'W2': jax.random.normal(ks[8], (D, FF), jnp.float32) * (1.0 / math.sqrt(FF)), 'b2': jnp.zeros((D,), jnp.float32), 'g1': jnp.ones((D,), jnp.float32), 'be1': jnp.zeros((D,), jnp.float32), 'g2': jnp.ones((D,), jnp.float32), 'be2': jnp.zeros((D,), jnp.float32)}
    _L0_xattn_all = _L0_xattn_setup()
    _L0_xattn_in = {k: v for k, v in _L0_xattn_all.items() if k in ('Wq', 'Wk', 'Wv', 'Wo', 'W1', 'b1', 'W2', 'b2', 'g1', 'be1', 'g2', 'be2')}
    del _L0_xattn_all

    def _L0_attn_setup():
        import jax, jax.numpy as jnp
        import numpy as np
        D_MODEL = 256
        HEAD_DIM = 64
        CHUNK = 64
        N_HEADS = D_MODEL // HEAD_DIM
        MEM_ALPHA = 0.03

        def _forward(out, Ww, Wr, decay, log_alpha):
            B, T, D = out.shape
            H, d, C = (N_HEADS, HEAD_DIM, CHUNK)
            x = out.astype(jnp.float32)
            gamma = jax.nn.sigmoid(decay)
            log_gamma = jnp.log(gamma)
            v = (x @ Ww.T).reshape(B, T, H, d).transpose(0, 2, 1, 3)
            xh = x.reshape(B, T, H, d)
            rk = xh / jnp.maximum(jnp.linalg.norm(xh, axis=-1, keepdims=True), 1e-12)
            rk = rk.transpose(0, 2, 1, 3)
            wk = jnp.concatenate([jnp.zeros((B, H, 1, d), jnp.float32), rk[:, :, :-1]], axis=2)
            BH = B * H
            gamma_bh = jnp.tile(gamma, B)
            log_gamma_bh = jnp.tile(log_gamma, B)
            v = v.reshape(BH, T, d)
            rk = rk.reshape(BH, T, d)
            wk = wk.reshape(BH, T, d)
            pad = -T % C
            if pad:
                z = ((0, 0), (0, pad), (0, 0))
                v, rk, wk = (jnp.pad(v, z), jnp.pad(rk, z), jnp.pad(wk, z))
            T_pad = T + pad
            N = T_pad // C
            v = v.reshape(BH, N, C, d)
            rk = rk.reshape(BH, N, C, d)
            wk = wk.reshape(BH, N, C, d)
            p = jnp.arange(C)
            diffs = jnp.maximum(p[:, None] - p[None, :], 0).astype(jnp.float32)
            L = jnp.tril(jnp.exp(diffs * log_gamma_bh[:, None, None]))
            strict = jnp.tril(jnp.ones((C, C), bool), -1)
            A0 = -jnp.where(strict, jnp.einsum('bnid,bnjd->bnij', wk, wk) * L[:, None], 0.0)
            eye = jnp.eye(C, dtype=jnp.float32)
            A = jnp.linalg.inv(eye - A0)
            gp = gamma_bh[:, None, None] ** p[None, :, None]
            gp_tail = gamma_bh[:, None, None] ** (C - 1 - p)[None, :, None]
            gamma_C = (gamma_bh ** C)[:, None, None]
            intra = jnp.where(strict, jnp.einsum('bnid,bnjd->bnij', rk, wk) * L[:, None], 0.0)
            rk_g = rk * gp[:, None]
            wk_g = (wk * gp_tail[:, None]).transpose(0, 1, 3, 2)

            def step(S, inp):
                A_i, v_i, wk_i, rkg_i, wkg_i, intra_i = inp
                v_corr = A_i @ v_i
                wk_corr = A_i @ wk_i
                v_new = v_corr - wk_corr @ S
                o_i = rkg_i @ S + intra_i @ v_new
                S = gamma_C * S + wkg_i @ v_new
                return (S, o_i)
            mv = lambda a: jnp.moveaxis(a, 1, 0)
            S0 = jnp.zeros((BH, d, d), jnp.float32)
            _, o = jax.lax.scan(step, S0, (mv(A), mv(v), mv(wk), mv(rk_g), mv(wk_g), mv(intra)))
            o = jnp.moveaxis(o, 0, 1).reshape(B, H, T_pad, d)
            alpha = jnp.exp(log_alpha)[None, :, None, None]
            o = (alpha * o).transpose(0, 2, 1, 3).reshape(B, T_pad, D)[:, :T]
            return out + (o @ Wr.T).astype(out.dtype)
        key = jax.random.key(seed)
        k0, k1, k2 = jax.random.split(key, 3)
        B, T = (2, 2048)
        out = jax.random.normal(k0, (B, T, D_MODEL), jnp.float32)
        Ww = jax.random.normal(k1, (D_MODEL, D_MODEL), jnp.float32) * 0.02
        Wr = jax.random.normal(k2, (D_MODEL, D_MODEL), jnp.float32) * 0.02
        decay = jnp.full((N_HEADS,), 4.6, jnp.float32)
        log_alpha = jnp.log(jnp.full((N_HEADS,), MEM_ALPHA, jnp.float32))
        return {'out': out, 'Ww': Ww, 'Wr': Wr, 'decay': decay, 'log_alpha': log_alpha}
    _L0_attn_all = _L0_attn_setup()
    _L0_attn_in = {k: v for k, v in _L0_attn_all.items() if k in ('Ww', 'Wr', 'decay', 'log_alpha')}
    del _L0_attn_all

    def _L0_ffn_setup():
        import jax, jax.numpy as jnp
        import numpy as np
        NUM_EXPERTS = 8
        HIDDEN = 256
        FFN = 1024
        BATCH = 2
        SEQ = 512
        key = jax.random.key(seed)
        k_x, k_g, k_u, k_d = jax.random.split(key, 4)
        scale_in = 1.0 / np.sqrt(HIDDEN)
        scale_mid = 1.0 / np.sqrt(FFN)
        return {'hidden_states': jax.random.normal(k_x, (BATCH, SEQ, HIDDEN), dtype=jnp.float32), 'Wg': jax.random.normal(k_g, (NUM_EXPERTS, HIDDEN, FFN), dtype=jnp.float32) * scale_in, 'Wu': jax.random.normal(k_u, (NUM_EXPERTS, HIDDEN, FFN), dtype=jnp.float32) * scale_in, 'Wd': jax.random.normal(k_d, (NUM_EXPERTS, FFN, HIDDEN), dtype=jnp.float32) * scale_mid}
    _L0_ffn_all = _L0_ffn_setup()
    _L0_ffn_in = {k: v for k, v in _L0_ffn_all.items() if k in ('Wg', 'Wu', 'Wd')}
    del _L0_ffn_all

    def _L1_xattn_setup():
        import jax, jax.numpy as jnp
        import numpy as np
        key = jax.random.key(seed)
        ks = jax.random.split(key, 5)
        b, n_q, n_kv = (16, 128, 1024)
        query_dim, context_dim, heads, dim_head = (256, 256, 16, 64)
        inner = heads * dim_head
        x = jax.random.normal(ks[0], (b, n_q, query_dim), dtype=jnp.float32)
        context = jax.random.normal(ks[1], (b, n_kv, context_dim), dtype=jnp.float32)
        Wq = jax.random.normal(ks[2], (query_dim, inner), dtype=jnp.float32) * query_dim ** (-0.5)
        Wkv = jax.random.normal(ks[3], (context_dim, 2 * inner), dtype=jnp.float32) * context_dim ** (-0.5)
        Wout = jax.random.normal(ks[4], (inner, query_dim), dtype=jnp.float32) * inner ** (-0.5)
        bout = jnp.zeros((query_dim,), dtype=jnp.float32)
        return {'x': x, 'context': context, 'Wq': Wq, 'Wkv': Wkv, 'Wout': Wout, 'bout': bout}
    _L1_xattn_all = _L1_xattn_setup()
    _L1_xattn_in = {k: v for k, v in _L1_xattn_all.items() if k in ('Wq', 'Wkv', 'Wout', 'bout')}
    del _L1_xattn_all

    def _L1_attn_setup():
        import jax, jax.numpy as jnp
        import numpy as np
        HEADS = 16
        BIAS_STRENGTH = 0.1
        LN_EPS = 1e-05

        def _layernorm(x, gamma, beta):
            mu = jnp.mean(x, axis=-1, keepdims=True)
            var = jnp.mean((x - mu) ** 2, axis=-1, keepdims=True)
            return (x - mu) * jax.lax.rsqrt(var + LN_EPS) * gamma + beta

        def _spatial_bias(spatial_centers, N, dtype):
            diff = spatial_centers[:, None, :] - spatial_centers[None, :, :]
            dist = jnp.sqrt(jnp.sum(diff * diff, axis=-1))
            max_dist = jnp.max(dist)
            core = jnp.where(max_dist > 1e-06, -dist / max_dist, 0.0) * BIAS_STRENGTH
            P = spatial_centers.shape[0]
            bias = jnp.zeros((N, N), dtype=dtype)
            return bias.at[1:P + 1, 1:P + 1].set(core.astype(dtype))
        key = jax.random.key(seed)
        ks = jax.random.split(key, 4)
        B, N, D, P = (2, 512, 256, 256)
        return {'x': jax.random.normal(ks[0], (B, N, D), dtype=jnp.float32), 'W_qkv': jax.random.normal(ks[1], (3 * D, D), dtype=jnp.float32) * D ** (-0.5), 'W_proj': jax.random.normal(ks[2], (D, D), dtype=jnp.float32) * D ** (-0.5), 'b_proj': jnp.zeros((D,), dtype=jnp.float32), 'ln_gamma': jnp.ones((D,), dtype=jnp.float32), 'ln_beta': jnp.zeros((D,), dtype=jnp.float32), 'spatial_centers': jax.random.uniform(ks[3], (P, 2), dtype=jnp.float32)}
    _L1_attn_all = _L1_attn_setup()
    _L1_attn_in = {k: v for k, v in _L1_attn_all.items() if k in ('W_qkv', 'W_proj', 'b_proj', 'ln_gamma', 'ln_beta', 'spatial_centers')}
    del _L1_attn_all

    def _L1_ffn_setup():
        import jax, jax.numpy as jnp
        import numpy as np
        D_MODEL, D_FF, N_EXP = (256, 1024, 8)
        key = jax.random.key(seed)
        ks = jax.random.split(key, 8)
        s = lambda fan_in: 1.0 / np.sqrt(fan_in)
        x = jax.random.normal(ks[0], (4, 512, D_MODEL), dtype=jnp.float32)
        Wr = jax.random.uniform(ks[1], (N_EXP, D_MODEL), jnp.float32, -s(D_MODEL), s(D_MODEL))
        br = jax.random.uniform(ks[2], (N_EXP,), jnp.float32, -s(D_MODEL), s(D_MODEL))
        W1 = jax.random.uniform(ks[3], (N_EXP, D_FF, D_MODEL), jnp.float32, -s(D_MODEL), s(D_MODEL))
        b1 = jax.random.uniform(ks[4], (N_EXP, D_FF), jnp.float32, -s(D_MODEL), s(D_MODEL))
        W2 = jax.random.uniform(ks[5], (N_EXP, D_MODEL, D_FF), jnp.float32, -s(D_FF), s(D_FF))
        b2 = jax.random.uniform(ks[6], (N_EXP, D_MODEL), jnp.float32, -s(D_FF), s(D_FF))
        return {'x': x, 'Wr': Wr, 'br': br, 'W1': W1, 'b1': b1, 'W2': W2, 'b2': b2}
    _L1_ffn_all = _L1_ffn_setup()
    _L1_ffn_in = {k: v for k, v in _L1_ffn_all.items() if k in ('Wr', 'br', 'W1', 'b1', 'W2', 'b2')}
    del _L1_ffn_all
    return {'x': x, 'ctx_1024': ctx_1024, 'fside_Bx16xSxS2_0': fside_Bx16xSxS2_0, 'L0_xattn_Wq': _L0_xattn_in['Wq'], 'L0_xattn_Wk': _L0_xattn_in['Wk'], 'L0_xattn_Wv': _L0_xattn_in['Wv'], 'L0_xattn_Wo': _L0_xattn_in['Wo'], 'L0_xattn_W1': _L0_xattn_in['W1'], 'L0_xattn_b1': _L0_xattn_in['b1'], 'L0_xattn_W2': _L0_xattn_in['W2'], 'L0_xattn_b2': _L0_xattn_in['b2'], 'L0_xattn_g1': _L0_xattn_in['g1'], 'L0_xattn_be1': _L0_xattn_in['be1'], 'L0_xattn_g2': _L0_xattn_in['g2'], 'L0_xattn_be2': _L0_xattn_in['be2'], 'L0_attn_Ww': _L0_attn_in['Ww'], 'L0_attn_Wr': _L0_attn_in['Wr'], 'L0_attn_decay': _L0_attn_in['decay'], 'L0_attn_log_alpha': _L0_attn_in['log_alpha'], 'L0_ffn_Wg': _L0_ffn_in['Wg'], 'L0_ffn_Wu': _L0_ffn_in['Wu'], 'L0_ffn_Wd': _L0_ffn_in['Wd'], 'L1_xattn_Wq': _L1_xattn_in['Wq'], 'L1_xattn_Wkv': _L1_xattn_in['Wkv'], 'L1_xattn_Wout': _L1_xattn_in['Wout'], 'L1_xattn_bout': _L1_xattn_in['bout'], 'L1_attn_W_qkv': _L1_attn_in['W_qkv'], 'L1_attn_W_proj': _L1_attn_in['W_proj'], 'L1_attn_b_proj': _L1_attn_in['b_proj'], 'L1_attn_ln_gamma': _L1_attn_in['ln_gamma'], 'L1_attn_ln_beta': _L1_attn_in['ln_beta'], 'L1_attn_spatial_centers': _L1_attn_in['spatial_centers'], 'L1_ffn_Wr': _L1_ffn_in['Wr'], 'L1_ffn_br': _L1_ffn_in['br'], 'L1_ffn_W1': _L1_ffn_in['W1'], 'L1_ffn_b1': _L1_ffn_in['b1'], 'L1_ffn_W2': _L1_ffn_in['W2'], 'L1_ffn_b2': _L1_ffn_in['b2']}

def reference(x, ctx_1024, fside_Bx16xSxS2_0, L0_xattn_Wq, L0_xattn_Wk, L0_xattn_Wv, L0_xattn_Wo, L0_xattn_W1, L0_xattn_b1, L0_xattn_W2, L0_xattn_b2, L0_xattn_g1, L0_xattn_be1, L0_xattn_g2, L0_xattn_be2, L0_attn_Ww, L0_attn_Wr, L0_attn_decay, L0_attn_log_alpha, L0_ffn_Wg, L0_ffn_Wu, L0_ffn_Wd, L1_xattn_Wq, L1_xattn_Wkv, L1_xattn_Wout, L1_xattn_bout, L1_attn_W_qkv, L1_attn_W_proj, L1_attn_b_proj, L1_attn_ln_gamma, L1_attn_ln_beta, L1_attn_spatial_centers, L1_ffn_Wr, L1_ffn_br, L1_ffn_W1, L1_ffn_b1, L1_ffn_W2, L1_ffn_b2):
    import jax
    import jax.numpy as jnp

    def _L0_xattn_ref(x_q, x_kv, bias, Wq, Wk, Wv, Wo, W1, b1, W2, b2, g1, be1, g2, be2):
        import jax, jax.numpy as jnp
        import numpy as np
        import math
        H = 16
        D = 256
        FF = 1024
        DK = D // H
        EPS = 1e-05

        def layer_norm(x, g, b):
            mu = jnp.mean(x, axis=-1, keepdims=True)
            var = jnp.var(x, axis=-1, keepdims=True)
            return (x - mu) * jax.lax.rsqrt(var + EPS) * g + b
        B, S, _ = x_q.shape

        def split(x):
            return x.reshape(B, -1, H, DK).transpose(0, 2, 1, 3)
        q = split(x_q @ Wq.T)
        k = split(x_kv @ Wk.T)
        v = split(x_kv @ Wv.T)
        scores = jnp.einsum('bhqd,bhkd->bhqk', q, k) / math.sqrt(DK) + bias
        p = jax.nn.softmax(scores, axis=-1)
        o = jnp.einsum('bhqk,bhkd->bhqd', p, v)
        o = o.transpose(0, 2, 1, 3).reshape(B, S, D)
        x = x_q + o @ Wo.T
        h = jax.nn.gelu(layer_norm(x, g1, be1) @ W1.T + b1, approximate=False)
        x = x + h @ W2.T + b2
        return layer_norm(x, g2, be2)

    def _L0_attn_ref(out, Ww, Wr, decay, log_alpha):
        import jax, jax.numpy as jnp
        import numpy as np
        D_MODEL = 256
        HEAD_DIM = 64
        CHUNK = 64
        N_HEADS = D_MODEL // HEAD_DIM
        MEM_ALPHA = 0.03

        def _forward(out, Ww, Wr, decay, log_alpha):
            B, T, D = out.shape
            H, d, C = (N_HEADS, HEAD_DIM, CHUNK)
            x = out.astype(jnp.float32)
            gamma = jax.nn.sigmoid(decay)
            log_gamma = jnp.log(gamma)
            v = (x @ Ww.T).reshape(B, T, H, d).transpose(0, 2, 1, 3)
            xh = x.reshape(B, T, H, d)
            rk = xh / jnp.maximum(jnp.linalg.norm(xh, axis=-1, keepdims=True), 1e-12)
            rk = rk.transpose(0, 2, 1, 3)
            wk = jnp.concatenate([jnp.zeros((B, H, 1, d), jnp.float32), rk[:, :, :-1]], axis=2)
            BH = B * H
            gamma_bh = jnp.tile(gamma, B)
            log_gamma_bh = jnp.tile(log_gamma, B)
            v = v.reshape(BH, T, d)
            rk = rk.reshape(BH, T, d)
            wk = wk.reshape(BH, T, d)
            pad = -T % C
            if pad:
                z = ((0, 0), (0, pad), (0, 0))
                v, rk, wk = (jnp.pad(v, z), jnp.pad(rk, z), jnp.pad(wk, z))
            T_pad = T + pad
            N = T_pad // C
            v = v.reshape(BH, N, C, d)
            rk = rk.reshape(BH, N, C, d)
            wk = wk.reshape(BH, N, C, d)
            p = jnp.arange(C)
            diffs = jnp.maximum(p[:, None] - p[None, :], 0).astype(jnp.float32)
            L = jnp.tril(jnp.exp(diffs * log_gamma_bh[:, None, None]))
            strict = jnp.tril(jnp.ones((C, C), bool), -1)
            A0 = -jnp.where(strict, jnp.einsum('bnid,bnjd->bnij', wk, wk) * L[:, None], 0.0)
            eye = jnp.eye(C, dtype=jnp.float32)
            A = jnp.linalg.inv(eye - A0)
            gp = gamma_bh[:, None, None] ** p[None, :, None]
            gp_tail = gamma_bh[:, None, None] ** (C - 1 - p)[None, :, None]
            gamma_C = (gamma_bh ** C)[:, None, None]
            intra = jnp.where(strict, jnp.einsum('bnid,bnjd->bnij', rk, wk) * L[:, None], 0.0)
            rk_g = rk * gp[:, None]
            wk_g = (wk * gp_tail[:, None]).transpose(0, 1, 3, 2)

            def step(S, inp):
                A_i, v_i, wk_i, rkg_i, wkg_i, intra_i = inp
                v_corr = A_i @ v_i
                wk_corr = A_i @ wk_i
                v_new = v_corr - wk_corr @ S
                o_i = rkg_i @ S + intra_i @ v_new
                S = gamma_C * S + wkg_i @ v_new
                return (S, o_i)
            mv = lambda a: jnp.moveaxis(a, 1, 0)
            S0 = jnp.zeros((BH, d, d), jnp.float32)
            _, o = jax.lax.scan(step, S0, (mv(A), mv(v), mv(wk), mv(rk_g), mv(wk_g), mv(intra)))
            o = jnp.moveaxis(o, 0, 1).reshape(B, H, T_pad, d)
            alpha = jnp.exp(log_alpha)[None, :, None, None]
            o = (alpha * o).transpose(0, 2, 1, 3).reshape(B, T_pad, D)[:, :T]
            return out + (o @ Wr.T).astype(out.dtype)
        return _forward(out, Ww, Wr, decay, log_alpha)

    def _L0_ffn_ref(hidden_states, Wg, Wu, Wd):
        import jax, jax.numpy as jnp
        import numpy as np
        NUM_EXPERTS = 8
        HIDDEN = 256
        FFN = 1024
        BATCH = 2
        SEQ = 512
        B, S, H = hidden_states.shape
        x = hidden_states.reshape(-1, H)

        def expert_step(acc, w):
            wg, wu, wd = w
            h = jax.nn.silu(x @ wg) * (x @ wu)
            return (acc + h @ wd, None)
        acc, _ = jax.lax.scan(expert_step, jnp.zeros_like(x), (Wg, Wu, Wd))
        return acc.reshape(B, S, H)

    def _L1_xattn_ref(x, context, Wq, Wkv, Wout, bout):
        import jax, jax.numpy as jnp
        import numpy as np
        heads, dim_head = (16, 64)
        b, n_q, _ = x.shape
        n_kv = context.shape[1]
        scale = dim_head ** (-0.5)
        q = x @ Wq
        kv = context @ Wkv
        k, v = jnp.split(kv, 2, axis=-1)

        def split_heads(t):
            bb, n, _ = t.shape
            return t.reshape(bb, n, heads, dim_head).transpose(0, 2, 1, 3)
        q, k, v = map(split_heads, (q, k, v))
        i_idx = jnp.arange(n_q)[:, None]
        j_idx = jnp.arange(n_kv)[None, :]
        mask = j_idx % n_q == i_idx
        sim = jnp.einsum('bhid,bhjd->bhij', q, k) * scale
        max_neg = -jnp.finfo(sim.dtype).max
        sim = jnp.where(mask[None, None, :, :], sim, max_neg)
        attn = jax.nn.softmax(sim, axis=-1)
        out = jnp.einsum('bhij,bhjd->bhid', attn, v)
        out = out.transpose(0, 2, 1, 3).reshape(b, n_q, heads * dim_head)
        return out @ Wout + bout

    def _L1_attn_ref(x, W_qkv, W_proj, b_proj, ln_gamma, ln_beta, spatial_centers):
        import jax, jax.numpy as jnp
        import numpy as np
        HEADS = 16
        BIAS_STRENGTH = 0.1
        LN_EPS = 1e-05

        def _layernorm(x, gamma, beta):
            mu = jnp.mean(x, axis=-1, keepdims=True)
            var = jnp.mean((x - mu) ** 2, axis=-1, keepdims=True)
            return (x - mu) * jax.lax.rsqrt(var + LN_EPS) * gamma + beta

        def _spatial_bias(spatial_centers, N, dtype):
            diff = spatial_centers[:, None, :] - spatial_centers[None, :, :]
            dist = jnp.sqrt(jnp.sum(diff * diff, axis=-1))
            max_dist = jnp.max(dist)
            core = jnp.where(max_dist > 1e-06, -dist / max_dist, 0.0) * BIAS_STRENGTH
            P = spatial_centers.shape[0]
            bias = jnp.zeros((N, N), dtype=dtype)
            return bias.at[1:P + 1, 1:P + 1].set(core.astype(dtype))
        B, N, D = x.shape
        H = HEADS
        hd = D // H
        scale = hd ** (-0.5)
        qkv = jnp.einsum('bnd,ed->bne', x, W_qkv)
        qkv = qkv.reshape(B, N, 3, H, hd).transpose(2, 0, 3, 1, 4)
        q, k, v = (qkv[0], qkv[1], qkv[2])
        attn = jnp.einsum('bhnd,bhmd->bhnm', q, k) * scale
        P = spatial_centers.shape[0]
        if N >= P + 1:
            attn = attn + _spatial_bias(spatial_centers, N, x.dtype)[None, None]
        attn = jax.nn.softmax(attn, axis=-1)
        out = jnp.einsum('bhnm,bhmd->bhnd', attn, v)
        out = out.transpose(0, 2, 1, 3).reshape(B, N, D)
        out = jnp.einsum('bnd,ed->bne', out, W_proj) + b_proj
        return out + _layernorm(x, ln_gamma, ln_beta)

    def _L1_ffn_ref(x, Wr, br, W1, b1, W2, b2):
        import jax, jax.numpy as jnp
        import numpy as np
        D_MODEL, D_FF, N_EXP = (256, 1024, 8)
        B, S, D = x.shape
        xf = x.reshape(-1, D)
        logits = xf @ Wr.T + br
        expert_idx = jnp.argmax(logits, axis=-1)
        h = jax.nn.relu(jnp.einsum('td,efd->etf', xf, W1) + b1[:, None, :])
        y = jnp.einsum('etf,edf->etd', h, W2) + b2[:, None, :]
        out = y[expert_idx, jnp.arange(xf.shape[0])]
        return out.reshape(B, S, D)
    x = x + _L0_xattn_ref(_layernorm(x, axis=-1), ctx_1024, fside_Bx16xSxS2_0, L0_xattn_Wq, L0_xattn_Wk, L0_xattn_Wv, L0_xattn_Wo, L0_xattn_W1, L0_xattn_b1, L0_xattn_W2, L0_xattn_b2, L0_xattn_g1, L0_xattn_be1, L0_xattn_g2, L0_xattn_be2)
    x = x + _L0_attn_ref(_layernorm(x, axis=-1), L0_attn_Ww, L0_attn_Wr, L0_attn_decay, L0_attn_log_alpha)
    x = x + _L0_ffn_ref(_layernorm(x, axis=-1), L0_ffn_Wg, L0_ffn_Wu, L0_ffn_Wd)
    x = x + _L1_xattn_ref(_layernorm(x, axis=-1), ctx_1024, L1_xattn_Wq, L1_xattn_Wkv, L1_xattn_Wout, L1_xattn_bout)
    x = x + _L1_attn_ref(_layernorm(x, axis=-1), L1_attn_W_qkv, L1_attn_W_proj, L1_attn_b_proj, L1_attn_ln_gamma, L1_attn_ln_beta, L1_attn_spatial_centers)
    x = x + _L1_ffn_ref(_layernorm(x, axis=-1), L1_ffn_Wr, L1_ffn_br, L1_ffn_W1, L1_ffn_b1, L1_ffn_W2, L1_ffn_b2)
    return x

_drawn_inputs = setup_inputs


def setup_inputs(seed=0):
    import zlib

    import numpy as np

    out = dict(_drawn_inputs(seed))
    spreads = {'L0_xattn_b1': (0.0, 0.1),
     'L0_xattn_b2': (0.0, 0.1),
     'L0_xattn_g1': (1.0, 0.2),
     'L0_xattn_be1': (0.0, 0.1),
     'L0_xattn_g2': (1.0, 0.2),
     'L0_xattn_be2': (0.0, 0.1),
     'L0_attn_decay': (4.599999904632568, 0.6),
     'L0_attn_log_alpha': (-3.5065579414367676, 0.6),
     'L1_xattn_bout': (0.0, 0.1),
     'L1_attn_b_proj': (0.0, 0.327),
     'L1_attn_ln_gamma': (1.0, 0.2),
     'L1_attn_ln_beta': (0.0, 0.341)}
    factors = {'fside_Bx16xSxS2_0': 8.0,
     'L0_attn_Ww': 8.0,
     'L0_attn_Wr': 8.0,
     'L1_ffn_br': 4.491,
     'L1_ffn_b1': 8.0,
     'L1_ffn_b2': 8.0}
    for name, (base, spread) in spreads.items():
        noise = np.random.default_rng([zlib.crc32(name.encode()), seed]).standard_normal(out[name].shape)
        drawn = base * np.exp(spread * noise) if base else spread * noise
        out[name] = jnp.asarray(drawn.astype(out[name].dtype))
    for name, factor in factors.items():
        out[name] = (out[name] * factor).astype(out[name].dtype)
    return out
```

```python
import numpy as np

import concourse.bass as bass
from concourse import mybir
from concourse.alu_op_type import AluOpType as ALU

F32 = mybir.dt.float32
ACT = mybir.ActivationFunctionType
AX = mybir.AxisListType

P = 128
B, S, D = 8, 64, 256
TOK = B * S
NT = TOK // P
KC = D // P
KEYS = 1024
KT = KEYS // P
H, DK = 16, 16
FF, FC = 1024, 8
NEXP = 8
MH, MD = 4, 64
LEVELS = 6
XH, XD = 16, 64
GRP, GI = 8, 8
GM = KEYS // S
EPS = 1e-5
BIG = 1e30


def const_layout():
    p = np.arange(P)[:, None]
    c = np.arange(P)[None, :]
    c8 = np.arange(8)[None, :]
    i, j = c, p
    same = (i // S) == (j // S)
    parts = {
        "ident": (p == c),
        "head8": (p // DK == c8),
        "pair32": (p // 64 == np.arange(32)[None, :] // DK),
        "pick64": (p % 64 == np.arange(64)[None, :]),
        "half2": ((p % 32) // DK == np.arange(2)[None, :]),
        "group": np.where(p % GI == c % GI, 0.0, -BIG),
        "upper": same & (i > j),
        "dist": np.where(same & (i > j), i - j, 0),
        "low0": same & (p % 2 == 1) & (c == p - 1),
        "first": np.broadcast_to(8.0 - c8, (P, 8)),
        "rowsel": np.concatenate([np.broadcast_to(p == e, (P, P)) for e in range(NEXP)], 1),
    }
    for k in range(LEVELS):
        s = 2 ** k
        parts[f"up{k}"] = (i // (2 * s) == j // (2 * s)) & (i // s % 2 == 1) & (j // s % 2 == 0)
    at, where, cols = 0, {}, []
    for name, a in parts.items():
        a = np.asarray(a, np.float32)
        where[name] = (at, at + a.shape[1])
        at += a.shape[1]
        cols.append(a)
    return where, np.concatenate(cols, 1)


CONST_AT, CONST = const_layout()
NVEC = 8
V_B2, V_G2, V_BE2, V_BOUT, V_BPROJ, V_LNG, V_LNB, V_RBR = range(NVEC)


class Chain:

    def __init__(self, eng, sem):
        self.eng, self.sem, self.base, self.n = eng, sem, 0, 0

    def add(self, ins):
        self.n += 1
        return ins.then_inc(self.sem, 1)

    def sync(self):
        self.eng.wait_ge(self.sem, self.base + self.n)

    def step(self, ins):
        self.add(ins)
        self.sync()

    def enter(self, i, per):
        self.before, self.per = self.base + self.n, per
        self.base, self.n = i * per + self.before, 0

    def leave(self, times):
        assert self.n == self.per, self.n
        self.base, self.n = self.before + times * self.per, 0


def perceiver(nc, A, out):
    sems = {}

    def sem(name):
        if name not in sems:
            sems[name] = nc.alloc_semaphore(name)
        return sems[name]

    def sb(name, *shape):
        return nc.alloc_sbuf_tensor(name, [P, *shape], F32)

    consts = sb("consts", CONST.shape[1])
    x_tok = sb("x_tok", NT, D)
    xn_tok = sb("xn_tok", NT, D)
    y_tok = sb("y_tok", NT, D)
    tmp_tok = sb("tmp_tok", NT, D)
    xnT = sb("xnT", KC, TOK)
    aT = sb("aT", KC, TOK)
    vecs = sb("vecs", NVEC, D)
    cols = sb("cols", 12 + 2 * MH)
    small = sb("small", 256)
    hT = sb("hT", FC, TOK)
    arena = sb("arena", 38000)
    PS = nc.alloc_psum_tensor("PS", [P, 8, 512], F32)

    def C(name):
        a, b = CONST_AT[name]
        return consts[:, a:b]

    class Carve:
        def __init__(self, at=0):
            self.at = at

        def __call__(self, *shape):
            n = int(np.prod(shape))
            v = arena[:, self.at:self.at + n]
            self.at += n
            assert self.at <= 38000, self.at
            if len(shape) == 1:
                return v
            names = "abcd"[:len(shape)]
            return v.rearrange(f"p ({' '.join(names)}) -> p {' '.join(names)}",
                               **{k: s for k, s in zip(names[1:], shape[1:])})

    def bank(n, k=1):
        return PS[:, n:n + k, :].rearrange("p a b -> p (a b)")

    def bcast(ap, axis, shape):
        return ap.unsqueeze(axis).to_broadcast([ap.shape[0], *shape])

    def settle(eng, name):
        eng.sem_inc(sem(f"waited_{name}"), 1)

    stats = small[:, 0:24].rearrange("p (t s) -> p t s", t=NT)
    mv = small[:, 24:32].rearrange("p (t s) -> p t s", t=NT)
    var_eps, std, rstd = small[:, 32:36], small[:, 36:40], small[:, 40:44]

    zero8 = small[:, 64:64 + P]

    ca = Carve()
    wq0, wk0, wv0, wo0 = (ca(KC, D) for _ in range(4))
    w1_0, w2_0 = ca(KC, FF), ca(FC, D)
    ww, wr = ca(KC, D), ca(KC, D)
    after_w = ca.at
    ring = ca(8, KEYS)
    ctxT0 = ca(KC, KEYS)
    kT0 = ca(KC, KEYS)
    v0 = ca(KT, D)
    pT = ca(2, 4, KT, P)
    qz0 = ca(KC, 8, S)
    qT0 = ca(KC, TOK)
    nmax0, rsum0, rinv0 = ca(8), ca(8), ca(4)
    rdiag = ca(4, 32)
    osel, osel2 = ca(S), ca(S)
    cb = Carve(after_w)
    decayed = cb(MH, P)
    low0g = cb(MH, P)
    MT, IT, T, TT, CT, X = (cb(MH, NT, P) for _ in range(6))
    vb, vnew = cb(NT, D), cb(NT, D)
    rkT, wkT = cb(KC, TOK), cb(KC, B, S)
    ssq, rinvB = cb(NT * MH), cb(NT * MH)
    cc = Carve(cb.at)
    cc.at = max(cc.at, after_w)
    wg = [cc(KC, FF) for _ in range(2)]
    wu = [cc(KC, FF) for _ in range(2)]
    wd = [cc(FC, D) for _ in range(2)]
    sg = cc(2, TOK)
    cd = Carve()
    U = cd(KC, XH, TOK)
    wq1, wkT1, wv1, wo1 = cd(KC, FF), cd(FC, D), cd(KC, FF), cd(FC, D)
    ctxT1, ctxG = cd(KC, KEYS), cd(GRP, D)
    Ub = cd(KC, GRP, P)
    Z, PTx = cd(2, 4, P), cd(2, 4, P)
    qz1 = cd(2, 2, TOK)
    mx1, rs1, ri1 = cd(2, 4), cd(2, 4), cd(2, 4)
    ce = Carve()
    wqkv, wproj = ce(KC, 3 * D), ce(KC, D)
    qTe = ce(KC, TOK)
    kTz = ce(KC, 8, TOK)
    ve = ce(NT, D)
    Ze = ce(NT, H, S)
    Pz = ce(NT, H, P)
    PzT = ce(2, H, P)
    mxe, rse, rie = ce(NT, H), ce(NT, H), ce(NT, H)
    cf = Carve()
    wf1 = [cf(KC, FF) for _ in range(2)]
    wf2 = [cf(FC, D) for _ in range(2)]
    bf1 = [cf(FC) for _ in range(2)]
    wrt, b2f = cf(KC, NEXP), cf(D)
    rel = cf(2, TOK)
    logit, eq8, oh8 = cf(NT, NEXP), cf(NT, NEXP), cf(NT, NEXP)
    top = cf(NT)
    ohT = cf(TOK)
    chosen = cf(NEXP, TOK)

    def ln_dve(dve, ch, k, src, dst):
        for t in range(NT):
            ch.add(dve.bn_stats(stats[:, t, :], src[:, t, :]))
        ch.sync()
        for t in range(NT):
            ch.add(dve.bn_aggr(mv[:, t, :], stats[:, t, :]))
        ch.sync()
        dve.tensor_scalar_add(var_eps, mv[:, :, 1], EPS).then_inc(sem("ln_var"), 1)
        dve.wait_ge(sem("ln_std"), k)
        ch.step(dve.reciprocal(rstd, std))
        for t in range(NT):
            last = dve.tensor_scalar(dst[:, t, :], src[:, t, :], mv[:, t, 0:1], rstd[:, t:t + 1],
                                     ALU.subtract, ALU.mult)
            if t < NT - 1:
                ch.add(last)
        return last

    def ln_act(act, k):
        act.wait_ge(sem("ln_var"), k)
        act.activation(std, var_eps, ACT.Sqrt).then_inc(sem("ln_std"), 1)

    def tr_pe(pe, k, src, b0=0):
        pe.wait_ge(sem("tr_src"), k)
        for kc in range(KC):
            for t in range(NT):
                last = pe.transpose(PS[:, b0 + kc, t * P:(t + 1) * P],
                                    src[:, t, kc * P:(kc + 1) * P], C("ident"))
            last.then_inc(sem("tr_ps"), 1)

    def tr_dve(dve, k, dst, b0=0, affine=None):
        dve.wait_ge(sem("tr_ps"), 2 * k - 1)
        if affine:
            dve.tensor_scalar(dst[:, 0], bank(b0), cols[:, 0:1], cols[:, 2:3], ALU.mult,
                              ALU.add).then_inc(sem("tr_sb"), 1)
        else:
            dve.tensor_copy(dst[:, 0], bank(b0)).then_inc(sem("tr_sb"), 1)

    def tr_act(act, k, dst, b0=0, affine=None):
        act.wait_ge(sem("tr_ps"), 2 * k)
        if affine:
            act.activation(dst[:, 1], bank(b0 + 1), ACT.Identity, scale=cols[:, 1:2],
                           bias=cols[:, 3:4]).then_inc(sem("tr_sb"), 1)
        else:
            act.copy(dst[:, 1], bank(b0 + 1)).then_inc(sem("tr_sb"), 1)

    def tok_mm(pe, lhsT, rhs, b0, s, n=D):
        kk = lhsT.shape[1]
        for t in range(NT):
            for k in range(kk):
                last = pe.matmul(PS[:, b0 + t // 2, (t % 2) * D:(t % 2) * D + n],
                                 lhsT[:, k, t * P:(t + 1) * P], rhs[:, k, 0:n],
                                 start=k == 0, stop=k == kk - 1)
            if t % 2:
                last.then_inc(s, 1)

    def two(ap, i):
        return ap[:, 2 * i:2 * i + 2, :].rearrange("p a b -> p (a b)")

    def vec(i):
        return bcast(vecs[:, i, :], 1, (2, D))

    def pair(ap, i):
        return ap[:, 2 * i:2 * i + 2, :]

    def bankpair(b):
        return PS[:, b, :].rearrange("p (a b) -> p a b", a=2)

    with nc.Block() as block:

        @block.sync
        def _(sp):
            sp.dma_start(x_tok[:], A["x"].rearrange("(t p) d -> p t d", p=P)).then_inc(sem("in_x"), 16)
            sp.dma_start(consts[:], A["consts"]).then_inc(sem("in_const"), 16)

            def w_in(dst, src, s):
                sp.dma_start(dst, src.rearrange("(k p) n -> p k n", p=P)).then_inc(sem(s), 16)
            w_in(wq0, A["wq0"], "in_wq0")
            w_in(wk0, A["wk0"], "in_wkv0")
            w_in(wv0, A["wv0"], "in_wkv0")
            with sp.Fori(0, B) as b:
                sp.wait_ge(sem("a_vps"), b * 4 + 1)
                settle(sp, "sp")
                sp.dma_start(ctxT0, A["ctxT"][bass.ds(b, 1)].rearrange("a (k p) n -> p (a k) n", p=P))\
                  .then_inc(sem("a_ctx_in"), 16)
                for u in range(8):
                    sp.wait_ge(sem("a_tps"), b * 16 + 2 * u + 3)
                    settle(sp, "sp")
                    sp.dma_start(ring[:, u, :],
                                 A["bias"][bass.ds(b, 1), 2 * u:2 * u + 2].rearrange("a h q k -> (a h q) k"))\
                      .then_inc(sem(f"a_bias_in{u}"), 16)
                sp.wait_ge(sem("a_ctx_in"), b * 16 + 16)
                settle(sp, "sp")
            w_in(wo0, A["wo0"], "in_wo0")
            w_in(w1_0, A["w1_0"], "in_w12")
            w_in(w2_0, A["w2_0"], "in_w12")
            w_in(ww, A["ww"], "in_wwr")
            w_in(wr, A["wr"], "in_wwr")
            sp.dma_start(cols[:], A["cols"]).then_inc(sem("in_vecs"), 16)
            sp.dma_start(vecs[:], A["vecs"].partition_broadcast(P)).then_inc(sem("in_vecs"), 16)
            sp.wait_ge(sem("a_ot"), 2 * B + 1)
            with sp.Fori(0, NEXP // 2) as i:
                for e2 in range(2):
                    sp.wait_ge(sem(f"c_wfree{e2}"), i + 1)
                    settle(sp, "sp")
                    e = bass.ds(i * 2 + e2, 1)
                    for dst, src in ((wg, "wg"), (wu, "wu"), (wd, "wd")):
                        sp.dma_start(dst[e2], A[src][e].rearrange("a (k p) n -> p (a k) n", p=P))\
                          .then_inc(sem(f"c_w{e2}"), 16)
            sp.wait_ge(sem("x_tok"), 3)
            w_in(wq1, A["wq1"], "in_wq1")
            w_in(wkT1, A["wkT1"], "in_wk1")
            w_in(wv1, A["wv1"], "in_wvo1")
            w_in(wo1, A["wo1"], "in_wvo1")
            with sp.Fori(0, B) as b:
                sp.wait_ge(sem("d_sim"), b * 2 + 1)
                settle(sp, "sp")
                sp.dma_start(ctxT1, A["ctxT"][bass.ds(b, 1)].rearrange("a (k p) n -> p (a k) n", p=P))\
                  .then_inc(sem("d_ctxT"), 16)
                sp.wait_ge(sem("d_w"), b * 4 + 1)
                settle(sp, "sp")
                sp.dma_start(ctxG, A["ctxG"][bass.ds(b, 1)].rearrange("a p g n -> p (a g) n"))\
                  .then_inc(sem("d_ctxG"), 16)
            sp.wait_ge(sem("x_tok"), 4)
            w_in(wqkv, A["wqkv"], "in_wqkv")
            w_in(wproj, A["wproj"], "in_wproj")
            sp.wait_ge(sem("x_tok"), 5)
            w_in(wrt, A["wrt"], "in_wrt")
            sp.dma_start(b2f[0:NEXP], A["b2f"]).then_inc(sem("in_wrt"), 16)
            with sp.Fori(0, NEXP // 2) as i:
                for e2 in range(2):
                    sp.wait_ge(sem(f"f_wfree{e2}"), i + 1)
                    settle(sp, "sp")
                    e = bass.ds(i * 2 + e2, 1)
                    for dst, src in ((wf1, "w1f"), (wf2, "w2f")):
                        sp.dma_start(dst[e2], A[src][e].rearrange("a (k p) n -> p (a k) n", p=P))\
                          .then_inc(sem(f"f_w{e2}"), 16)
                    sp.dma_start(bf1[e2], A["b1f"][e].rearrange("a p n -> (a p) n"))\
                      .then_inc(sem(f"f_w{e2}"), 16)
            sp.wait_ge(sem("x_tok"), 6)
            sp.dma_start(out.rearrange("(t p) d -> p t d", p=P), x_tok[:]).then_inc(sem("stored"), 16)
            sp.wait_ge(sem("stored"), 16)

        @block.tensor
        def _(pe):
            pe.sem_inc(sem("a_vps"), 1)
            pe.sem_inc(sem("a_tps"), 16)
            for e2 in range(2):
                pe.sem_inc(sem(f"c_wfree{e2}"), 1)
                pe.sem_inc(sem(f"f_wfree{e2}"), 1)
            pe.sem_inc(sem("d_sim"), 1)
            pe.sem_inc(sem("d_w"), 1)
            pe.sem_inc(sem("c_dn"), 4)
            pe.sem_inc(sem("f_dn"), 4)

            pe.wait_ge(sem("in_const"), 16)
            tr_pe(pe, 1, xn_tok)
            pe.wait_ge(sem("in_wq0"), 16)
            pe.wait_ge(sem("tr_sb"), 2)
            for mo in range(KC):
                for ki in range(KC):
                    last = pe.matmul(bank(2 + mo), wq0[:, ki, mo * P:(mo + 1) * P], xnT[:, ki],
                                     start=ki == 0, stop=ki == KC - 1)
                last.then_inc(sem("a_qps"), 1)
            pe.wait_ge(sem("in_wkv0"), 32)
            pe.wait_ge(sem("a_qsb"), 2)

            with pe.Fori(0, B) as b:
                def scores(u):
                    if u % 4 == 0:
                        pe.wait_ge(sem("a_kev"), b * 4 + (2 if u < 4 else 4))
                    pe.wait_ge(sem("a_z"), b * 8 + u + 1)
                    for half in range(2):
                        last = pe.matmul(bank(2 * (u % 2) + half),
                                         qz0[:, u // 4, 2 * (u % 4):2 * (u % 4) + 2, :],
                                         kT0[:, u // 4, half * 512:(half + 1) * 512],
                                         start=True, stop=True)
                    last.then_inc(sem("a_s"), 1)

                def transposes(u):
                    pe.wait_ge(sem("a_exp"), b * 8 + u + 1)
                    for g in range(2):
                        if u == 0:
                            pe.wait_ge(sem("a_vev"), b * 4 + 3 + g)
                        else:
                            pe.wait_ge(sem(f"a_tev{g}"), b * 8 + u + 1)
                        for c in range(4):
                            last = pe.transpose(PS[:, 4 + g, c * P:(c + 1) * P],
                                                ring[:, u, (4 * g + c) * P:(4 * g + c + 1) * P], C("ident"))
                        last.then_inc(sem("a_tps"), 1)

                def weighted(kc):
                    for g in range(2):
                        pe.wait_ge(sem(f"a_tev{g}"), b * 8 + 4 * kc + 5)
                    pe.wait_ge(sem("a_ot"), b * 2 + kc + 1)
                    for kt in range(KT):
                        for j in range(4):
                            pe.matmul(PS[32 * j:32 * j + 32, 6, 0:P],
                                      v0[:, kt, kc * P + 32 * j:kc * P + 32 * j + 32],
                                      pT[:, kc, j, kt, :], start=kt == 0, stop=kt == KT - 1)
                    pe.wait_ge(sem("a_rl"), b * 2 + kc + 1)
                    for j in range(4):
                        last = pe.matmul(PS[32 * j:32 * j + 32, 7, 0:S], rdiag[:, j, :], C("pick64"),
                                         start=True, stop=True)
                    last.then_inc(sem("a_pv"), 1)

                pe.wait_ge(sem("a_ctx_in"), b * 16 + 16)
                for n in range(4):
                    mo, half = n // 2, n % 2
                    if n < 2:
                        pe.wait_ge(sem(f"a_tev{n}"), b * 8 + 1)
                    else:
                        pe.wait_ge(sem("a_kev"), b * 4 + n - 1)
                    for ki in range(KC):
                        last = pe.matmul(bank(4 + half), wk0[:, ki, mo * P:(mo + 1) * P],
                                         ctxT0[:, ki, half * 512:(half + 1) * 512],
                                         start=ki == 0, stop=ki == KC - 1)
                    last.then_inc(sem("a_kps"), 1)
                pe.wait_ge(sem("a_qz"), b + 1)
                scores(0)
                scores(1)
                for n in range(4):
                    if n < 2:
                        pe.wait_ge(sem("a_kev"), b * 4 + 3 + n)
                    else:
                        pe.wait_ge(sem("a_vev"), b * 4 + n - 1)
                    for kt in (2 * n, 2 * n + 1):
                        for ki in range(KC):
                            last = pe.matmul(PS[:, 4 + n % 2, (kt % 2) * D:(kt % 2 + 1) * D],
                                             ctxT0[:, ki, kt * P:(kt + 1) * P], wv0[:, ki, :],
                                             start=ki == 0, stop=ki == KC - 1)
                    last.then_inc(sem("a_vps"), 1)
                for u in range(2, 8):
                    scores(u)
                    transposes(u - 2)
                    if u == 5:
                        weighted(0)
                transposes(6)
                transposes(7)
                weighted(1)

            pe.wait_ge(sem("in_wo0"), 16)
            pe.wait_ge(sem("a_ot"), 2 * B + 1)
            tok_mm(pe, aT, wo0, 0, sem("a2_o"))
            tr_pe(pe, 2, tmp_tok, 4)
            pe.wait_ge(sem("in_w12"), 32)
            pe.wait_ge(sem("tr_sb"), 4)
            for c in range(FC):
                if c >= 4:
                    pe.wait_ge(sem("a2_g"), c - 3)
                for ki in range(KC):
                    last = pe.matmul(bank(c % 4), w1_0[:, ki, c * P:(c + 1) * P], xnT[:, ki],
                                     start=ki == 0, stop=ki == KC - 1)
                last.then_inc(sem("a2_h"), 1)
            pe.wait_ge(sem("a2_g"), 8)
            tok_mm(pe, hT, w2_0, 4, sem("a2_y"))

            tr_pe(pe, 3, xn_tok)
            pe.wait_ge(sem("in_wwr"), 32)
            pe.wait_ge(sem("tr_sb"), 6)
            tok_mm(pe, xnT, ww, 2, sem("b_v"))
            tr_pe(pe, 4, tmp_tok, 4)
            pe.wait_ge(sem("tr_sb"), 8)
            for h in range(MH):
                r = slice(64 * (h % 2), 64 * (h % 2) + 64)
                for t in range(NT):
                    wk_t = wkT[r, h // 2, 2 * t:2 * t + 2, :].rearrange("p a b -> p (a b)")
                    rk_t = rkT[r, h // 2, t * P:(t + 1) * P]
                    if t == 0 and h == 2:
                        pe.wait_ge(sem("b_vsb"), 2)
                    pe.matmul(PS[:, h, t * P:(t + 1) * P], wk_t, wk_t, start=True, stop=True)
                    last = pe.matmul(PS[:, 4 + h, t * P:(t + 1) * P], wk_t, rk_t, start=True, stop=True)
                last.then_inc(sem("b_gram"), 1)
            for k in range(1, LEVELS):
                for h in range(MH):
                    pe.wait_ge(sem("b_ct"), 4 * (k - 1) + h + 1)
                    for t in range(NT):
                        last = pe.matmul(PS[:, h, t * P:(t + 1) * P], CT[:, h, t, :], T[:, h, t, :],
                                         start=True, stop=True)
                    last.then_inc(sem("b_x"), 1)
                for h in range(MH):
                    pe.wait_ge(sem("b_xsb"), 4 * (k - 1) + h + 1)
                    for t in range(NT):
                        last = pe.matmul(PS[:, h, t * P:(t + 1) * P], X[:, h, t, :], TT[:, h, t, :],
                                         start=True, stop=True)
                    if k == LEVELS - 1:
                        last.then_inc(sem("b_tx"), 1)
                        continue
                    for t in range(NT):
                        last = pe.matmul(PS[:, 4 + h, t * P:(t + 1) * P], TT[:, h, t, :], X[:, h, t, :],
                                         start=True, stop=True)
                    last.then_inc(sem("b_tx"), 1)
            pe.wait_ge(sem("b_inv"), 4)
            for t in range(NT):
                for h in range(MH):
                    last = pe.matmul(PS[:, 4 + t // 2, (t % 2) * D + h * MD:(t % 2) * D + (h + 1) * MD],
                                     TT[:, h, t, :], vb[:, t, h * MD:(h + 1) * MD], start=True, stop=True)
                if t % 2:
                    last.then_inc(sem("b_vn"), 1)
            pe.wait_ge(sem("b_vnsb"), 2)
            for t in range(NT):
                for h in range(MH):
                    last = pe.matmul(PS[:, 6 + t // 2, (t % 2) * D + h * MD:(t % 2) * D + (h + 1) * MD],
                                     IT[:, h, t, :], vnew[:, t, h * MD:(h + 1) * MD], start=True, stop=True)
                if t % 2:
                    last.then_inc(sem("b_o"), 1)
            tr_pe(pe, 5, tmp_tok, 0)
            pe.wait_ge(sem("tr_sb"), 10)
            tok_mm(pe, aT, wr, 2, sem("b_out"))

            tr_pe(pe, 6, xn_tok)
            pe.wait_ge(sem("tr_sb"), 12)
            pe.wait_ge(sem("c_zero"), 1)
            for t in range(NT):
                pe.matmul(PS[:, 4 + t, 0:D], zero8, wr[:, 0, :], start=True, stop=False)
            with pe.Fori(0, NEXP // 2) as i:
                def down(s):
                    pe.wait_ge(sem("c_hd"), i * 16 + s + 3)
                    for t in range(NT):
                        last = pe.matmul(PS[:, 4 + t, 0:D], hT[:, s % 4, t * P:(t + 1) * P],
                                         wd[s // 8][:, s % 8, :], start=False, stop=False)
                    last.then_inc(sem("c_dn"), 1)
                    if s % 8 == 7:
                        pe.drain().then_inc(sem(f"c_wfree{s // 8}"), 1)

                for s in range(16):
                    e2, c = s // 8, s % 8
                    if c == 0:
                        pe.wait_ge(sem(f"c_w{e2}"), i * 48 + 48)
                    pe.wait_ge(sem("c_hd"), i * 16 + s + 1)
                    for w, b0, name in ((wg, 0, "c_g"), (wu, 2, "c_u")):
                        for ki in range(KC):
                            last = pe.matmul(bank(b0 + s % 2), w[e2][:, ki, c * P:(c + 1) * P], xnT[:, ki],
                                             start=ki == 0, stop=ki == KC - 1)
                        last.then_inc(sem(name), 1)
                    if s >= 2:
                        down(s - 2)
                down(14)
                down(15)
            for t in range(NT):
                last = pe.matmul(PS[:, 4 + t, 0:D], zero8, wr[:, 0, :], start=False, stop=True)
            last.then_inc(sem("c_done"), 1)

            tr_pe(pe, 7, xn_tok)
            pe.wait_ge(sem("tr_sb"), 14)
            pe.wait_ge(sem("in_wq1"), 16)
            pe.wait_ge(sem("in_wk1"), 16)
            pe.wait_ge(sem("d_qz0"), 1)

            def q_mm(c):
                if c >= 2:
                    pe.wait_ge(sem("d_qa"), c - 1)
                    pe.wait_ge(sem("d_qd"), c - 1)
                for ki in range(KC):
                    last = pe.matmul(bank(c % 2), wq1[:, ki, c * P:(c + 1) * P], xnT[:, ki],
                                     start=ki == 0, stop=ki == KC - 1)
                last.then_inc(sem("d_q"), 1)

            q_mm(0)
            for c in range(FC):
                if c + 1 < FC:
                    q_mm(c + 1)
                pe.wait_ge(sem("d_qa"), c + 1)
                pe.wait_ge(sem("d_qd"), c + 1)
                for h2 in range(2):
                    for dc in range(KC):
                        if c:
                            pe.wait_ge(sem(f"d_ue{dc}"), 2 * (c - 1) + h2 + 1)
                        pe.matmul(bank(2 + 2 * h2 + dc), wkT1[:, c, dc * P:(dc + 1) * P],
                                  qz1[:, c % 2, h2, :], start=True, stop=True).then_inc(sem(f"d_u{dc}"), 1)
            with pe.Fori(0, B) as b:
                pe.wait_ge(sem("d_ctxT"), b * 16 + 16)
                pe.wait_ge(sem("d_ub"), b + 1)
                for hf in range(2):
                    for g in range(4 * hf, 4 * hf + 4):
                        for dc in range(KC):
                            last = pe.matmul(PS[:, hf, (g % 4) * P:(g % 4 + 1) * P],
                                             Ub[:, dc, g, :],
                                             ctxT1[:, dc, :].rearrange("p (m i) -> p m i", i=S)[:, :, g * GI:(g + 1) * GI],
                                             start=dc == 0, stop=dc == KC - 1)
                    last.then_inc(sem("d_sim"), 1)
                pe.wait_ge(sem("d_ctxG"), b * 16 + 16)
                for hf in range(2):
                    pe.wait_ge(sem("d_p"), b * 2 + hf + 1)
                    for g in range(4):
                        last = pe.transpose(PS[:, 2 + hf, g * P:(g + 1) * P], Z[:, hf, g, :], C("ident"))
                    last.then_inc(sem("d_t"), 1)
                for hf in range(2):
                    pe.wait_ge(sem("d_te"), b * 2 + hf + 1)
                    for dc in range(KC):
                        for g in range(4):
                            last = pe.matmul(PS[:, 4 + 2 * hf + dc, g * P:(g + 1) * P],
                                             ctxG[:, 4 * hf + g, dc * P:(dc + 1) * P], PTx[:, hf, g, :],
                                             start=True, stop=True)
                        last.then_inc(sem("d_w"), 1)
            pe.wait_ge(sem("in_wvo1"), 32)
            pe.wait_ge(sem("d_we0"), 2 * B)
            pe.wait_ge(sem("d_we1"), 2 * B)
            for c in range(FC):
                if c >= 2:
                    pe.wait_ge(sem("d_oe"), c - 1)
                for ki in range(KC):
                    for h2 in range(2):
                        last = pe.matmul(PS[64 * h2:64 * h2 + 64, c % 2, :],
                                         wv1[:, ki, (2 * c + h2) * XD:(2 * c + h2 + 1) * XD],
                                         U[:, ki, 2 * c + h2, :], start=ki == 0, stop=ki == KC - 1)
                last.then_inc(sem("d_o"), 1)
            pe.wait_ge(sem("d_oe"), FC)
            tok_mm(pe, hT, wo1, 2, sem("d_out"))

            tr_pe(pe, 8, xn_tok)
            pe.wait_ge(sem("tr_sb"), 16)
            pe.wait_ge(sem("in_wqkv"), 16)
            for mo in range(4):
                for ki in range(KC):
                    last = pe.matmul(bank(2 + mo), wqkv[:, ki, mo * P:(mo + 1) * P], xnT[:, ki],
                                     start=ki == 0, stop=ki == KC - 1)
                last.then_inc(sem("e_qk"), 1)
            tok_mm(pe, xnT, wqkv[:, :, 2 * D:3 * D], 6, sem("e_v"))
            pe.wait_ge(sem("e_qsb"), 4)
            pe.wait_ge(sem("e_ksb"), 2)
            for t in range(NT):
                for kc in range(KC):
                    for b2 in range(2):
                        tk = slice((2 * t + b2) * S, (2 * t + b2 + 1) * S)
                        last = pe.matmul(PS[64 * b2:64 * b2 + 64, 2 * t + kc, :], qTe[:, kc, tk],
                                         kTz[:, kc, :, tk], start=True, stop=True)
                    last.then_inc(sem("e_s"), 1)
            for t in range(NT):
                pe.wait_ge(sem("e_p"), t + 1)
                for g in range(4):
                    n = 4 * t + g
                    if n >= 4:
                        pe.wait_ge(sem("e_te"), n - 3)
                    if n == 0:
                        pe.wait_ge(sem("e_z"), 2 * NT)
                    for hh in range(4):
                        last = pe.transpose(PS[:, n % 4, hh * P:(hh + 1) * P], Pz[:, t, 4 * g + hh, :], C("ident"))
                    last.then_inc(sem("e_t"), 1)
                pe.wait_ge(sem("e_te"), 4 * t + 4)
                for h in range(H):
                    last = pe.matmul(PS[:, 4 + t // 2, (t % 2) * D + h * DK:(t % 2) * D + (h + 1) * DK],
                                     PzT[:, t % 2, h, :], ve[:, t, h * DK:(h + 1) * DK], start=True, stop=True)
                if t % 2:
                    last.then_inc(sem("e_o"), 1)
            tr_pe(pe, 9, tmp_tok, 0)
            pe.wait_ge(sem("tr_sb"), 18)
            pe.wait_ge(sem("in_wproj"), 16)
            tok_mm(pe, aT, wproj, 2, sem("e_out"))

            tr_pe(pe, 10, xn_tok)
            pe.wait_ge(sem("tr_sb"), 20)
            pe.wait_ge(sem("in_wrt"), 32)
            for t in range(NT):
                for ki in range(KC):
                    last = pe.matmul(PS[:, 2, t * NEXP:(t + 1) * NEXP], xnT[:, ki, t * P:(t + 1) * P],
                                     wrt[:, ki, :], start=ki == 0, stop=ki == KC - 1)
            last.then_inc(sem("f_log"), 1)
            pe.wait_ge(sem("f_oh"), 1)
            for t in range(NT):
                last = pe.transpose(PS[0:NEXP, 3, t * P:(t + 1) * P], oh8[:, t, :], C("ident"))
            last.then_inc(sem("f_oht"), 1)
            pe.wait_ge(sem("f_ohs"), 1)
            for e in range(NEXP):
                if e >= 2:
                    pe.wait_ge(sem("f_ch"), e - 1)
                a, _ = CONST_AT["rowsel"]
                pe.matmul(bank(e % 2), consts[0:NEXP, a + e * P:a + (e + 1) * P], ohT[0:NEXP],
                          start=True, stop=True).then_inc(sem("f_sel"), 1)
            pe.wait_ge(sem("f_ch"), NEXP)
            for t in range(NT):
                pe.matmul(PS[:, 4 + t, 0:D], ohT[0:NEXP, t * P:(t + 1) * P], b2f[0:NEXP],
                          start=True, stop=False)
            with pe.Fori(0, NEXP // 2) as i:
                def down(s):
                    pe.wait_ge(sem("f_hd"), i * 16 + s + 5)
                    for t in range(NT):
                        last = pe.matmul(PS[:, 4 + t, 0:D], hT[:, s % 4, t * P:(t + 1) * P],
                                         wf2[s // 8][:, s % 8, :], start=False, stop=False)
                    last.then_inc(sem("f_dn"), 1)
                    if s % 8 == 7:
                        pe.drain().then_inc(sem(f"f_wfree{s // 8}"), 1)

                for s in range(16):
                    e2, c = s // 8, s % 8
                    if c == 0:
                        pe.wait_ge(sem(f"f_w{e2}"), i * 48 + 48)
                    pe.wait_ge(sem("f_hd"), i * 16 + s + 1)
                    for ki in range(KC):
                        last = pe.matmul(bank(s % 4), wf1[e2][:, ki, c * P:(c + 1) * P], xnT[:, ki],
                                         start=ki == 0, stop=ki == KC - 1)
                    last.then_inc(sem("f_up"), 1)
                    if s >= 2:
                        down(s - 2)
                down(14)
                down(15)
            for t in range(NT):
                last = pe.matmul(PS[:, 4 + t, 0:D], zero8[0:NEXP], b2f[0:NEXP], start=False, stop=True)
            last.then_inc(sem("f_done"), 1)

        @block.scalar
        def _(act):
            act.sem_inc(sem("a_tev1"), 1)

            ln_act(act, 1)
            tr_act(act, 1, xnT)
            for mo in range(KC):
                act.wait_ge(sem("a_qps"), mo + 1)
                act.mul(qT0[:, mo], bank(2 + mo), DK ** -0.5).then_inc(sem("a_qsb"), 1)
            with act.Fori(0, B) as b:
                def exps(u):
                    act.wait_ge(sem("a_z"), b * 8 + u + 3)
                    act.activation(ring[:, u, :], ring[:, u, :], ACT.Exp, bias=nmax0[:, u:u + 1], scale=-1.0,
                                   accum_out=rsum0[:, u:u + 1]).then_inc(sem("a_exp"), 1)

                def evac(u):
                    act.wait_ge(sem("a_tps"), b * 16 + 2 * u + 18)
                    act.copy(pT[:, u // 4, u % 4, 4:8, :].rearrange("p a b -> p (a b)"), bank(5))\
                       .then_inc(sem("a_tev1"), 1)

                for n in range(4):
                    act.wait_ge(sem("a_kps"), b * 4 + n + 1)
                    act.copy(kT0[:, n // 2, (n % 2) * 512:(n % 2 + 1) * 512], bank(4 + n % 2))\
                       .then_inc(sem("a_kev"), 1)
                exps(0)
                exps(1)
                for n in range(4):
                    act.wait_ge(sem("a_vps"), b * 4 + n + 2)
                    act.copy(v0[:, 2 * n:2 * n + 2, :].rearrange("p a b -> p (a b)"), bank(4 + n % 2))\
                       .then_inc(sem("a_vev"), 1)
                for u in range(2, 8):
                    exps(u)
                    evac(u - 2)
                evac(6)
                evac(7)
            ln_act(act, 2)
            act.wait_ge(sem("in_vecs"), 32)
            tr_act(act, 2, xnT, 4, affine=True)
            for c in range(FC):
                act.wait_ge(sem("a2_h"), c + 1)
                act.activation(hT[:, c, :], bank(c % 4), ACT.Gelu, bias=cols[:, 4 + c:5 + c])\
                   .then_inc(sem("a2_g"), 1)
            ln_act(act, 3)

            ln_act(act, 4)
            tr_act(act, 3, xnT)
            for i in range(2):
                act.wait_ge(sem("b_v"), i + 1)
                act.copy(two(vb, i), bank(2 + i)).then_inc(sem("b_vsb"), 1)
            act.wait_ge(sem("b_ss"), 1)
            act.activation(rinvB, ssq, ACT.Sqrt).then_inc(sem("b_norm"), 1)
            dec, lal = cols[:, 12:12 + MH], cols[:, 12 + MH:12 + 2 * MH]
            ed, lg, alpha = small[:, 44:48], small[:, 48:52], small[:, 52:56]
            act.activation(ed, dec, ACT.Exp, scale=-1.0).then_inc(sem("b_ed"), 1)
            act.wait_ge(sem("b_ed1"), 1)
            act.activation(lg, small[:, 56:60], ACT.Ln).then_inc(sem("b_ln"), 1)
            act.activation(alpha, lal, ACT.Exp).then_inc(sem("b_al"), 1)
            act.wait_ge(sem("b_nlg"), 1)
            for h in range(MH):
                act.activation(decayed[:, h, :], C("dist"), ACT.Exp, scale=small[:, 60 + h:61 + h])\
                   .then_inc(sem("b_dec"), 1)
            act.wait_ge(sem("tr_ps"), 8)
            act.copy(rkT[:, 1], bank(5))
            act.copy(wkT[:, 1, :, 1:S], bank(5).rearrange("p (b s) -> p b s", b=B)[:, :, 0:S - 1])\
               .then_inc(sem("tr_sb"), 1)
            for k in range(1, LEVELS):
                for h in range(MH):
                    act.wait_ge(sem("b_x"), 4 * (k - 1) + h + 1)
                    act.copy(X[:, h].rearrange("p a b -> p (a b)"), bank(h)).then_inc(sem("b_xsb"), 1)
            for i in range(2):
                act.wait_ge(sem("b_vn"), i + 1)
                act.copy(two(vnew, i), bank(4 + i)).then_inc(sem("b_vnsb"), 1)
            tr_act(act, 5, aT)

            ln_act(act, 5)
            tr_act(act, 6, xnT)
            with act.Fori(0, NEXP // 2) as i:
                for s in range(16):
                    act.wait_ge(sem("c_g"), i * 16 + s + 1)
                    act.activation(sg[:, s % 2, :], bank(s % 2), ACT.Silu).then_inc(sem("c_sg"), 1)

            ln_act(act, 6)
            tr_act(act, 7, xnT)
            for c in range(FC):
                act.wait_ge(sem("d_q"), c + 1)
                if c == 0:
                    act.wait_ge(sem("d_qz0"), 1)
                if c >= 2:
                    act.wait_ge(sem("d_u0"), 2 * (c - 1))
                    act.wait_ge(sem("d_u1"), 2 * (c - 1))
                act.mul(qz1[0:64, c % 2, 0, :], PS[0:64, c % 2, :], XD ** -0.5).then_inc(sem("d_qa"), 1)
                for h2 in range(2):
                    act.wait_ge(sem("d_u1"), 2 * c + h2 + 1)
                    act.copy(U[:, 1, 2 * c + h2, :], bank(3 + 2 * h2)).then_inc(sem("d_ue1"), 1)
            with act.Fori(0, B) as b:
                for hf in range(2):
                    act.wait_ge(sem("d_z"), b * 2 + hf + 1)
                    act.activation(Z[:, hf], Z[:, hf], ACT.Exp).then_inc(sem("d_e"), 1)
                for hf in range(2):
                    act.wait_ge(sem("d_t"), b * 2 + hf + 1)
                    act.copy(PTx[:, hf].rearrange("p a b -> p (a b)"), bank(2 + hf)).then_inc(sem("d_te"), 1)
                for hf in range(2):
                    act.wait_ge(sem("d_w"), b * 4 + hf * 2 + 3)
                    act.copy(U[:, 1, :, bass.ds(b * S + hf * 32, 32)].rearrange("p h (g i) -> p g h i", g=4),
                             PS[:, 5 + 2 * hf, :].rearrange("p (g h i) -> p g h i", g=4, h=XH))\
                       .then_inc(sem("d_we1"), 1)
            for c in range(FC):
                act.wait_ge(sem("d_o"), c + 1)
                act.copy(hT[:, c, :], bank(c % 2)).then_inc(sem("d_oe"), 1)

            ln_act(act, 7)
            tr_act(act, 8, xnT)
            for mo in range(KC):
                act.wait_ge(sem("e_qk"), mo + 1)
                act.mul(qTe[:, mo, :], bank(2 + mo), DK ** -0.5).then_inc(sem("e_qsb"), 1)
            for i in range(2):
                act.wait_ge(sem("e_v"), i + 1)
                act.copy(two(ve, i), bank(6 + i)).then_inc(sem("e_qsb"), 1)
            for n in range(2 * NT):
                act.wait_ge(sem("e_z"), n + 1)
                v = Ze[:, n // 2, 8 * (n % 2):8 * (n % 2) + 8, :]
                act.activation(v, v, ACT.Exp).then_inc(sem("e_e"), 1)
            for n in range(4 * NT):
                act.wait_ge(sem("e_t"), n + 1)
                act.copy(PzT[:, n // 4 % 2, 4 * (n % 4):4 * (n % 4) + 4, :].rearrange("p a b -> p (a b)"),
                         bank(n % 4)).then_inc(sem("e_te"), 1)
            tr_act(act, 9, aT)
            ln_act(act, 8)
            ln_act(act, 9)
            tr_act(act, 10, xnT)
            act.wait_ge(sem("f_oht"), 1)
            act.copy(ohT[0:NEXP], PS[0:NEXP, 3, :]).then_inc(sem("f_ohs"), 1)
            for e in range(NEXP):
                act.wait_ge(sem("f_sel"), e + 1)
                act.copy(chosen[:, e, :], bank(e % 2)).then_inc(sem("f_ch"), 1)
            with act.Fori(0, NEXP // 2) as i:
                for s in range(16):
                    if s % 8 == 0:
                        act.wait_ge(sem(f"f_w{s // 8}"), i * 48 + 48)
                    act.wait_ge(sem("f_up"), i * 16 + s + 1)
                    act.wait_ge(sem("f_hd"), i * 16 + s + 3)
                    act.activation(rel[:, s % 2, :], bank(s % 4), ACT.Relu, bias=bf1[s // 8][:, s % 8:s % 8 + 1])\
                       .then_inc(sem("f_rel"), 1)

        @block.vector
        def _(dve):
            ch = Chain(dve, sem("dve_own"))
            dve.sem_inc(sem("a_z"), 2)
            dve.sem_inc(sem("a_tev0"), 1)
            dve.sem_inc(sem("a_ot"), 1)
            dve.sem_inc(sem("c_hd"), 2)
            dve.sem_inc(sem("f_hd"), 4)
            dve.memset(zero8, 0.0).then_inc(sem("c_zero"), 1)

            dve.wait_ge(sem("in_x"), 16)
            ln_dve(dve, ch, 1, x_tok, xn_tok).then_inc(sem("tr_src"), 1)
            tr_dve(dve, 1, xnT)
            dve.wait_ge(sem("a_qsb"), 2)
            dve.wait_ge(sem("in_const"), 16)
            with dve.Fori(0, B) as b:
                def scores(u):
                    dve.wait_ge(sem("a_s"), b * 8 + u + 1)
                    dve.wait_ge(sem(f"a_bias_in{u}"), b * 16 + 16)
                    settle(dve, "dve")
                    dve.tensor_tensor_reduce(out=ring[:, u, :], in0=bank(2 * (u % 2), 2), in1=ring[:, u, :],
                                             scale=-1.0, scalar=3e38, op0=ALU.add, op1=ALU.min,
                                             accum_out=nmax0[:, u:u + 1]).then_inc(sem("a_z"), 1)

                def evac(u):
                    dve.wait_ge(sem("a_tps"), b * 16 + 2 * u + 17)
                    dve.tensor_copy(pT[:, u // 4, u % 4, 0:4, :].rearrange("p a b -> p (a b)"), bank(4))\
                       .then_inc(sem("a_tev0"), 1)

                def inverse(kc):
                    dve.wait_ge(sem("a_exp"), b * 8 + 4 * kc + 4)
                    ch.step(dve.reciprocal(rinv0, rsum0[:, 4 * kc:4 * kc + 4]))
                    dve.tensor_tensor(rdiag, bcast(rinv0, 2, (4, 32)), bcast(C("pair32"), 1, (4, 32)),
                                      ALU.mult).then_inc(sem("a_rl"), 1)

                def outputs(kc):
                    dve.wait_ge(sem("a_pv"), b * 2 + kc + 1)
                    ch.step(dve.tensor_scalar(osel, PS[:, 6, 0:S], C("half2")[:, 0:1], None, ALU.mult))
                    ch.step(dve.scalar_tensor_tensor(osel2, PS[:, 6, S:2 * S], C("half2")[:, 1:2], osel,
                                                     ALU.mult, ALU.add))
                    dve.tensor_tensor(aT[:, kc, bass.ds(b * S, S)], osel2, PS[:, 7, 0:S], ALU.mult)\
                       .then_inc(sem("a_ot"), 1)

                ch.enter(b, 7)
                for kc in range(KC):
                    last = dve.tensor_tensor(qz0[:, kc], bcast(qT0[:, kc, bass.ds(b * S, S)], 1, (8, S)),
                                             bcast(C("head8"), 2, (8, S)), ALU.mult)
                    if kc == 0:
                        ch.add(last)
                last.then_inc(sem("a_qz"), 1)
                scores(0)
                scores(1)
                for u in range(2, 8):
                    scores(u)
                    evac(u - 2)
                    if u == 5:
                        inverse(0)
                    if u == 6:
                        outputs(0)
                evac(6)
                evac(7)
                inverse(1)
                outputs(1)
                ch.leave(B)

            for i in range(2):
                dve.wait_ge(sem("a2_o"), i + 1)
                ch.add(dve.tensor_tensor(two(y_tok, i), bank(i), two(xn_tok, i), ALU.add))
            ch.sync()
            ln_dve(dve, ch, 2, y_tok, tmp_tok).then_inc(sem("tr_src"), 1)
            dve.wait_ge(sem("in_vecs"), 32)
            tr_dve(dve, 2, xnT, 4, affine=True)
            for i in range(2):
                dve.wait_ge(sem("a2_y"), i + 1)
                ch.add(dve.tensor_tensor(two(tmp_tok, i), bank(4 + i), two(y_tok, i), ALU.add))
            ch.sync()
            for i in range(2):
                ch.add(dve.tensor_tensor(pair(tmp_tok, i), pair(tmp_tok, i), vec(V_B2), ALU.add))
            ch.sync()
            ch.step(ln_dve(dve, ch, 3, tmp_tok, y_tok))
            for i in range(2):
                ch.add(dve.tensor_tensor(pair(y_tok, i), pair(y_tok, i), vec(V_G2), ALU.mult))
            ch.sync()
            for i in range(2):
                ch.add(dve.tensor_tensor(pair(y_tok, i), pair(y_tok, i), vec(V_BE2), ALU.add))
            ch.sync()
            dve.tensor_tensor(x_tok[:], x_tok[:], y_tok[:], ALU.add).then_inc(sem("x_tok"), 1)
            dve.wait_ge(sem("x_tok"), 1)

            ln_dve(dve, ch, 4, x_tok, xn_tok).then_inc(sem("tr_src"), 1)
            tr_dve(dve, 3, xnT)
            heads = lambda ap: ap[:].rearrange("p t (h d) -> p (t h) d", h=MH)
            dve.wait_ge(sem("tr_src"), 3)
            ch.step(dve.tensor_tensor(tmp_tok[:], xn_tok[:], xn_tok[:], ALU.mult))
            dve.reduce_sum(ssq, heads(tmp_tok), axis=AX.X).then_inc(sem("b_ss"), 1)
            dve.wait_ge(sem("b_norm"), 1)
            ch.step(dve.tensor_scalar_max(rinvB, rinvB, 1e-12))
            ch.step(dve.reciprocal(rinvB, rinvB))
            dve.tensor_tensor(heads(tmp_tok), heads(xn_tok), bcast(rinvB, 2, (NT * MH, MD)), ALU.mult)\
               .then_inc(sem("tr_src"), 1)
            dve.wait_ge(sem("b_ed"), 1)
            dve.tensor_scalar_add(small[:, 56:60], small[:, 44:48], 1.0).then_inc(sem("b_ed1"), 1)
            dve.wait_ge(sem("b_ln"), 1)
            dve.tensor_scalar_mul(small[:, 60:64], small[:, 48:52], -1.0).then_inc(sem("b_nlg"), 1)
            ch.step(dve.reciprocal(small[:, 192:196], small[:, 56:60]))
            ch.step(dve.tensor_tensor(low0g, bcast(C("low0"), 1, (MH, P)), bcast(small[:, 192:196], 2, (MH, P)),
                                      ALU.mult))
            ch.step(dve.memset(wkT[:, :, :, 0:1], 0.0))
            dve.wait_ge(sem("tr_ps"), 7)
            ch.add(dve.tensor_copy(rkT[:, 0], bank(4)))
            dve.tensor_copy(wkT[:, 0, :, 1:S], bank(4).rearrange("p (b s) -> p b s", b=B)[:, :, 0:S - 1])\
               .then_inc(sem("tr_sb"), 1)
            dve.wait_ge(sem("b_dec"), MH)
            ch.step(dve.tensor_tensor(decayed, decayed, bcast(C("upper"), 1, (MH, P)), ALU.mult))
            tiles = lambda ap: bcast(ap, 1, (NT, P))
            for h in range(MH):
                dve.wait_ge(sem("b_gram"), h + 1)
                gram = PS[:, h, :].rearrange("p (t c) -> p t c", t=NT)
                cross = PS[:, 4 + h, :].rearrange("p (t c) -> p t c", t=NT)
                ch.add(dve.tensor_tensor(MT[:, h], gram, tiles(decayed[:, h, :]), ALU.mult))
                ch.add(dve.tensor_tensor(IT[:, h], cross, tiles(decayed[:, h, :]), ALU.mult))
                ch.step(dve.tensor_tensor(T[:, h], gram, tiles(low0g[:, h, :]), ALU.mult))
                ch.add(dve.tensor_tensor(T[:, h], tiles(C("ident")), T[:, h], ALU.subtract))
                ch.step(dve.tensor_tensor(TT[:, h], MT[:, h], tiles(C("up0")), ALU.mult))
                ch.step(dve.tensor_tensor(TT[:, h], tiles(C("ident")), TT[:, h], ALU.subtract))
                dve.tensor_tensor(CT[:, h], MT[:, h], tiles(C("up1")), ALU.mult).then_inc(sem("b_ct"), 1)
            for k in range(1, LEVELS):
                for h in range(MH):
                    dve.wait_ge(sem("b_tx"), 4 * (k - 1) + h + 1)
                    new_tt = PS[:, h, :].rearrange("p (t c) -> p t c", t=NT)
                    new_t = PS[:, 4 + h, :].rearrange("p (t c) -> p t c", t=NT)
                    if k == LEVELS - 1:
                        dve.tensor_tensor(TT[:, h], TT[:, h], new_tt, ALU.subtract).then_inc(sem("b_inv"), 1)
                        continue
                    ch.add(dve.tensor_tensor(TT[:, h], TT[:, h], new_tt, ALU.subtract))
                    ch.add(dve.tensor_tensor(T[:, h], T[:, h], new_t, ALU.subtract))
                    dve.tensor_tensor(CT[:, h], MT[:, h], tiles(C(f"up{k + 1}")), ALU.mult)\
                       .then_inc(sem("b_ct"), 1)
            dve.wait_ge(sem("b_al"), 1)
            for i in range(2):
                dve.wait_ge(sem("b_o"), i + 1)
                last = dve.tensor_tensor(pair(tmp_tok, i).rearrange("p t (h d) -> p t h d", h=MH),
                                         PS[:, 6 + i, :].rearrange("p (t h d) -> p t h d", t=2, h=MH),
                                         bcast(bcast(small[:, 52:56], 1, (2, MH)), 3, (2, MH, MD)), ALU.mult)
                if i == 0:
                    ch.add(last)
            last.then_inc(sem("tr_src"), 1)
            tr_dve(dve, 5, aT)
            ch.step(dve.tensor_tensor(x_tok[:], x_tok[:], xn_tok[:], ALU.add))
            for i in range(2):
                dve.wait_ge(sem("b_out"), i + 1)
                ch.add(dve.tensor_tensor(two(x_tok, i), bank(2 + i), two(x_tok, i), ALU.add))
            ch.sync()
            dve.sem_inc(sem("x_tok"), 1)

            ln_dve(dve, ch, 5, x_tok, xn_tok).then_inc(sem("tr_src"), 1)
            tr_dve(dve, 6, xnT)
            with dve.Fori(0, NEXP // 2) as i:
                for s in range(16):
                    dve.wait_ge(sem("c_sg"), i * 16 + s + 1)
                    dve.wait_ge(sem("c_u"), i * 16 + s + 1)
                    dve.wait_ge(sem("c_dn"), i * 16 + s + 1)
                    dve.tensor_tensor(hT[:, s % 4, :], bank(2 + s % 2), sg[:, s % 2, :], ALU.mult)\
                       .then_inc(sem("c_hd"), 1)
            dve.wait_ge(sem("c_done"), 1)
            for t in range(NT):
                ch.add(dve.tensor_tensor(x_tok[:, t, :], PS[:, 4 + t, 0:D], x_tok[:, t, :], ALU.add))
            ch.sync()
            dve.sem_inc(sem("x_tok"), 1)

            ln_dve(dve, ch, 6, x_tok, xn_tok).then_inc(sem("tr_src"), 1)
            dve.memset(qz1[:], 0.0).then_inc(sem("d_qz0"), 1)
            tr_dve(dve, 7, xnT)
            dve.wait_ge(sem("d_qz0"), 1)
            for c in range(FC):
                dve.wait_ge(sem("d_q"), c + 1)
                dve.wait_ge(sem("d_qa"), c + 1)
                dve.tensor_scalar_mul(qz1[64:128, c % 2, 1, :], PS[64:128, c % 2, :], XD ** -0.5)\
                   .then_inc(sem("d_qd"), 1)
                for h2 in range(2):
                    dve.wait_ge(sem("d_u0"), 2 * c + h2 + 1)
                    dve.tensor_copy(U[:, 0, 2 * c + h2, :], bank(2 + 2 * h2)).then_inc(sem("d_ue0"), 1)
            dve.wait_ge(sem("d_ue1"), 2 * FC)
            dve.wait_ge(sem("d_ue0"), 2 * FC)
            with dve.Fori(0, B) as b:
                ch.enter(b, 9)
                settle(dve, "dve")
                for dc in range(KC):
                    last = dve.tensor_copy(Ub[:, dc].rearrange("p g (h i) -> p g h i", i=GI),
                                           U[:, dc, :, bass.ds(b * S, S)].rearrange("p h (g i) -> p g h i", i=GI))
                    if dc == 0:
                        ch.add(last)
                last.then_inc(sem("d_ub"), 1)
                for hf in range(2):
                    dve.wait_ge(sem("d_sim"), b * 2 + hf + 2)
                    ch.step(dve.tensor_tensor(Z[:, hf], PS[:, hf, :].rearrange("p (g c) -> p g c", g=4),
                                              bcast(C("group"), 1, (4, P)), ALU.add))
                    ch.step(dve.reduce_max(mx1[:, hf, :], Z[:, hf], axis=AX.X))
                    dve.tensor_tensor(Z[:, hf], Z[:, hf], bcast(mx1[:, hf, :], 2, (4, P)), ALU.subtract)\
                       .then_inc(sem("d_z"), 1)
                for hf in range(2):
                    dve.wait_ge(sem("d_e"), b * 2 + hf + 1)
                    ch.step(dve.reduce_sum(rs1[:, hf, :], Z[:, hf], axis=AX.X))
                    ch.step(dve.reciprocal(ri1[:, hf, :], rs1[:, hf, :]))
                    dve.tensor_tensor(Z[:, hf], Z[:, hf], bcast(ri1[:, hf, :], 2, (4, P)), ALU.mult)\
                       .then_inc(sem("d_p"), 1)
                for hf in range(2):
                    dve.wait_ge(sem("d_w"), b * 4 + hf * 2 + 2)
                    settle(dve, "dve")
                    dve.tensor_copy(U[:, 0, :, bass.ds(b * S + hf * 32, 32)].rearrange("p h (g i) -> p g h i", g=4),
                                    PS[:, 4 + 2 * hf, :].rearrange("p (g h i) -> p g h i", g=4, h=XH))\
                       .then_inc(sem("d_we0"), 1)
                ch.leave(B)
            ch.step(dve.tensor_tensor(pair(x_tok, 0), pair(x_tok, 0), vec(V_BOUT), ALU.add))
            ch.step(dve.tensor_tensor(pair(x_tok, 1), pair(x_tok, 1), vec(V_BOUT), ALU.add))
            for i in range(2):
                dve.wait_ge(sem("d_out"), i + 1)
                ch.add(dve.tensor_tensor(two(x_tok, i), bank(2 + i), two(x_tok, i), ALU.add))
            ch.sync()
            dve.sem_inc(sem("x_tok"), 1)

            ln_dve(dve, ch, 7, x_tok, xn_tok).then_inc(sem("tr_src"), 1)
            tr_dve(dve, 8, xnT)
            for kc in range(KC):
                dve.wait_ge(sem("e_qk"), 3 + kc)
                dve.tensor_tensor(kTz[:, kc], bcast(bank(4 + kc), 1, (8, TOK)), bcast(C("head8"), 2, (8, TOK)),
                                  ALU.mult).then_inc(sem("e_ksb"), 1)
            ch.step(dve.memset(Pz[:], 0.0))
            for n in range(2 * NT):
                t, hs = n // 2, slice(8 * (n % 2), 8 * (n % 2) + 8)
                s3 = PS[:, n, :].rearrange("p (h k) -> p h k", h=8)
                dve.wait_ge(sem("e_s"), n + 1)
                ch.step(dve.reduce_max(mxe[:, t, hs], s3, axis=AX.X))
                dve.tensor_tensor(Ze[:, t, hs, :], s3, bcast(mxe[:, t, hs], 2, (8, S)), ALU.subtract)\
                   .then_inc(sem("e_z"), 1)
            for t in range(NT):
                dve.wait_ge(sem("e_e"), 2 * t + 2)
                ch.step(dve.reduce_sum(rse[:, t, :], Ze[:, t], axis=AX.X))
                ch.step(dve.reciprocal(rie[:, t, :], rse[:, t, :]))
                for b2 in range(2):
                    r = slice(64 * b2, 64 * b2 + 64)
                    last = dve.tensor_tensor(Pz[r, t, :, 64 * b2:64 * b2 + 64], Ze[r, t],
                                             bcast(rie[r, t, :], 2, (H, S)), ALU.mult)
                    if b2 == 0:
                        ch.add(last)
                last.then_inc(sem("e_p"), 1)
            for i in range(2):
                dve.wait_ge(sem("e_o"), i + 1)
                last = dve.tensor_copy(two(tmp_tok, i), bank(4 + i))
                if i == 0:
                    ch.add(last)
            last.then_inc(sem("tr_src"), 1)
            tr_dve(dve, 9, aT)
            ch.step(ln_dve(dve, ch, 8, xn_tok, y_tok))
            for i in range(2):
                ch.step(dve.tensor_tensor(pair(y_tok, i), pair(y_tok, i), vec(V_LNG), ALU.mult))
                ch.step(dve.tensor_tensor(pair(y_tok, i), pair(y_tok, i), vec(V_LNB), ALU.add))
                ch.step(dve.tensor_tensor(pair(y_tok, i), pair(y_tok, i), vec(V_BPROJ), ALU.add))
                dve.wait_ge(sem("e_out"), i + 1)
                ch.step(dve.tensor_tensor(two(y_tok, i), bank(2 + i), two(y_tok, i), ALU.add))
                ch.step(dve.tensor_tensor(two(x_tok, i), two(x_tok, i), two(y_tok, i), ALU.add))
            dve.sem_inc(sem("x_tok"), 1)

            ln_dve(dve, ch, 9, x_tok, xn_tok).then_inc(sem("tr_src"), 1)
            tr_dve(dve, 10, xnT)
            dve.wait_ge(sem("f_log"), 1)
            router_b = bcast(vecs[:, V_RBR, 0:NEXP], 1, (NT, NEXP))
            ch.step(dve.tensor_tensor(logit, PS[:, 2, 0:NT * NEXP].rearrange("p (t e) -> p t e", t=NT), router_b,
                                      ALU.add))
            ch.step(dve.reduce_max(top, logit, axis=AX.X))
            ch.step(dve.tensor_tensor(eq8, logit, bcast(top, 2, (NT, NEXP)), ALU.is_equal))
            ch.step(dve.tensor_tensor(eq8, eq8, bcast(C("first"), 1, (NT, NEXP)), ALU.mult))
            ch.step(dve.reduce_max(top, eq8, axis=AX.X))
            dve.tensor_tensor(oh8, eq8, bcast(top, 2, (NT, NEXP)), ALU.is_equal).then_inc(sem("f_oh"), 1)
            dve.wait_ge(sem("f_ch"), NEXP)
            with dve.Fori(0, NEXP // 2) as i:
                for s in range(16):
                    dve.wait_ge(sem("f_rel"), i * 16 + s + 1)
                    dve.wait_ge(sem("f_dn"), i * 16 + s + 1)
                    dve.tensor_tensor(hT[:, s % 4, :], rel[:, s % 2, :],
                                      chosen[:, bass.ds(i * 2 + s // 8, 1), :].rearrange("p a n -> p (a n)"), ALU.mult)\
                       .then_inc(sem("f_hd"), 1)
            dve.wait_ge(sem("f_done"), 1)
            for t in range(NT):
                ch.add(dve.tensor_tensor(x_tok[:, t, :], PS[:, 4 + t, 0:D], x_tok[:, t, :], ALU.add))
            ch.sync()
            dve.sem_inc(sem("x_tok"), 1)


def kernel(**inputs):
    import concourse.bacc as bacc
    from concourse.bass_utils import run_bass_kernel_spmd as run

    a = {k: np.asarray(v) for k, v in inputs.items()}
    t = lambda k: np.ascontiguousarray(a[k].T)
    ctx = a["ctx_1024"]
    cols = np.concatenate([
        a["L0_xattn_g1"].reshape(KC, P).T, a["L0_xattn_be1"].reshape(KC, P).T,
        a["L0_xattn_b1"].reshape(FC, P).T,
        np.broadcast_to(a["L0_attn_decay"], (P, MH)), np.broadcast_to(a["L0_attn_log_alpha"], (P, MH))], 1)
    vecs = np.zeros((NVEC, D), np.float32)
    for i, k in enumerate(["L0_xattn_b2", "L0_xattn_g2", "L0_xattn_be2", "L1_xattn_bout", "L1_attn_b_proj",
                           "L1_attn_ln_gamma", "L1_attn_ln_beta"]):
        vecs[i] = a[k]
    vecs[V_RBR, :NEXP] = a["L1_ffn_br"]
    arrays = {
        "x": a["x"].reshape(TOK, D), "bias": a["fside_Bx16xSxS2_0"], "consts": CONST,
        "ctxT": ctx.transpose(0, 2, 1),
        "ctxG": ctx.reshape(B, GM, GRP, GI, D).transpose(0, 1, 3, 2, 4).reshape(B, P, GRP, D),
        "wq0": t("L0_xattn_Wq"), "wk0": t("L0_xattn_Wk"), "wv0": t("L0_xattn_Wv"), "wo0": t("L0_xattn_Wo"),
        "w1_0": t("L0_xattn_W1"), "w2_0": t("L0_xattn_W2"), "ww": t("L0_attn_Ww"), "wr": t("L0_attn_Wr"),
        "wg": a["L0_ffn_Wg"], "wu": a["L0_ffn_Wu"], "wd": a["L0_ffn_Wd"],
        "wq1": a["L1_xattn_Wq"], "wkT1": a["L1_xattn_Wkv"][:, :XH * XD].T, "wv1": a["L1_xattn_Wkv"][:, XH * XD:],
        "wo1": a["L1_xattn_Wout"], "wqkv": t("L1_attn_W_qkv"), "wproj": t("L1_attn_W_proj"),
        "wrt": t("L1_ffn_Wr"), "b2f": a["L1_ffn_b2"],
        "w1f": a["L1_ffn_W1"].transpose(0, 2, 1), "w2f": a["L1_ffn_W2"].transpose(0, 2, 1),
        "b1f": a["L1_ffn_b1"].reshape(NEXP, FC, P).transpose(0, 2, 1),
        "cols": cols, "vecs": vecs,
    }
    nc = bacc.Bacc("TRN2", target_bir_lowering=False, num_devices=1)
    A, sent = {}, {}
    for k, v in arrays.items():
        v = np.ascontiguousarray(v)
        sent[f"in_{k}"] = v
        A[k] = nc.dram_tensor(f"in_{k}", v.shape, mybir.dt.from_np(v.dtype), kind="ExternalInput").ap()
    out = nc.dram_tensor("out", (TOK, D), F32, kind="ExternalOutput").ap()
    perceiver(nc, A, out)
    r = run(nc, [sent], core_ids=[0])
    return r.results[0]["out"].reshape(B, S, D)
```

```python
import numpy as np

import concourse.bass as bass
from concourse import mybir
from concourse.alu_op_type import AluOpType as ALU

F32 = mybir.dt.float32
F32R = mybir.dt.float32r
ACT = mybir.ActivationFunctionType
AX = mybir.AxisListType

P = 128
B, S, D = 8, 64, 256
TOK = B * S
NT = TOK // P
KC = D // P
KEYS = 1024
KT = KEYS // P
H, DK = 16, 16
FF, FC = 1024, 8
NEXP = 8
NB = NT + NEXP - 1
ROW1 = KC * FF + FC * D + FC
MH, MD = 4, 64
LEVELS = 6
XH, XD = 16, 64
GRP, GI = 8, 8
GM = KEYS // S
EPS = 1e-5
BIG = 1e30


def const_layout():
    p = np.arange(P)[:, None]
    c = np.arange(P)[None, :]
    c8 = np.arange(8)[None, :]
    i, j = c, p
    same = (i // S) == (j // S)
    parts = {
        "ident": (p == c),
        "head8": (p // DK == c8),
        "pair32": (p // 64 == np.arange(32)[None, :] // DK),
        "pick64": (p % 64 == np.arange(64)[None, :]),
        "half2": ((p % 32) // DK == np.arange(2)[None, :]),
        "group": np.where(p % GI == c % GI, 0.0, -BIG),
        "upper": same & (i > j),
        "dist": np.where(same & (i > j), i - j, 0),
        "low0": same & (p % 2 == 1) & (c == p - 1),
        "first": np.broadcast_to(8.0 - c8, (P, 8)),
        "ones": np.ones((P, P)),
        "earlier": (p < c),
        "column": np.broadcast_to(c, (P, P)),
        "row": p,
        "full": np.broadcast_to(P * np.arange(NT), (P, NT)),
        "before": np.broadcast_to((P * (c8.T > c8)).reshape(1, -1), (P, NEXP * NEXP)),
        "upto": np.broadcast_to((P * (c8.T >= c8)).reshape(1, -1), (P, NEXP * NEXP)),
        "block": np.broadcast_to(P * np.arange(NB), (P, NB)),
        "slot": p + P * np.arange(NB),
    }
    for k in range(LEVELS):
        s = 2 ** k
        parts[f"up{k}"] = (i // (2 * s) == j // (2 * s)) & (i // s % 2 == 1) & (j // s % 2 == 0)
    at, where, cols = 0, {}, []
    for name, a in parts.items():
        a = np.asarray(a, np.float32)
        where[name] = (at, at + a.shape[1])
        at += a.shape[1]
        cols.append(a)
    return where, np.concatenate(cols, 1)


CONST_AT, CONST = const_layout()
NVEC = 8
V_B2, V_G2, V_BE2, V_BOUT, V_BPROJ, V_LNG, V_LNB, V_RBR = range(NVEC)


TILES = [("V", n) for n in range(4)] + [("T", u, g) for u in range(6) for g in range(2)]
TILES += [("K", n) for n in range(4)] + [("T", u, g) for u in (6, 7) for g in range(2)]


def tile_bank(*tile):
    return 4 + TILES.index(tile) % 3


class Chain:

    def __init__(self, eng, sem):
        self.eng, self.sem, self.base, self.n = eng, sem, 0, 0

    def add(self, ins):
        self.n += 1
        return ins.then_inc(self.sem, 1)

    def sync(self):
        self.eng.wait_ge(self.sem, self.base + self.n)

    def step(self, ins):
        self.add(ins)
        self.sync()

    def enter(self, i, per):
        self.before, self.per = self.base + self.n, per
        self.base, self.n = i * per + self.before, 0

    def leave(self, times):
        assert self.n == self.per, self.n
        self.base, self.n = self.before + times * self.per, 0


def perceiver(nc, A, out):
    sems = {}

    def sem(name):
        if name not in sems:
            sems[name] = nc.alloc_semaphore(name)
        return sems[name]

    def sb(name, *shape):
        return nc.alloc_sbuf_tensor(name, [P, *shape], F32)

    consts = sb("consts", CONST.shape[1])
    x_tok = sb("x_tok", NT, D)
    xn_tok = sb("xn_tok", NT, D)
    y_tok = sb("y_tok", NT, D)
    tmp_tok = sb("tmp_tok", NT, D)
    xnT = sb("xnT", KC, TOK)
    aT = sb("aT", KC, TOK)
    vecs = sb("vecs", NVEC, D)
    cols = sb("cols", 12 + 2 * MH)
    small = sb("small", 256)
    hT = sb("hT", FC, TOK)
    xnT_h = nc.alloc_sbuf_tensor("xnT_h", [P, KC, TOK], F32R)
    xnT_l = nc.alloc_sbuf_tensor("xnT_l", [P, KC, TOK], F32R)
    arena_base = nc.sbuf_base
    arena = sb("arena", 36000)
    PS = nc.alloc_psum_tensor("PS", [P, 8, 512], F32)

    def C(name):
        a, b = CONST_AT[name]
        return consts[:, a:b]

    class Carve:
        def __init__(self, at=0):
            self.at = at

        def __call__(self, *shape):
            n = int(np.prod(shape))
            v = arena[:, self.at:self.at + n]
            self.at += n
            assert self.at <= 36000, self.at
            if len(shape) == 1:
                return v
            names = "abcd"[:len(shape)]
            return v.rearrange(f"p ({' '.join(names)}) -> p {' '.join(names)}",
                               **{k: s for k, s in zip(names[1:], shape[1:])})

    def carve_r(carve, name, *shape):
        carve.at += -(arena_base // 4 + carve.at) % 8
        t = nc.alloc_sbuf_tensor_at(name, [P, *shape], F32R, offset=arena_base + 4 * carve.at)
        carve.at += int(np.prod(shape))
        assert carve.at <= 36000, carve.at
        return t

    def wide(ap):
        return ap.bitcast(F32)

    def bank(n, k=1):
        return PS[:, n:n + k, :].rearrange("p a b -> p (a b)")

    def bcast(ap, axis, shape):
        return ap.unsqueeze(axis).to_broadcast([ap.shape[0], *shape])

    def settle(eng):
        eng.sem_inc(sem("waited"), 1)

    stats = small[:, 0:24].rearrange("p (t s) -> p t s", t=NT)
    mv = small[:, 24:32].rearrange("p (t s) -> p t s", t=NT)
    var_eps, std, rstd = small[:, 32:36], small[:, 36:40], small[:, 40:44]

    zero8 = small[:, 64:64 + P]

    ca = Carve()
    w1_0, w2_0 = ca(KC, FF), ca(FC, D)
    ww, wr, wo0 = ca(KC, D), ca(KC, D), ca(KC, D)
    after_w = ca.at
    ca = Carve()
    pT = ca(4, KT, P)
    rsum0, nmax0, rinv0 = ca(8), ca(8), ca(4)
    ca.at = after_w
    ring = ca(8, KEYS)
    ctxT0 = hT[:].rearrange("p a b -> p (a b)")[:, 0:KC * KEYS].rearrange("p (k n) -> p k n", k=KC)
    v0 = hT[:].rearrange("p a b -> p (a b)")[:, KC * KEYS:].rearrange("p (k n) -> p k n", k=KT)
    ctx_h, ctx_l = carve_r(ca, "ctx_h", KC, KEYS), carve_r(ca, "ctx_l", KC, KEYS)
    kT_h, kT_l = carve_r(ca, "kT_h", KC, KEYS), carve_r(ca, "kT_l", KC, KEYS)
    qz_h, qz_l = carve_r(ca, "qz_h", KC, 8, S), carve_r(ca, "qz_l", KC, 8, S)
    q_h, q_l = carve_r(ca, "q_h", KC, TOK), carve_r(ca, "q_l", KC, TOK)
    wk_h, wk_l = carve_r(ca, "wk_h", KC, D), carve_r(ca, "wk_l", KC, D)
    wv_h, wv_l = carve_r(ca, "wv_h", KC, D), carve_r(ca, "wv_l", KC, D)
    qT0 = ca(KC, TOK)
    wq0, wk0, wv0 = ca(KC, D), ca(KC, D), ca(KC, D)
    rdiag = ca(4, 32)
    osel, osel2 = ca(S), ca(S)
    cb = Carve(after_w)
    decayed = cb(MH, P)
    low0g = cb(MH, P)
    MT, IT, T, TT, CT, X = (cb(MH, NT, P) for _ in range(6))
    vb, vnew = cb(NT, D), cb(NT, D)
    rkT, wkT = cb(KC, TOK), cb(KC, B, S)
    ssq, rinvB = cb(NT * MH), cb(NT * MH)
    cc = Carve(cb.at)
    CW = 6 * P
    stage = [cc(FC, CW) for _ in range(2)]
    cc = Carve(0)
    w_h, w_l = carve_r(cc, "w_h", 4, CW), carve_r(cc, "w_l", 4, CW)
    h_h, h_l = carve_r(cc, "h_h", 4, TOK), carve_r(cc, "h_l", 4, TOK)
    sg, hm = cc(2, TOK), cc(2, TOK)
    assert cc.at <= cb.at
    cd = Carve()
    U = cd(KC, XH, TOK)
    wq1, wkT1, wv1, wo1 = cd(KC, FF), cd(FC, D), cd(KC, FF), cd(FC, D)
    hT_flat = hT[:].rearrange("p a b -> p (a b)")
    ctxT1 = [cd(KC, KEYS), hT_flat[:, 0:KC * KEYS].rearrange("p (k n) -> p k n", k=KC)]
    ctxG = [cd(GRP, D), hT_flat[:, KC * KEYS:].rearrange("p (g n) -> p g n", g=GRP)]
    Ub = cd(KC, GRP, P)
    Z, PTx = cd(2, 4, P), cd(2, 4, P)
    qz1 = cd(2, 2, TOK)
    mx1, rs1, ri1 = cd(2, 4), cd(2, 4), cd(2, 4)
    ce = Carve()
    wqkv, wproj = ce(KC, 3 * D), ce(KC, D)
    qTe = ce(KC, TOK)
    kTz = ce(KC, 8, TOK)
    ve = ce(NT, D)
    Ze = ce(NT, H, S)
    Pz = ce(NT, H, P)
    PzT = ce(2, H, P)
    mxe, rse, rie = ce(NT, H), ce(NT, H), ce(NT, H)
    cf = Carve()
    wblk = cf(3, ROW1)
    wf1 = [wblk[:, j, 0:KC * FF].rearrange("p (k n) -> p k n", k=KC) for j in range(3)]
    wf2 = [wblk[:, j, KC * FF:KC * FF + FC * D].rearrange("p (k n) -> p k n", k=FC) for j in range(3)]
    bf1 = [wblk[:, j, KC * FF + FC * D:] for j in range(3)]
    wrt, b2f = cf(KC, NEXP), cf(D)
    logit, eq8, oh8 = cf(NT, NEXP), cf(NT, NEXP), cf(NT, NEXP)
    top = cf(NT)
    ohT8 = cf(TOK)
    over, blocks8 = cf(NEXP, NT), cf(NEXP)
    ends3, ends, starts3, starts = cf(NEXP, NEXP), cf(NEXP), cf(NEXP, NEXP), cf(NEXP)
    ended, owner, owner_row = cf(NB, NEXP), cf(NB), cf(NB)
    place3, place = cf(NT, NEXP), cf(NT)
    rel_place = cf(NB, NT)
    placed = cf(NT, P)
    placeT = cf(TOK)
    xg = cf(KC, P)
    hb = cf(FC, P)
    xn_h, xn_l = carve_r(cf, "xn_h", NT, D), carve_r(cf, "xn_l", NT, D)
    pick = carve_r(cf, "pick", 3, NT, P)
    pickT = carve_r(cf, "pickT", 3, TOK)
    yb_h, yb_l = carve_r(cf, "yb_h", D), carve_r(cf, "yb_l", D)
    rows = nc.alloc_sbuf_tensor_at("rows", [P, NB], mybir.dt.int32, offset=arena_base + 4 * cf.at)
    cf(NB)

    def ln_dve(dve, ch, k, src, dst):
        for t in range(NT):
            ch.add(dve.bn_stats(stats[:, t, :], src[:, t, :]))
        ch.sync()
        for t in range(NT):
            ch.add(dve.bn_aggr(mv[:, t, :], stats[:, t, :]))
        ch.sync()
        dve.tensor_scalar_add(var_eps, mv[:, :, 1], EPS).then_inc(sem("ln_var"), 1)
        dve.wait_ge(sem("ln_std"), k)
        ch.step(dve.reciprocal(rstd, std))
        for t in range(NT):
            last = dve.tensor_scalar(dst[:, t, :], src[:, t, :], mv[:, t, 0:1], rstd[:, t:t + 1],
                                     ALU.subtract, ALU.mult)
            if t < NT - 1:
                ch.add(last)
        return last

    def ln_act(act, k):
        act.wait_ge(sem("ln_var"), k)
        act.activation(std, var_eps, ACT.Sqrt).then_inc(sem("ln_std"), 1)

    def tr_pe(pe, k, src, b0=0):
        pe.wait_ge(sem("tr_src"), k)
        for kc in range(KC):
            for t in range(NT):
                last = pe.transpose(PS[:, b0 + kc, t * P:(t + 1) * P],
                                    src[:, t, kc * P:(kc + 1) * P], C("ident"))
            last.then_inc(sem("tr_ps"), 1)

    def tr_dve(dve, k, dst, b0=0, affine=None):
        dve.wait_ge(sem("tr_ps"), 2 * k - 1)
        if affine:
            dve.tensor_scalar(dst[:, 0], bank(b0), cols[:, 0:1], cols[:, 2:3], ALU.mult,
                              ALU.add).then_inc(sem("tr_sb"), 1)
        else:
            dve.tensor_copy(dst[:, 0], bank(b0)).then_inc(sem("tr_sb"), 1)

    def tr_act(act, k, dst, b0=0, affine=None):
        act.wait_ge(sem("tr_ps"), 2 * k)
        if affine:
            act.activation(dst[:, 1], bank(b0 + 1), ACT.Identity, scale=cols[:, 1:2],
                           bias=cols[:, 3:4]).then_inc(sem("tr_sb"), 1)
        else:
            act.copy(dst[:, 1], bank(b0 + 1)).then_inc(sem("tr_sb"), 1)

    def split_act(act, k, b0=0):
        act.wait_ge(sem("tr_ps"), 2 * k)
        for kc in range(KC):
            act.copy(xnT_h[:, kc], bank(b0 + kc)).then_inc(sem("tr_h"), 1)

    def split_dve(dve, n, b0=0):
        for kc in range(KC):
            dve.wait_ge(sem("tr_h"), 2 * n + kc - 1)
            dve.tensor_tensor(xnT_l[:, kc], bank(b0 + kc), wide(xnT_h[:, kc]), ALU.subtract)\
               .then_inc(sem("tr_l"), 1)

    def mm3(pe, out, a, b, start=True, stop=True):
        pe.matmul(out, a[0], b[0], start=start, stop=False)
        pe.matmul(out, a[0], b[1], start=False, stop=False)
        return pe.matmul(out, a[1], b[0], start=False, stop=stop)

    def tok_mm(pe, lhsT, rhs, b0, s, n=D):
        kk = lhsT.shape[1]
        for t in range(NT):
            for k in range(kk):
                last = pe.matmul(PS[:, b0 + t // 2, (t % 2) * D:(t % 2) * D + n],
                                 lhsT[:, k, t * P:(t + 1) * P], rhs[:, k, 0:n],
                                 start=k == 0, stop=k == kk - 1)
            if t % 2:
                last.then_inc(s, 1)

    def two(ap, i):
        return ap[:, 2 * i:2 * i + 2, :].rearrange("p a b -> p (a b)")

    def vec(i):
        return bcast(vecs[:, i, :], 1, (2, D))

    def pair(ap, i):
        return ap[:, 2 * i:2 * i + 2, :]

    def bankpair(b):
        return PS[:, b, :].rearrange("p (a b) -> p a b", a=2)

    with nc.Block() as block:

        @block.sync
        def _(sp):
            sp.dma_start(x_tok[:], A["x"].rearrange("(t p) d -> p t d", p=P)).then_inc(sem("in_x"), 16)
            sp.dma_start(consts[:], A["consts"]).then_inc(sem("in_const"), 16)

            def w_in(dst, src, s):
                sp.dma_start(dst, src.rearrange("(k p) n -> p k n", p=P)).then_inc(sem(s), 16)
            w_in(wq0, A["wq0"], "in_wq0")
            w_in(wk0, A["wk0"], "in_wkv0")
            w_in(wv0, A["wv0"], "in_wkv0")
            with sp.Fori(0, B) as b:
                sp.wait_ge(sem("a_cl"), b * 2 + 1)
                settle(sp)
                sp.dma_start(ctxT0, A["ctxT"][bass.ds(b, 1)].rearrange("a (k p) n -> p (a k) n", p=P))\
                  .then_inc(sem("a_ctx_in"), 16)
                for u in range(8):
                    sp.wait_ge(sem("a_tps"), b * 16 + 2 * u + 3)
                    settle(sp)
                    sp.dma_start(ring[:, u, :],
                                 A["bias"][bass.ds(b, 1), 2 * u:2 * u + 2].rearrange("a h q k -> (a h q) k"))\
                      .then_inc(sem(f"a_bias_in{u}"), 16)
            sp.wait_ge(sem("a_ot"), 2 * B + 1)
            w_in(wo0, A["wo0"], "in_wo0")
            w_in(w1_0, A["w1_0"], "in_w12")
            w_in(w2_0, A["w2_0"], "in_w12")
            w_in(ww, A["ww"], "in_wwr")
            w_in(wr, A["wr"], "in_wwr")
            sp.dma_start(cols[:], A["cols"]).then_inc(sem("in_vecs"), 16)
            sp.dma_start(vecs[:], A["vecs"].partition_broadcast(P)).then_inc(sem("in_vecs"), 16)
            with sp.Fori(0, NEXP // 2) as i:
                for e2 in range(2):
                    sp.wait_ge(sem("c_wl"), i * 16 + 8 * e2 + 8)
                    settle(sp)
                    sp.dma_start(stage[e2], A["wall"][bass.ds(i * 2 + e2, 1)].rearrange("a p c n -> p (a c) n"))\
                      .then_inc(sem(f"c_w{e2}"), 16)
            sp.wait_ge(sem("x_tok"), 3)
            w_in(wq1, A["wq1"], "in_wq1")
            w_in(wkT1, A["wkT1"], "in_wk1")
            w_in(wv1, A["wv1"], "in_wvo1")
            w_in(wo1, A["wo1"], "in_wvo1")
            with sp.Fori(0, B // 2) as i:
                for j in range(2):
                    b = i * 2 + j
                    sp.wait_ge(sem("d_sim"), b * 2 + 1)
                    settle(sp)
                    sp.dma_start(ctxT1[j], A["ctxT"][bass.ds(b, 1)].rearrange("a (k p) n -> p (a k) n", p=P))\
                      .then_inc(sem(f"d_ctxT{j}"), 16)
                    sp.wait_ge(sem("d_w"), b * 4 + 1)
                    settle(sp)
                    sp.dma_start(ctxG[j], A["ctxG"][bass.ds(b, 1)].rearrange("a p g n -> p (a g) n"))\
                      .then_inc(sem(f"d_ctxG{j}"), 16)
            sp.wait_ge(sem("x_tok"), 4)
            w_in(wqkv, A["wqkv"], "in_wqkv")
            w_in(wproj, A["wproj"], "in_wproj")
            sp.wait_ge(sem("x_tok"), 5)
            w_in(wrt, A["wrt"], "in_wrt")
            sp.dma_start(b2f[0:NEXP], A["b2f"]).then_inc(sem("in_wrt"), 16)
            sp.wait_ge(sem("x_tok"), 6)
            sp.dma_start(out.rearrange("(t p) d -> p t d", p=P), x_tok[:]).then_inc(sem("stored"), 16)
            sp.wait_ge(sem("stored"), 16)

        @block.gpsimd
        def _(pool):
            pool.wait_ge(sem("d_ue0"), 2 * FC)
            with pool.Fori(0, B) as b:
                pool.wait_ge(sem("d_sim"), b * 2 + 3)
                settle(pool)
                pool.tensor_copy(Ub[:, 0].rearrange("p g (h i) -> p g h i", i=GI),
                                 U[:, 0, :, bass.ds(b * S, S)].rearrange("p h (g i) -> p g h i", i=GI))\
                    .then_inc(sem("d_ub0"), 1)

            pool.wait_ge(sem("f_rows"), 1)
            for k in range(NB):
                if k >= 3:
                    pool.wait_ge(sem("f_dn"), k - 2)
                pool.indirect_dma_start(wblk[:, k % 3, :], None, A["wf"],
                                        bass.IndirectOffsetOnAxis(ap=rows[:, k:k + 1], axis=0))\
                    .then_inc(sem(f"f_w{k % 3}"), 16)

        @block.tensor
        def _(pe):
            pe.sem_inc(sem("a_tps"), 16)
            pe.sem_inc(sem("d_sim"), 3)
            pe.sem_inc(sem("d_w"), 5)
            pe.sem_inc(sem("d_t"), 2)
            pe.sem_inc(sem("c_dn"), 4)

            pe.wait_ge(sem("in_const"), 16)
            tr_pe(pe, 1, xn_tok)
            pe.wait_ge(sem("in_wq0"), 16)
            pe.wait_ge(sem("tr_sb"), 2)
            for mo in range(KC):
                for ki in range(KC):
                    last = pe.matmul(bank(2 + mo), wq0[:, ki, mo * P:(mo + 1) * P], xnT[:, ki],
                                     start=ki == 0, stop=ki == KC - 1)
                last.then_inc(sem("a_qps"), 1)


            def tile_free(b, *tile, keys=True):
                at = TILES.index(tile)
                back = 3
                while not keys and TILES[at - back][0] == "K":
                    back += 3
                old, ob = TILES[at - back], b if at >= back else b - 1
                if old[0] == "V":
                    pe.wait_ge(sem("a_vev"), ob * 4 + old[1] + 1)
                elif old[0] == "K":
                    pe.wait_ge(sem("a_kl"), (ob + 1) * 4 + old[1] + 1)
                else:
                    pe.wait_ge(sem(f"a_tev{old[2]}"), ob * 8 + old[1] + 3)

            def keys(b, free=lambda n: None):
                pe.wait_ge(sem("a_cl"), b * 2 + 3)
                for n in range(4):
                    free(n)
                    for ki in range(KC):
                        w, c = slice((n // 2) * P, (n // 2 + 1) * P), slice((n % 2) * 512, (n % 2 + 1) * 512)
                        last = mm3(pe, bank(tile_bank("K", n)), (wk_h[:, ki, w], wk_l[:, ki, w]),
                                   (ctx_h[:, ki, c], ctx_l[:, ki, c]), ki == 0, ki == KC - 1)
                    last.then_inc(sem("a_kps"), 1)

            def weighted(b, kc):
                for g in range(2):
                    pe.wait_ge(sem(f"a_tev{g}"), b * 8 + 4 * kc + 6)
                pe.wait_ge(sem("a_ot"), b * 2 + kc + 1)
                for kt in range(KT):
                    for j in range(4):
                        pe.matmul(PS[32 * j:32 * j + 32, 7, 0:P],
                                  v0[:, kt, kc * P + 32 * j:kc * P + 32 * j + 32],
                                  pT[:, j, kt, :], start=kt == 0, stop=kt == KT - 1)
                pe.wait_ge(sem("a_rl"), b * 2 + kc + 1)
                for j in range(4):
                    last = pe.matmul(PS[32 * j:32 * j + 32, 7, P:P + S], rdiag[:, j, :], C("pick64"),
                                     start=True, stop=True)
                last.then_inc(sem("a_pv"), 1)

            def batch(b, first=False, last_batch=False):
                def scores(u):
                    if u % 4 == 0:
                        pe.wait_ge(sem("a_kl"), b * 4 + (2 if u < 4 else 4))
                        pe.wait_ge(sem("a_qz"), b * 4 + (2 if u < 4 else 4))
                    pe.wait_ge(sem("a_z"), b * 8 + u + 1)
                    kc, j = u // 4, u % 4
                    q = [t[:, kc, 2 * j:2 * j + 2, :].rearrange("p a b -> p (a b)") for t in (qz_h, qz_l)]
                    for half in range(2):
                        c = slice(half * 512, (half + 1) * 512)
                        last = mm3(pe, bank(2 * (u % 2) + half), q, (kT_h[:, kc, c], kT_l[:, kc, c]))
                    last.then_inc(sem("a_s"), 1)

                def transposes(u):
                    pe.wait_ge(sem("a_exp"), b * 8 + u + 1)
                    for g in range(2):
                        tile_free(b, "T", u, g, keys=not last_batch)
                        n = tile_bank("T", u, g)
                        for c in range(4):
                            last = pe.transpose(PS[:, n, c * P:(c + 1) * P],
                                                ring[:, u, (4 * g + c) * P:(4 * g + c + 1) * P], C("ident"))
                        last.then_inc(sem("a_tps"), 1)

                scores(0)
                scores(1)
                if not first:
                    weighted(b - 1, 1)
                pe.wait_ge(sem("a_kl"), b * 4 + 4)
                for n in range(4):
                    if not (first and n < 3):
                        tile_free(b, "V", n)
                    for kt in (2 * n, 2 * n + 1):
                        for ki in range(KC):
                            c = slice(kt * P, (kt + 1) * P)
                            last = mm3(pe, PS[:, tile_bank("V", n), (kt % 2) * D:(kt % 2 + 1) * D],
                                       (ctx_h[:, ki, c], ctx_l[:, ki, c]), (wv_h[:, ki], wv_l[:, ki]),
                                       ki == 0, ki == KC - 1)
                    last.then_inc(sem("a_vps"), 1)
                for u in range(2, 8):
                    scores(u)
                    transposes(u - 2)
                    if u == 5:
                        weighted(b, 0)
                if not last_batch:
                    keys(b + 1, lambda n: tile_free(b, "K", n))
                transposes(6)
                transposes(7)

            pe.wait_ge(sem("a_wkv"), 2)
            def first_free(n):
                if n == 3:
                    pe.wait_ge(sem("a_kl"), 1)
            keys(0, first_free)
            batch(0, first=True)
            with pe.Fori(1, B - 1) as b:
                batch(b)
            batch(B - 1, last_batch=True)
            weighted(B - 1, 1)

            pe.wait_ge(sem("in_wo0"), 16)
            pe.wait_ge(sem("a_ot"), 2 * B + 1)
            tok_mm(pe, aT, wo0, 0, sem("a2_o"))
            tr_pe(pe, 2, tmp_tok, 4)
            pe.wait_ge(sem("in_w12"), 32)
            pe.wait_ge(sem("tr_sb"), 4)
            for c in range(FC):
                if c >= 4:
                    pe.wait_ge(sem("a2_g"), c - 3)
                for ki in range(KC):
                    last = pe.matmul(bank(c % 4), w1_0[:, ki, c * P:(c + 1) * P], xnT[:, ki],
                                     start=ki == 0, stop=ki == KC - 1)
                last.then_inc(sem("a2_h"), 1)
            pe.wait_ge(sem("a2_g"), 8)
            tok_mm(pe, hT, w2_0, 4, sem("a2_y"))

            tr_pe(pe, 3, xn_tok)
            pe.wait_ge(sem("in_wwr"), 32)
            pe.wait_ge(sem("tr_sb"), 6)
            tok_mm(pe, xnT, ww, 2, sem("b_v"))
            tr_pe(pe, 4, tmp_tok, 4)
            pe.wait_ge(sem("tr_sb"), 8)
            for h in range(MH):
                r = slice(64 * (h % 2), 64 * (h % 2) + 64)
                for t in range(NT):
                    wk_t = wkT[r, h // 2, 2 * t:2 * t + 2, :].rearrange("p a b -> p (a b)")
                    rk_t = rkT[r, h // 2, t * P:(t + 1) * P]
                    if t == 0 and h == 2:
                        pe.wait_ge(sem("b_vsb"), 2)
                    pe.matmul(PS[:, h, t * P:(t + 1) * P], wk_t, wk_t, start=True, stop=True)
                    last = pe.matmul(PS[:, 4 + h, t * P:(t + 1) * P], wk_t, rk_t, start=True, stop=True)
                last.then_inc(sem("b_gram"), 1)
            for k in range(1, LEVELS):
                for h in range(MH):
                    pe.wait_ge(sem("b_ct"), 4 * (k - 1) + h + 1)
                    for t in range(NT):
                        last = pe.matmul(PS[:, h, t * P:(t + 1) * P], CT[:, h, t, :], T[:, h, t, :],
                                         start=True, stop=True)
                    last.then_inc(sem("b_x"), 1)
                for h in range(MH):
                    pe.wait_ge(sem("b_xsb"), 4 * (k - 1) + h + 1)
                    for t in range(NT):
                        last = pe.matmul(PS[:, h, t * P:(t + 1) * P], X[:, h, t, :], TT[:, h, t, :],
                                         start=True, stop=True)
                    if k == LEVELS - 1:
                        last.then_inc(sem("b_tx"), 1)
                        continue
                    for t in range(NT):
                        last = pe.matmul(PS[:, 4 + h, t * P:(t + 1) * P], TT[:, h, t, :], X[:, h, t, :],
                                         start=True, stop=True)
                    last.then_inc(sem("b_tx"), 1)
            pe.wait_ge(sem("b_inv"), 4)
            for t in range(NT):
                for h in range(MH):
                    last = pe.matmul(PS[:, 4 + t // 2, (t % 2) * D + h * MD:(t % 2) * D + (h + 1) * MD],
                                     TT[:, h, t, :], vb[:, t, h * MD:(h + 1) * MD], start=True, stop=True)
                if t % 2:
                    last.then_inc(sem("b_vn"), 1)
            pe.wait_ge(sem("b_vnsb"), 2)
            for t in range(NT):
                for h in range(MH):
                    last = pe.matmul(PS[:, 6 + t // 2, (t % 2) * D + h * MD:(t % 2) * D + (h + 1) * MD],
                                     IT[:, h, t, :], vnew[:, t, h * MD:(h + 1) * MD], start=True, stop=True)
                if t % 2:
                    last.then_inc(sem("b_o"), 1)
            tr_pe(pe, 5, tmp_tok, 0)
            pe.wait_ge(sem("tr_sb"), 10)
            tok_mm(pe, aT, wr, 2, sem("b_out"))

            tr_pe(pe, 6, xn_tok)
            pe.wait_ge(sem("tr_l"), 2)
            pe.wait_ge(sem("c_zero"), 1)
            for t in range(NT):
                pe.matmul(PS[:, 4 + t, 0:D], zero8, y_tok[:, 0, :], start=True, stop=False)
            with pe.Fori(0, NEXP // 2) as i:
                def down(s):
                    pe.wait_ge(sem("c_hl"), i * 16 + s + 1)
                    for t in range(NT):
                        tk = slice(t * P, (t + 1) * P)
                        last = mm3(pe, PS[:, 4 + t, 0:D], (h_h[:, s % 4, tk], h_l[:, s % 4, tk]),
                                   (w_h[:, s % 4, 4 * P:], w_l[:, s % 4, 4 * P:]), False, False)
                    last.then_inc(sem("c_dn"), 1)

                for s in range(16):
                    pe.wait_ge(sem("c_wl"), i * 16 + s + 17)
                    pe.wait_ge(sem("c_hd"), i * 16 + s + 1)
                    for at, b0, name in ((0, 0, "c_g"), (2, 2, "c_u")):
                        for ki in range(KC):
                            w = slice((at + ki) * P, (at + ki + 1) * P)
                            last = mm3(pe, bank(b0 + s % 2), (w_h[:, s % 4, w], w_l[:, s % 4, w]),
                                       (xnT_h[:, ki], xnT_l[:, ki]), ki == 0, ki == KC - 1)
                        last.then_inc(sem(name), 1)
                    if s >= 2:
                        down(s - 2)
                down(14)
                down(15)
            for t in range(NT):
                last = pe.matmul(PS[:, 4 + t, 0:D], zero8, y_tok[:, 0, :], start=False, stop=True)
            last.then_inc(sem("c_done"), 1)

            tr_pe(pe, 7, xn_tok)
            pe.wait_ge(sem("tr_sb"), 12)
            pe.wait_ge(sem("in_wq1"), 16)
            pe.wait_ge(sem("in_wk1"), 16)
            pe.wait_ge(sem("d_qz0"), 1)

            def q_mm(c):
                if c >= 2:
                    pe.wait_ge(sem("d_qa"), c - 1)
                    pe.wait_ge(sem("d_qd"), c - 1)
                for ki in range(KC):
                    last = pe.matmul(bank(c % 2), wq1[:, ki, c * P:(c + 1) * P], xnT[:, ki],
                                     start=ki == 0, stop=ki == KC - 1)
                last.then_inc(sem("d_q"), 1)

            q_mm(0)
            for c in range(FC):
                if c + 1 < FC:
                    q_mm(c + 1)
                pe.wait_ge(sem("d_qa"), c + 1)
                pe.wait_ge(sem("d_qd"), c + 1)
                for h2 in range(2):
                    for dc in range(KC):
                        if c:
                            pe.wait_ge(sem(f"d_ue{dc}"), 2 * (c - 1) + h2 + 1)
                        pe.matmul(bank(2 + 2 * h2 + dc), wkT1[:, c, dc * P:(dc + 1) * P],
                                  qz1[:, c % 2, h2, :], start=True, stop=True).then_inc(sem(f"d_u{dc}"), 1)

            def sims(i, j):
                b = i * 2 + j
                pe.wait_ge(sem(f"d_ctxT{j}"), i * 16 + 16)
                pe.wait_ge(sem("d_ub0"), b + 1)
                pe.wait_ge(sem("d_ub1"), b + 1)
                for hf in range(2):
                    pe.wait_ge(sem("d_z"), b * 2 + hf + 1)
                    for g in range(4 * hf, 4 * hf + 4):
                        for dc in range(KC):
                            last = pe.matmul(PS[:, hf, (g % 4) * P:(g % 4 + 1) * P],
                                             Ub[:, dc, g, :],
                                             ctxT1[j][:, dc, :].rearrange("p (m i) -> p m i", i=S)[:, :, g * GI:(g + 1) * GI],
                                             start=dc == 0, stop=dc == KC - 1)
                    last.then_inc(sem("d_sim"), 1)

            def sums(i, j):
                b = i * 2 + j
                for hf in range(2):
                    pe.wait_ge(sem("d_p"), b * 2 + hf + 1)
                    for g in range(4):
                        last = pe.transpose(PS[:, 2 + hf, g * P:(g + 1) * P], Z[:, hf, g, :], C("ident"))
                    last.then_inc(sem("d_t"), 1)
                pe.wait_ge(sem(f"d_ctxG{j}"), i * 16 + 16)
                for hf in range(2):
                    pe.wait_ge(sem("d_te"), b * 2 + hf + 1)
                    for dc in range(KC):
                        pe.wait_ge(sem(f"d_we{dc}"), b * 2 + hf + 1)
                        for g in range(4):
                            last = pe.matmul(PS[:, 4 + 2 * hf + dc, g * P:(g + 1) * P],
                                             ctxG[j][:, 4 * hf + g, dc * P:(dc + 1) * P], PTx[:, hf, g, :],
                                             start=True, stop=True)
                        last.then_inc(sem("d_w"), 1)

            sims(0, 0)
            with pe.Fori(0, B // 2 - 1) as i:
                sims(i, 1)
                sums(i, 0)
                sims(i + 1, 0)
                sums(i, 1)
            sims(B // 2 - 1, 1)
            sums(B // 2 - 1, 0)
            sums(B // 2 - 1, 1)
            pe.wait_ge(sem("in_wvo1"), 32)
            pe.wait_ge(sem("d_we0"), 2 * B + 2)
            pe.wait_ge(sem("d_we1"), 2 * B + 2)
            for c in range(FC):
                if c >= 2:
                    pe.wait_ge(sem("d_oe"), c - 1)
                for ki in range(KC):
                    for h2 in range(2):
                        last = pe.matmul(PS[64 * h2:64 * h2 + 64, c % 2, :],
                                         wv1[:, ki, (2 * c + h2) * XD:(2 * c + h2 + 1) * XD],
                                         U[:, ki, 2 * c + h2, :], start=ki == 0, stop=ki == KC - 1)
                last.then_inc(sem("d_o"), 1)
            pe.wait_ge(sem("d_oe"), FC)
            tok_mm(pe, hT, wo1, 2, sem("d_out"))

            tr_pe(pe, 8, xn_tok)
            pe.wait_ge(sem("tr_sb"), 14)
            pe.wait_ge(sem("in_wqkv"), 16)
            for mo in range(4):
                for ki in range(KC):
                    last = pe.matmul(bank(2 + mo), wqkv[:, ki, mo * P:(mo + 1) * P], xnT[:, ki],
                                     start=ki == 0, stop=ki == KC - 1)
                last.then_inc(sem("e_qk"), 1)
            tok_mm(pe, xnT, wqkv[:, :, 2 * D:3 * D], 6, sem("e_v"))
            pe.wait_ge(sem("e_qsb"), 4)
            pe.wait_ge(sem("e_ksb"), 2)
            for t in range(NT):
                for kc in range(KC):
                    for b2 in range(2):
                        tk = slice((2 * t + b2) * S, (2 * t + b2 + 1) * S)
                        last = pe.matmul(PS[64 * b2:64 * b2 + 64, 2 * t + kc, :], qTe[:, kc, tk],
                                         kTz[:, kc, :, tk], start=True, stop=True)
                    last.then_inc(sem("e_s"), 1)
            for t in range(NT):
                pe.wait_ge(sem("e_p"), t + 1)
                for g in range(4):
                    n = 4 * t + g
                    if n >= 4:
                        pe.wait_ge(sem("e_te"), n - 3)
                    if n == 0:
                        pe.wait_ge(sem("e_z"), 2 * NT)
                    for hh in range(4):
                        last = pe.transpose(PS[:, n % 4, hh * P:(hh + 1) * P], Pz[:, t, 4 * g + hh, :], C("ident"))
                    last.then_inc(sem("e_t"), 1)
                pe.wait_ge(sem("e_te"), 4 * t + 4)
                for h in range(H):
                    last = pe.matmul(PS[:, 4 + t // 2, (t % 2) * D + h * DK:(t % 2) * D + (h + 1) * DK],
                                     PzT[:, t % 2, h, :], ve[:, t, h * DK:(h + 1) * DK], start=True, stop=True)
                if t % 2:
                    last.then_inc(sem("e_o"), 1)
            tr_pe(pe, 9, tmp_tok, 0)
            pe.wait_ge(sem("tr_sb"), 16)
            pe.wait_ge(sem("in_wproj"), 16)
            tok_mm(pe, aT, wproj, 2, sem("e_out"))

            tr_pe(pe, 10, xn_tok)
            pe.wait_ge(sem("tr_sb"), 18)
            pe.wait_ge(sem("in_wrt"), 32)
            for t in range(NT):
                for ki in range(KC):
                    last = pe.matmul(PS[:, 2, t * NEXP:(t + 1) * NEXP], xnT[:, ki, t * P:(t + 1) * P],
                                     wrt[:, ki, :], start=ki == 0, stop=ki == KC - 1)
            last.then_inc(sem("f_log"), 1)
            pe.wait_ge(sem("f_oh8"), 1)
            for t in range(NT + 1):
                for t2 in range(min(t + 1, NT)):
                    last = pe.matmul(PS[:, 4, t * NEXP:(t + 1) * NEXP], C("earlier" if t2 == t else "ones"),
                                     oh8[:, t2, :], start=t2 == 0, stop=t2 == min(t, NT - 1))
            last.then_inc(sem("f_count"), 1)
            for t in range(NT):
                last = pe.transpose(PS[0:NEXP, 3, t * P:(t + 1) * P], oh8[:, t, :], C("ident"))
            last.then_inc(sem("f_oht"), 1)

            def gather(k, j):
                pe.wait_ge(sem("f_pick"), k + 1)
                for kc in range(KC):
                    for t in range(NT):
                        for part in (xn_h, xn_l):
                            last = pe.matmul(PS[:, 0, kc * P:(kc + 1) * P], part[:, t, kc * P:(kc + 1) * P],
                                             pick[:, j, t, :], start=t == 0 and part is xn_h,
                                             stop=t == NT - 1 and part is xn_l)
                last.then_inc(sem("f_x"), 1)

            def scatter(k, j):
                pe.wait_ge(sem("f_yl"), k + 1)
                pe.wait_ge(sem("f_pickT"), k + 1)
                for t in range(NT):
                    for part in (yb_h, yb_l):
                        pe.matmul(PS[:, 6 + t // 2, (t % 2) * D:(t % 2 + 1) * D],
                                  pickT[:, j, t * P:(t + 1) * P], part[:], start=False, stop=False)

            def step(i, j, first=False, last_step=False):
                k = i * 3 + j
                pe.wait_ge(sem(f"f_w{j}"), i * 16 + 16)
                pe.wait_ge(sem("f_xg"), k + 1)
                for c in range(FC):
                    for ki in range(KC):
                        last = pe.matmul(PS[:, 1 + c // 4, (c % 4) * P:(c % 4 + 1) * P],
                                         wf1[j][:, ki, c * P:(c + 1) * P], xg[:, ki, :],
                                         start=ki == 0, stop=ki == KC - 1)
                    if c % 4 == 3:
                        last.then_inc(sem("f_upd" if c // 4 else "f_upa"), 1)
                if not first:
                    scatter(k - 1, (j + 2) % 3)
                if not last_step:
                    gather(k + 1, (j + 1) % 3)
                for c in range(FC):
                    pe.wait_ge(sem("f_hd" if c // 4 else "f_ha"), k * 4 + c % 4 + 1)
                    last = pe.matmul(PS[:, 5, 0:D], hb[:, c, :], wf2[j][:, c, :], start=c == 0, stop=c == FC - 1)
                last.then_inc(sem("f_dn"), 1)

            pe.wait_ge(sem("f_xnl"), 1)
            gather(0, 0)
            pe.wait_ge(sem("f_placed"), 1)
            pe.matmul(bank(4), C("ones"), placed.rearrange("p a b -> p (a b)"), start=True, stop=True)\
              .then_inc(sem("f_place"), 1)
            pe.wait_ge(sem("f_ohs"), 1)
            for t in range(NT):
                if t % 2 == 0:
                    pe.matmul(bank(6 + t // 2), zero8, two(xn_tok, 0), start=True, stop=False)
                pe.matmul(PS[:, 6 + t // 2, (t % 2) * D:(t % 2 + 1) * D], ohT8[0:NEXP, t * P:(t + 1) * P],
                          b2f[0:NEXP], start=False, stop=False)
            step(0, 0, first=True)
            step(0, 1)
            step(0, 2)
            with pe.Fori(1, NB // 3) as i:
                for j in range(3):
                    step(i, j)
            step(NB // 3, 0)
            step(NB // 3, 1, last_step=True)
            scatter(NB - 1, 1)
            for i in range(2):
                last = pe.matmul(bank(6 + i), zero8, two(xn_tok, 0), start=False, stop=True)
            last.then_inc(sem("f_done"), 1)

        @block.scalar
        def _(act):
            act.sem_inc(sem("a_tev1"), 2)
            act.sem_inc(sem("d_we1"), 2)

            ln_act(act, 1)
            tr_act(act, 1, xnT)
            for mo in range(KC):
                act.wait_ge(sem("a_qps"), mo + 1)
                act.mul(qT0[:, mo], bank(2 + mo), DK ** -0.5).then_inc(sem("a_qsb"), 1)
            for mo in range(KC):
                act.wait_ge(sem("a_qsb"), mo + 1)
                act.copy(q_h[:, mo], qT0[:, mo]).then_inc(sem("a_qh"), 1)
            act.wait_ge(sem("in_wkv0"), 32)
            act.copy(wk_h[:], wk0).then_inc(sem("a_wkvh"), 1)
            act.copy(wv_h[:], wv0).then_inc(sem("a_wkvh"), 1)

            def context(b, ki):
                act.wait_ge(sem("a_ctx_in"), b * 16 + 16)
                act.copy(ctx_h[:, ki], ctxT0[:, ki]).then_inc(sem("a_ch"), 1)

            def keys(b):
                for n in range(4):
                    act.wait_ge(sem("a_kps"), b * 4 + n + 1)
                    act.copy(kT_h[:, n // 2, (n % 2) * 512:(n % 2 + 1) * 512], bank(tile_bank("K", n)))\
                       .then_inc(sem("a_kh"), 1)

            def batch(b, last_batch=False):
                def exps(u):
                    act.wait_ge(sem("a_z"), b * 8 + u + 3)
                    act.activation(ring[:, u, :], ring[:, u, :], ACT.Exp, bias=nmax0[:, u:u + 1], scale=-1.0,
                                   accum_out=rsum0[:, u:u + 1]).then_inc(sem("a_exp"), 1)

                def evac(u):
                    act.wait_ge(sem("a_tps"), b * 16 + 2 * u + 18)
                    act.copy(pT[:, u % 4, 4:8, :].rearrange("p a b -> p (a b)"), bank(tile_bank("T", u, 1)))\
                       .then_inc(sem("a_tev1"), 1)

                exps(0)
                exps(1)
                for n in range(4):
                    act.wait_ge(sem("a_vps"), b * 4 + n + 1)
                    act.copy(v0[:, 2 * n:2 * n + 2, :].rearrange("p a b -> p (a b)"), bank(tile_bank("V", n)))\
                       .then_inc(sem("a_vev"), 1)
                for u in range(2, 8):
                    evac(u - 2)
                    exps(u)
                    if not last_batch and u in (4, 5):
                        context(b + 1, u - 4)
                if not last_batch:
                    keys(b + 1)
                evac(6)
                evac(7)

            context(0, 0)
            context(0, 1)
            keys(0)
            batch(0)
            with act.Fori(1, B - 1) as b:
                batch(b)
            batch(B - 1, last_batch=True)
            ln_act(act, 2)
            act.wait_ge(sem("in_vecs"), 32)
            tr_act(act, 2, xnT, 4, affine=True)
            for c in range(FC):
                act.wait_ge(sem("a2_h"), c + 1)
                act.activation(hT[:, c, :], bank(c % 4), ACT.Gelu, bias=cols[:, 4 + c:5 + c])\
                   .then_inc(sem("a2_g"), 1)
            ln_act(act, 3)

            ln_act(act, 4)
            tr_act(act, 3, xnT)
            for i in range(2):
                act.wait_ge(sem("b_v"), i + 1)
                act.copy(two(vb, i), bank(2 + i)).then_inc(sem("b_vsb"), 1)
            act.wait_ge(sem("b_arguments"), 1)
            act.activation(rinvB, ssq, ACT.Sqrt).then_inc(sem("b_functions"), 1)
            dec, lal = cols[:, 12:12 + MH], cols[:, 12 + MH:12 + 2 * MH]
            ed, lg, alpha = small[:, 44:48], small[:, 48:52], small[:, 52:56]
            act.activation(ed, dec, ACT.Exp, scale=-1.0).then_inc(sem("b_functions"), 1)
            act.wait_ge(sem("b_arguments"), 2)
            act.activation(lg, small[:, 56:60], ACT.Ln).then_inc(sem("b_functions"), 1)
            act.activation(alpha, lal, ACT.Exp).then_inc(sem("b_functions"), 1)
            act.wait_ge(sem("b_arguments"), 3)
            for h in range(MH):
                act.activation(decayed[:, h, :], C("dist"), ACT.Exp, scale=small[:, 60 + h:61 + h])\
                   .then_inc(sem("b_functions"), 1)
            act.wait_ge(sem("tr_ps"), 8)
            act.copy(rkT[:, 1], bank(5))
            act.copy(wkT[:, 1, :, 1:S], bank(5).rearrange("p (b s) -> p b s", b=B)[:, :, 0:S - 1])\
               .then_inc(sem("tr_sb"), 1)
            for k in range(1, LEVELS):
                for h in range(MH):
                    act.wait_ge(sem("b_x"), 4 * (k - 1) + h + 1)
                    act.copy(X[:, h].rearrange("p a b -> p (a b)"), bank(h)).then_inc(sem("b_xsb"), 1)
            for i in range(2):
                act.wait_ge(sem("b_vn"), i + 1)
                act.copy(two(vnew, i), bank(4 + i)).then_inc(sem("b_vnsb"), 1)
            tr_act(act, 5, aT)

            ln_act(act, 5)
            def weights(i, s):
                if s % 8 == 0:
                    act.wait_ge(sem(f"c_w{s // 8 % 2}"), (i + s // 16) * 16 + 16)
                act.wait_ge(sem("c_dn"), i * 16 + s + 1)
                act.copy(w_h[:, s % 4, :], stage[s // 8 % 2][:, s % 8, :]).then_inc(sem("c_wh"), 1)

            def experts(i, last_two=False):
                for s in range(16):
                    act.wait_ge(sem("c_g"), i * 16 + s + 1)
                    act.activation(sg[:, s % 2, :], bank(s % 2), ACT.Silu).then_inc(sem("c_sg"), 1)
                    if not (last_two and s >= 14):
                        weights(i, s + 2)
                    act.wait_ge(sem("c_hd"), i * 16 + s + 3)
                    act.wait_ge(sem("c_dn"), i * 16 + s + 1)
                    act.copy(h_h[:, s % 4, :], hm[:, s % 2, :]).then_inc(sem("c_hh"), 1)

            weights(0, 0)
            weights(0, 1)
            split_act(act, 6)
            with act.Fori(0, NEXP // 2 - 1) as i:
                experts(i)
            experts(NEXP // 2 - 1, last_two=True)

            ln_act(act, 6)
            tr_act(act, 7, xnT)
            for c in range(FC):
                act.wait_ge(sem("d_q"), c + 1)
                if c == 0:
                    act.wait_ge(sem("d_qz0"), 1)
                if c >= 2:
                    act.wait_ge(sem("d_u0"), 2 * (c - 1))
                    act.wait_ge(sem("d_u1"), 2 * (c - 1))
                act.mul(qz1[0:64, c % 2, 0, :], PS[0:64, c % 2, :], XD ** -0.5).then_inc(sem("d_qa"), 1)
                for h2 in range(2):
                    act.wait_ge(sem("d_u1"), 2 * c + h2 + 1)
                    act.copy(U[:, 1, 2 * c + h2, :], bank(3 + 2 * h2)).then_inc(sem("d_ue1"), 1)

            def exps(b):
                for hf in range(2):
                    act.wait_ge(sem("d_z"), b * 2 + hf + 3)
                    for g in range(4):
                        last = act.activation(Z[:, hf, g, :], Z[:, hf, g, :], ACT.Exp, bias=mx1[:, hf, g:g + 1],
                                              scale=-1.0, accum_out=rs1[:, hf, g:g + 1])
                    last.then_inc(sem("d_e"), 1)

            def transposed(b):
                for hf in range(2):
                    act.wait_ge(sem("d_t"), b * 2 + hf + 3)
                    act.copy(PTx[:, hf].rearrange("p a b -> p (a b)"), bank(2 + hf)).then_inc(sem("d_te"), 1)

            def summed(b):
                for hf in range(2):
                    act.wait_ge(sem("d_w"), b * 4 + hf * 2 + 7)
                    act.copy(U[:, 1, :, bass.ds(b * S + hf * 32, 32)].rearrange("p h (g i) -> p g h i", g=4),
                             PS[:, 5 + 2 * hf, :].rearrange("p (g h i) -> p g h i", g=4, h=XH))\
                       .then_inc(sem("d_we1"), 1)

            exps(0)
            with act.Fori(1, B) as b:
                transposed(b - 1)
                exps(b)
                summed(b - 1)
            transposed(B - 1)
            summed(B - 1)
            for c in range(FC):
                act.wait_ge(sem("d_o"), c + 1)
                act.copy(hT[:, c, :], bank(c % 2)).then_inc(sem("d_oe"), 1)

            ln_act(act, 7)
            tr_act(act, 8, xnT)
            for mo in range(KC):
                act.wait_ge(sem("e_qk"), mo + 1)
                act.mul(qTe[:, mo, :], bank(2 + mo), DK ** -0.5).then_inc(sem("e_qsb"), 1)
            for i in range(2):
                act.wait_ge(sem("e_v"), i + 1)
                act.copy(two(ve, i), bank(6 + i)).then_inc(sem("e_qsb"), 1)
            for n in range(2 * NT):
                act.wait_ge(sem("e_z"), n + 1)
                v = Ze[:, n // 2, 8 * (n % 2):8 * (n % 2) + 8, :]
                act.activation(v, v, ACT.Exp).then_inc(sem("e_e"), 1)
            for n in range(4 * NT):
                act.wait_ge(sem("e_t"), n + 1)
                act.copy(PzT[:, n // 4 % 2, 4 * (n % 4):4 * (n % 4) + 4, :].rearrange("p a b -> p (a b)"),
                         bank(n % 4)).then_inc(sem("e_te"), 1)
            tr_act(act, 9, aT)
            ln_act(act, 8)
            ln_act(act, 9)
            tr_act(act, 10, xnT)
            act.copy(xn_h[:].rearrange("p a b -> p (a b)"), xn_tok[:].rearrange("p a b -> p (a b)"))\
               .then_inc(sem("f_xnh"), 1)
            act.wait_ge(sem("f_oht"), 1)
            act.copy(ohT8[0:NEXP], PS[0:NEXP, 3, :]).then_inc(sem("f_ohs"), 1)

            def tokens(k):
                act.wait_ge(sem("f_x"), k + 1)
                act.copy(xg.rearrange("p a b -> p (a b)"), PS[:, 0, 0:KC * P]).then_inc(sem("f_xg"), 1)

            def result(k):
                act.wait_ge(sem("f_dn"), k + 1)
                act.copy(yb_h[:], PS[:, 5, 0:D]).then_inc(sem("f_yh"), 1)

            def step(i, j, first=False, last_step=False):
                k = i * 3 + j
                if not first:
                    result(k - 1)
                act.wait_ge(sem(f"f_w{j}"), i * 16 + 16)
                act.wait_ge(sem("f_upa"), k + 1)
                for c in range(4):
                    act.activation(hb[:, c, :], PS[:, 1, c * P:(c + 1) * P], ACT.Relu, bias=bf1[j][:, c:c + 1])\
                       .then_inc(sem("f_ha"), 1)
                if not last_step:
                    tokens(k + 1)

            tokens(0)
            act.wait_ge(sem("f_place"), 1)
            act.copy(placeT, bank(4)).then_inc(sem("f_placeT"), 1)
            step(0, 0, first=True)
            step(0, 1)
            step(0, 2)
            with act.Fori(1, NB // 3) as i:
                for j in range(3):
                    step(i, j)
            step(NB // 3, 0)
            step(NB // 3, 1, last_step=True)
            result(NB - 1)

        @block.vector
        def _(dve):
            ch = Chain(dve, sem("dve_own"))
            dve.sem_inc(sem("a_z"), 2)
            dve.sem_inc(sem("a_tev0"), 2)
            dve.sem_inc(sem("a_ot"), 1)
            dve.sem_inc(sem("d_z"), 2)
            dve.sem_inc(sem("d_we0"), 2)
            dve.sem_inc(sem("c_hd"), 2)
            dve.sem_inc(sem("a_cl"), 1)
            dve.sem_inc(sem("c_wl"), 16)
            dve.memset(zero8, 0.0).then_inc(sem("c_zero"), 1)

            dve.wait_ge(sem("in_x"), 16)
            ln_dve(dve, ch, 1, x_tok, xn_tok).then_inc(sem("tr_src"), 1)
            tr_dve(dve, 1, xnT)

            def context(b, ki):
                dve.wait_ge(sem("a_ch"), b * 2 + ki + 1)
                dve.tensor_tensor(ctx_l[:, ki], ctxT0[:, ki], wide(ctx_h[:, ki]), ALU.subtract)\
                   .then_inc(sem("a_cl"), 1)

            def keys(b, also=lambda n: None):
                for n in range(4):
                    c = slice((n % 2) * 512, (n % 2 + 1) * 512)
                    dve.wait_ge(sem("a_kh"), b * 4 + n + 1)
                    dve.tensor_tensor(kT_l[:, n // 2, c], bank(tile_bank("K", n)), wide(kT_h[:, n // 2, c]),
                                      ALU.subtract).then_inc(sem("a_kl"), 1)
                    also(n)

            def queries(b, n):
                part, z = ((q_h, qz_h), (q_l, qz_l))[n % 2]
                dve.tensor_tensor(z[:, n // 2], bcast(wide(part[:, n // 2, bass.ds(b * S, S)]), 1, (8, S)),
                                  bcast(C("head8"), 2, (8, S)), ALU.mult).then_inc(sem("a_qz"), 1)

            def inverse(b, kc):
                dve.wait_ge(sem("a_exp"), b * 8 + 4 * kc + 4)
                ch.step(dve.reciprocal(rinv0, rsum0[:, 4 * kc:4 * kc + 4]))
                dve.tensor_tensor(rdiag, bcast(rinv0, 2, (4, 32)), bcast(C("pair32"), 1, (4, 32)),
                                  ALU.mult).then_inc(sem("a_rl"), 1)

            def outputs(b, kc):
                dve.wait_ge(sem("a_pv"), b * 2 + kc + 1)
                ch.step(dve.tensor_scalar(osel, PS[:, 7, 0:S], C("half2")[:, 0:1], None, ALU.mult))
                ch.step(dve.scalar_tensor_tensor(osel2, PS[:, 7, S:2 * S], C("half2")[:, 1:2], osel,
                                                 ALU.mult, ALU.add))
                dve.tensor_tensor(aT[:, kc, bass.ds(b * S, S)], osel2, PS[:, 7, P:P + S], ALU.mult)\
                   .then_inc(sem("a_ot"), 1)

            def batch(b, first=False, last_batch=False):
                def scores(u):
                    dve.wait_ge(sem("a_s"), b * 8 + u + 1)
                    dve.wait_ge(sem(f"a_bias_in{u}"), b * 16 + 16)
                    if not last_batch:
                        settle(dve)
                    dve.tensor_tensor_reduce(out=ring[:, u, :], in0=bank(2 * (u % 2), 2), in1=ring[:, u, :],
                                             scale=-1.0, scalar=3e38, op0=ALU.add, op1=ALU.min,
                                             accum_out=nmax0[:, u:u + 1]).then_inc(sem("a_z"), 1)

                def evac(u):
                    dve.wait_ge(sem("a_tps"), b * 16 + 2 * u + 17)
                    dve.tensor_copy(pT[:, u % 4, 0:4, :].rearrange("p a b -> p (a b)"), bank(tile_bank("T", u, 0)))\
                       .then_inc(sem("a_tev0"), 1)

                scores(0)
                scores(1)
                if not first:
                    inverse(b - 1, 1)
                    outputs(b - 1, 1)
                for u in range(2, 8):
                    scores(u)
                    evac(u - 2)
                    if not last_batch and u in (4, 5):
                        context(b + 1, u - 4)
                    if u == 5:
                        inverse(b, 0)
                    if u == 6:
                        outputs(b, 0)
                if not last_batch:
                    keys(b + 1, lambda n: queries(b + 1, n))
                evac(6)
                evac(7)

            for mo in range(KC):
                dve.wait_ge(sem("a_qh"), mo + 1)
                ch.add(dve.tensor_tensor(q_l[:, mo], qT0[:, mo], wide(q_h[:, mo]), ALU.subtract))
            dve.wait_ge(sem("a_wkvh"), 2)
            dve.tensor_tensor(wk_l[:], wk0, wide(wk_h[:]), ALU.subtract).then_inc(sem("a_wkv"), 1)
            dve.tensor_tensor(wv_l[:], wv0, wide(wv_h[:]), ALU.subtract).then_inc(sem("a_wkv"), 1)
            context(0, 0)
            context(0, 1)
            ch.sync()
            dve.wait_ge(sem("in_const"), 16)
            keys(0, lambda n: queries(0, n))
            batch(0, first=True)
            with dve.Fori(1, B - 1) as b:
                ch.enter(b - 1, 6)
                batch(b)
                ch.leave(B - 2)
            batch(B - 1, last_batch=True)
            inverse(B - 1, 1)
            outputs(B - 1, 1)

            for i in range(2):
                dve.wait_ge(sem("a2_o"), i + 1)
                ch.add(dve.tensor_tensor(two(y_tok, i), bank(i), two(xn_tok, i), ALU.add))
            ch.sync()
            ln_dve(dve, ch, 2, y_tok, tmp_tok).then_inc(sem("tr_src"), 1)
            dve.wait_ge(sem("in_vecs"), 32)
            tr_dve(dve, 2, xnT, 4, affine=True)
            for i in range(2):
                dve.wait_ge(sem("a2_y"), i + 1)
                ch.add(dve.tensor_tensor(two(tmp_tok, i), bank(4 + i), two(y_tok, i), ALU.add))
            ch.sync()
            for i in range(2):
                ch.add(dve.tensor_tensor(pair(tmp_tok, i), pair(tmp_tok, i), vec(V_B2), ALU.add))
            ch.sync()
            ch.step(ln_dve(dve, ch, 3, tmp_tok, y_tok))
            for i in range(2):
                ch.add(dve.tensor_tensor(pair(y_tok, i), pair(y_tok, i), vec(V_G2), ALU.mult))
            ch.sync()
            for i in range(2):
                ch.add(dve.tensor_tensor(pair(y_tok, i), pair(y_tok, i), vec(V_BE2), ALU.add))
            ch.sync()
            dve.tensor_tensor(x_tok[:], x_tok[:], y_tok[:], ALU.add).then_inc(sem("x_tok"), 1)
            dve.wait_ge(sem("x_tok"), 1)

            ln_dve(dve, ch, 4, x_tok, xn_tok).then_inc(sem("tr_src"), 1)
            tr_dve(dve, 3, xnT)
            heads = lambda ap: ap[:].rearrange("p t (h d) -> p (t h) d", h=MH)
            dve.wait_ge(sem("tr_src"), 3)
            ch.step(dve.tensor_tensor(tmp_tok[:], xn_tok[:], xn_tok[:], ALU.mult))
            dve.reduce_sum(ssq, heads(tmp_tok), axis=AX.X).then_inc(sem("b_arguments"), 1)
            dve.wait_ge(sem("b_functions"), 1)
            ch.step(dve.tensor_scalar_max(rinvB, rinvB, 1e-12))
            ch.step(dve.reciprocal(rinvB, rinvB))
            dve.tensor_tensor(heads(tmp_tok), heads(xn_tok), bcast(rinvB, 2, (NT * MH, MD)), ALU.mult)\
               .then_inc(sem("tr_src"), 1)
            dve.wait_ge(sem("b_functions"), 2)
            dve.tensor_scalar_add(small[:, 56:60], small[:, 44:48], 1.0).then_inc(sem("b_arguments"), 1)
            dve.wait_ge(sem("b_functions"), 3)
            dve.tensor_scalar_mul(small[:, 60:64], small[:, 48:52], -1.0).then_inc(sem("b_arguments"), 1)
            ch.step(dve.reciprocal(small[:, 192:196], small[:, 56:60]))
            ch.step(dve.tensor_tensor(low0g, bcast(C("low0"), 1, (MH, P)), bcast(small[:, 192:196], 2, (MH, P)),
                                      ALU.mult))
            ch.step(dve.memset(wkT[:, :, :, 0:1], 0.0))
            dve.wait_ge(sem("tr_ps"), 7)
            ch.add(dve.tensor_copy(rkT[:, 0], bank(4)))
            dve.tensor_copy(wkT[:, 0, :, 1:S], bank(4).rearrange("p (b s) -> p b s", b=B)[:, :, 0:S - 1])\
               .then_inc(sem("tr_sb"), 1)
            dve.wait_ge(sem("b_functions"), 4 + MH)
            ch.step(dve.tensor_tensor(decayed, decayed, bcast(C("upper"), 1, (MH, P)), ALU.mult))
            tiles = lambda ap: bcast(ap, 1, (NT, P))
            for h in range(MH):
                dve.wait_ge(sem("b_gram"), h + 1)
                gram = PS[:, h, :].rearrange("p (t c) -> p t c", t=NT)
                cross = PS[:, 4 + h, :].rearrange("p (t c) -> p t c", t=NT)
                ch.add(dve.tensor_tensor(MT[:, h], gram, tiles(decayed[:, h, :]), ALU.mult))
                ch.add(dve.tensor_tensor(IT[:, h], cross, tiles(decayed[:, h, :]), ALU.mult))
                ch.step(dve.tensor_tensor(T[:, h], gram, tiles(low0g[:, h, :]), ALU.mult))
                ch.add(dve.tensor_tensor(T[:, h], tiles(C("ident")), T[:, h], ALU.subtract))
                ch.step(dve.tensor_tensor(TT[:, h], MT[:, h], tiles(C("up0")), ALU.mult))
                ch.step(dve.tensor_tensor(TT[:, h], tiles(C("ident")), TT[:, h], ALU.subtract))
                dve.tensor_tensor(CT[:, h], MT[:, h], tiles(C("up1")), ALU.mult).then_inc(sem("b_ct"), 1)
            for k in range(1, LEVELS):
                for h in range(MH):
                    dve.wait_ge(sem("b_tx"), 4 * (k - 1) + h + 1)
                    new_tt = PS[:, h, :].rearrange("p (t c) -> p t c", t=NT)
                    new_t = PS[:, 4 + h, :].rearrange("p (t c) -> p t c", t=NT)
                    if k == LEVELS - 1:
                        dve.tensor_tensor(TT[:, h], TT[:, h], new_tt, ALU.subtract).then_inc(sem("b_inv"), 1)
                        continue
                    ch.add(dve.tensor_tensor(TT[:, h], TT[:, h], new_tt, ALU.subtract))
                    ch.add(dve.tensor_tensor(T[:, h], T[:, h], new_t, ALU.subtract))
                    dve.tensor_tensor(CT[:, h], MT[:, h], tiles(C(f"up{k + 1}")), ALU.mult)\
                       .then_inc(sem("b_ct"), 1)
            dve.wait_ge(sem("b_functions"), 4)
            for i in range(2):
                dve.wait_ge(sem("b_o"), i + 1)
                last = dve.tensor_tensor(pair(tmp_tok, i).rearrange("p t (h d) -> p t h d", h=MH),
                                         PS[:, 6 + i, :].rearrange("p (t h d) -> p t h d", t=2, h=MH),
                                         bcast(bcast(small[:, 52:56], 1, (2, MH)), 3, (2, MH, MD)), ALU.mult)
                if i == 0:
                    ch.add(last)
            last.then_inc(sem("tr_src"), 1)
            tr_dve(dve, 5, aT)
            ch.step(dve.tensor_tensor(x_tok[:], x_tok[:], xn_tok[:], ALU.add))
            for i in range(2):
                dve.wait_ge(sem("b_out"), i + 1)
                ch.add(dve.tensor_tensor(two(x_tok, i), bank(2 + i), two(x_tok, i), ALU.add))
            ch.sync()
            dve.sem_inc(sem("x_tok"), 1)

            ln_dve(dve, ch, 5, x_tok, xn_tok).then_inc(sem("tr_src"), 1)
            def weights(i, s):
                dve.wait_ge(sem("c_wh"), i * 16 + s + 1)
                dve.tensor_tensor(w_l[:, s % 4, :], stage[s // 8 % 2][:, s % 8, :], wide(w_h[:, s % 4, :]),
                                  ALU.subtract).then_inc(sem("c_wl"), 1)

            def experts(i, last_two=False):
                for s in range(16):
                    dve.wait_ge(sem("c_sg"), i * 16 + s + 1)
                    dve.wait_ge(sem("c_u"), i * 16 + s + 1)
                    dve.tensor_tensor(hm[:, s % 2, :], bank(2 + s % 2), sg[:, s % 2, :], ALU.mult)\
                       .then_inc(sem("c_hd"), 1)
                    if not (last_two and s >= 14):
                        weights(i, s + 2)
                    dve.wait_ge(sem("c_hh"), i * 16 + s + 1)
                    dve.tensor_tensor(h_l[:, s % 4, :], hm[:, s % 2, :], wide(h_h[:, s % 4, :]), ALU.subtract)\
                       .then_inc(sem("c_hl"), 1)

            weights(0, 0)
            weights(0, 1)
            split_dve(dve, 1)
            with dve.Fori(0, NEXP // 2 - 1) as i:
                experts(i)
            experts(NEXP // 2 - 1, last_two=True)
            dve.wait_ge(sem("c_done"), 1)
            for t in range(NT):
                ch.add(dve.tensor_tensor(x_tok[:, t, :], PS[:, 4 + t, 0:D], x_tok[:, t, :], ALU.add))
            ch.sync()
            dve.sem_inc(sem("x_tok"), 1)

            ln_dve(dve, ch, 6, x_tok, xn_tok).then_inc(sem("tr_src"), 1)
            dve.memset(qz1[:], 0.0).then_inc(sem("d_qz0"), 1)
            tr_dve(dve, 7, xnT)
            dve.wait_ge(sem("d_qz0"), 1)
            for c in range(FC):
                dve.wait_ge(sem("d_q"), c + 1)
                dve.wait_ge(sem("d_qa"), c + 1)
                dve.tensor_scalar_mul(qz1[64:128, c % 2, 1, :], PS[64:128, c % 2, :], XD ** -0.5)\
                   .then_inc(sem("d_qd"), 1)
                for h2 in range(2):
                    dve.wait_ge(sem("d_u0"), 2 * c + h2 + 1)
                    dve.tensor_copy(U[:, 0, 2 * c + h2, :], bank(2 + 2 * h2)).then_inc(sem("d_ue0"), 1)

            def grouped(b):
                settle(dve)
                dve.tensor_copy(Ub[:, 1].rearrange("p g (h i) -> p g h i", i=GI),
                                U[:, 1, :, bass.ds(b * S, S)].rearrange("p h (g i) -> p g h i", i=GI))\
                   .then_inc(sem("d_ub1"), 1)

            def scores(b):
                for hf in range(2):
                    dve.wait_ge(sem("d_sim"), b * 2 + hf + 4)
                    dve.wait_ge(sem("d_t"), b * 2 + hf + 1)
                    settle(dve)
                    for g in range(4):
                        last = dve.tensor_tensor_reduce(out=Z[:, hf, g, :], in0=PS[:, hf, g * P:(g + 1) * P],
                                                        in1=C("group"), scale=-1.0, scalar=3e38, op0=ALU.add,
                                                        op1=ALU.min, accum_out=mx1[:, hf, g:g + 1])
                    last.then_inc(sem("d_z"), 1)

            def probabilities(b):
                for hf in range(2):
                    dve.wait_ge(sem("d_e"), b * 2 + hf + 1)
                    ch.step(dve.reciprocal(ri1[:, hf, :], rs1[:, hf, :]))
                    dve.tensor_tensor(Z[:, hf], Z[:, hf], bcast(ri1[:, hf, :], 2, (4, P)), ALU.mult)\
                       .then_inc(sem("d_p"), 1)

            def summed(b):
                for hf in range(2):
                    dve.wait_ge(sem("d_w"), b * 4 + hf * 2 + 6)
                    settle(dve)
                    dve.tensor_copy(U[:, 0, :, bass.ds(b * S + hf * 32, 32)].rearrange("p h (g i) -> p g h i", g=4),
                                    PS[:, 4 + 2 * hf, :].rearrange("p (g h i) -> p g h i", g=4, h=XH))\
                       .then_inc(sem("d_we0"), 1)

            dve.wait_ge(sem("d_ue1"), 2 * FC)
            grouped(0)
            scores(0)
            grouped(1)
            probabilities(0)
            with dve.Fori(1, B - 1) as b:
                ch.enter(b - 1, 2)
                scores(b)
                grouped(b + 1)
                probabilities(b)
                summed(b - 1)
                ch.leave(B - 2)
            scores(B - 1)
            probabilities(B - 1)
            summed(B - 2)
            summed(B - 1)
            ch.step(dve.tensor_tensor(pair(x_tok, 0), pair(x_tok, 0), vec(V_BOUT), ALU.add))
            ch.step(dve.tensor_tensor(pair(x_tok, 1), pair(x_tok, 1), vec(V_BOUT), ALU.add))
            for i in range(2):
                dve.wait_ge(sem("d_out"), i + 1)
                ch.add(dve.tensor_tensor(two(x_tok, i), bank(2 + i), two(x_tok, i), ALU.add))
            ch.sync()
            dve.sem_inc(sem("x_tok"), 1)

            ln_dve(dve, ch, 7, x_tok, xn_tok).then_inc(sem("tr_src"), 1)
            tr_dve(dve, 8, xnT)
            for kc in range(KC):
                dve.wait_ge(sem("e_qk"), 3 + kc)
                dve.tensor_tensor(kTz[:, kc], bcast(bank(4 + kc), 1, (8, TOK)), bcast(C("head8"), 2, (8, TOK)),
                                  ALU.mult).then_inc(sem("e_ksb"), 1)
            ch.step(dve.memset(Pz[:], 0.0))
            for n in range(2 * NT):
                t, hs = n // 2, slice(8 * (n % 2), 8 * (n % 2) + 8)
                s3 = PS[:, n, :].rearrange("p (h k) -> p h k", h=8)
                dve.wait_ge(sem("e_s"), n + 1)
                ch.step(dve.reduce_max(mxe[:, t, hs], s3, axis=AX.X))
                dve.tensor_tensor(Ze[:, t, hs, :], s3, bcast(mxe[:, t, hs], 2, (8, S)), ALU.subtract)\
                   .then_inc(sem("e_z"), 1)
            for t in range(NT):
                dve.wait_ge(sem("e_e"), 2 * t + 2)
                ch.step(dve.reduce_sum(rse[:, t, :], Ze[:, t], axis=AX.X))
                ch.step(dve.reciprocal(rie[:, t, :], rse[:, t, :]))
                for b2 in range(2):
                    r = slice(64 * b2, 64 * b2 + 64)
                    last = dve.tensor_tensor(Pz[r, t, :, 64 * b2:64 * b2 + 64], Ze[r, t],
                                             bcast(rie[r, t, :], 2, (H, S)), ALU.mult)
                    if b2 == 0:
                        ch.add(last)
                last.then_inc(sem("e_p"), 1)
            for i in range(2):
                dve.wait_ge(sem("e_o"), i + 1)
                last = dve.tensor_copy(two(tmp_tok, i), bank(4 + i))
                if i == 0:
                    ch.add(last)
            last.then_inc(sem("tr_src"), 1)
            tr_dve(dve, 9, aT)
            ch.step(ln_dve(dve, ch, 8, xn_tok, y_tok))
            for i in range(2):
                ch.step(dve.tensor_tensor(pair(y_tok, i), pair(y_tok, i), vec(V_LNG), ALU.mult))
                ch.step(dve.tensor_tensor(pair(y_tok, i), pair(y_tok, i), vec(V_LNB), ALU.add))
                ch.step(dve.tensor_tensor(pair(y_tok, i), pair(y_tok, i), vec(V_BPROJ), ALU.add))
                dve.wait_ge(sem("e_out"), i + 1)
                ch.step(dve.tensor_tensor(two(y_tok, i), bank(2 + i), two(y_tok, i), ALU.add))
                ch.step(dve.tensor_tensor(two(x_tok, i), two(x_tok, i), two(y_tok, i), ALU.add))
            dve.sem_inc(sem("x_tok"), 1)

            ln_dve(dve, ch, 9, x_tok, xn_tok).then_inc(sem("tr_src"), 1)
            tr_dve(dve, 10, xnT)
            dve.wait_ge(sem("f_log"), 1)
            router_b = bcast(vecs[:, V_RBR, 0:NEXP], 1, (NT, NEXP))
            ch.step(dve.tensor_tensor(logit, PS[:, 2, 0:NT * NEXP].rearrange("p (t e) -> p t e", t=NT), router_b,
                                      ALU.add))
            ch.step(dve.reduce_max(top, logit, axis=AX.X))
            ch.step(dve.tensor_tensor(eq8, logit, bcast(top, 2, (NT, NEXP)), ALU.is_equal))
            ch.step(dve.tensor_tensor(eq8, eq8, bcast(C("first"), 1, (NT, NEXP)), ALU.mult))
            ch.step(dve.reduce_max(top, eq8, axis=AX.X))
            dve.tensor_tensor(oh8, eq8, bcast(top, 2, (NT, NEXP)), ALU.is_equal).then_inc(sem("f_oh8"), 1)
            dve.wait_ge(sem("f_xnh"), 1)
            dve.tensor_tensor(xn_l[:], xn_tok[:], wide(xn_h[:]), ALU.subtract).then_inc(sem("f_xnl"), 1)
            dve.wait_ge(sem("f_count"), 1)
            ch.step(dve.tensor_tensor(over, bcast(PS[:, 4, NT * NEXP:(NT + 1) * NEXP], 2, (NEXP, NT)),
                                      bcast(C("full"), 1, (NEXP, NT)), ALU.is_gt))
            ch.step(dve.reduce_sum(blocks8, over, axis=AX.X))
            square = lambda ap: ap.rearrange("p (a b) -> p a b", a=NEXP)
            ch.add(dve.tensor_tensor(ends3, bcast(blocks8, 1, (NEXP, NEXP)), square(C("upto")), ALU.mult))
            ch.step(dve.tensor_tensor(starts3, bcast(blocks8, 1, (NEXP, NEXP)), square(C("before")), ALU.mult))
            ch.add(dve.reduce_sum(ends, ends3, axis=AX.X))
            ch.step(dve.reduce_sum(starts, starts3, axis=AX.X))
            ch.add(dve.tensor_tensor(ended, bcast(ends, 1, (NB, NEXP)), bcast(C("block"), 2, (NB, NEXP)), ALU.is_le))
            ch.step(dve.tensor_tensor(place3, PS[:, 4, 0:NT * NEXP].rearrange("p (t e) -> p t e", t=NT),
                                      bcast(starts, 1, (NT, NEXP)), ALU.add))
            ch.add(dve.reduce_sum(owner, ended, axis=AX.X))
            ch.step(dve.tensor_tensor(place3, place3, oh8, ALU.mult))
            ch.step(dve.tensor_scalar(owner, owner, float(NEXP - 1), float(P), ALU.min, ALU.mult))
            ch.step(dve.tensor_scalar(owner_row, owner, C("row")[:, 0:1], None, ALU.add))
            dve.tensor_copy(rows[:], owner_row).then_inc(sem("f_rows"), 1)
            ch.step(dve.reduce_sum(place, place3, axis=AX.X))
            ch.step(dve.tensor_tensor(rel_place, bcast(place, 1, (NB, NT)), bcast(C("block"), 2, (NB, NT)),
                                      ALU.subtract))

            def picks(k, j):
                dve.tensor_tensor(pick[:, j], bcast(C("column"), 1, (NT, P)),
                                  bcast(rel_place[:, bass.ds(k, 1), :].rearrange("p a t -> p (a t)"), 2, (NT, P)),
                                  ALU.is_equal).then_inc(sem("f_pick"), 1)

            def picksT(k, j):
                dve.tensor_tensor(pickT[:, j, :], placeT, C("slot")[:, bass.ds(k, 1)].to_broadcast([P, TOK]),
                                  ALU.is_equal).then_inc(sem("f_pickT"), 1)

            def result(k):
                dve.wait_ge(sem("f_yh"), k + 1)
                dve.tensor_tensor(yb_l[:], PS[:, 5, 0:D], wide(yb_h[:]), ALU.subtract).then_inc(sem("f_yl"), 1)

            def step(i, j, first=False, last_steps=False):
                k = i * 3 + j
                if not first:
                    result(k - 1)
                dve.wait_ge(sem(f"f_w{j}"), i * 16 + 16)
                dve.wait_ge(sem("f_upd"), k + 1)
                for c in range(4):
                    dve.tensor_scalar(hb[:, 4 + c, :], PS[:, 2, c * P:(c + 1) * P], bf1[j][:, 4 + c:5 + c], 0.0,
                                      ALU.add, ALU.max).then_inc(sem("f_hd"), 1)
                if not last_steps:
                    picks(k + 2, (j + 2) % 3)
                picksT(k, j)

            picks(0, 0)
            dve.tensor_tensor(placed, bcast(C("ident"), 1, (NT, P)), bcast(place, 2, (NT, P)), ALU.mult)\
               .then_inc(sem("f_placed"), 1)
            picks(1, 1)
            dve.wait_ge(sem("f_placeT"), 1)
            step(0, 0, first=True)
            step(0, 1)
            step(0, 2)
            with dve.Fori(1, NB // 3) as i:
                for j in range(3):
                    step(i, j)
            step(NB // 3, 0, last_steps=True)
            step(NB // 3, 1, last_steps=True)
            result(NB - 1)
            dve.wait_ge(sem("f_done"), 1)
            for i in range(2):
                ch.add(dve.tensor_tensor(two(x_tok, i), bank(6 + i), two(x_tok, i), ALU.add))
            ch.sync()
            dve.sem_inc(sem("x_tok"), 1)


def kernel(**inputs):
    import concourse.bacc as bacc
    from concourse.bass_utils import run_bass_kernel_spmd as run

    a = {k: np.asarray(v) for k, v in inputs.items()}
    t = lambda k: np.ascontiguousarray(a[k].T)
    ctx = a["ctx_1024"]
    cols = np.concatenate([
        a["L0_xattn_g1"].reshape(KC, P).T, a["L0_xattn_be1"].reshape(KC, P).T,
        a["L0_xattn_b1"].reshape(FC, P).T,
        np.broadcast_to(a["L0_attn_decay"], (P, MH)), np.broadcast_to(a["L0_attn_log_alpha"], (P, MH))], 1)
    vecs = np.zeros((NVEC, D), np.float32)
    for i, k in enumerate(["L0_xattn_b2", "L0_xattn_g2", "L0_xattn_be2", "L1_xattn_bout", "L1_attn_b_proj",
                           "L1_attn_ln_gamma", "L1_attn_ln_beta"]):
        vecs[i] = a[k]
    vecs[V_RBR, :NEXP] = a["L1_ffn_br"]
    arrays = {
        "x": a["x"].reshape(TOK, D), "bias": a["fside_Bx16xSxS2_0"], "consts": CONST,
        "ctxT": ctx.transpose(0, 2, 1),
        "ctxG": ctx.reshape(B, GM, GRP, GI, D).transpose(0, 1, 3, 2, 4).reshape(B, P, GRP, D),
        "wq0": t("L0_xattn_Wq"), "wk0": t("L0_xattn_Wk"), "wv0": t("L0_xattn_Wv"), "wo0": t("L0_xattn_Wo"),
        "w1_0": t("L0_xattn_W1"), "w2_0": t("L0_xattn_W2"), "ww": t("L0_attn_Ww"), "wr": t("L0_attn_Wr"),
        "wall": np.concatenate(
            [a[k].reshape(NEXP, KC, P, FC, P).transpose(0, 2, 3, 1, 4).reshape(NEXP, P, FC, KC * P)
             for k in ("L0_ffn_Wg", "L0_ffn_Wu")]
            + [a["L0_ffn_Wd"].reshape(NEXP, FC, P, D).transpose(0, 2, 1, 3)], 3),
        "wq1": a["L1_xattn_Wq"], "wkT1": a["L1_xattn_Wkv"][:, :XH * XD].T, "wv1": a["L1_xattn_Wkv"][:, XH * XD:],
        "wo1": a["L1_xattn_Wout"], "wqkv": t("L1_attn_W_qkv"), "wproj": t("L1_attn_W_proj"),
        "wrt": t("L1_ffn_Wr"), "b2f": a["L1_ffn_b2"],
        "wf": np.concatenate(
            [a["L1_ffn_W1"].reshape(NEXP, FF, KC, P).transpose(0, 3, 2, 1).reshape(NEXP * P, KC * FF),
             a["L1_ffn_W2"].reshape(NEXP, D, FC, P).transpose(0, 3, 2, 1).reshape(NEXP * P, FC * D),
             a["L1_ffn_b1"].reshape(NEXP, FC, P).transpose(0, 2, 1).reshape(NEXP * P, FC)], 1),
        "cols": cols, "vecs": vecs,
    }
    nc = bacc.Bacc("TRN2", target_bir_lowering=False, num_devices=1)
    A, sent = {}, {}
    for k, v in arrays.items():
        v = np.ascontiguousarray(v)
        sent[f"in_{k}"] = v
        A[k] = nc.dram_tensor(f"in_{k}", v.shape, mybir.dt.from_np(v.dtype), kind="ExternalInput").ap()
    out = nc.dram_tensor("out", (TOK, D), F32, kind="ExternalOutput").ap()
    perceiver(nc, A, out)
    r = run(nc, [sent], core_ids=[0])
    return r.results[0]["out"].reshape(B, S, D)
```

```python
import numpy as np

import concourse.bass as bass
from concourse import mybir
from concourse.alu_op_type import AluOpType as ALU

F32 = mybir.dt.float32
F32R = mybir.dt.float32r
ACT = mybir.ActivationFunctionType
AX = mybir.AxisListType

P = 128
B, S, D = 8, 64, 256
TOK = B * S
NT = TOK // P
KC = D // P
KEYS = 1024
KT = KEYS // P
H, DK = 16, 16
FF, FC = 1024, 8
NEXP = 8
NB = NT + NEXP - 1
ROW1 = KC * FF + FC * D + FC
MH, MD = 4, 64
LEVELS = 6
XH, XD = 16, 64
GRP, GI = 8, 8
GM = KEYS // S
EPS = 1e-5
BIG = 1e30


def const_layout():
    p = np.arange(P)[:, None]
    c = np.arange(P)[None, :]
    c8 = np.arange(8)[None, :]
    i, j = c, p
    same = (i // S) == (j // S)
    parts = {
        "ident": (p == c),
        "head8": (p // DK == c8),
        "pair32": (p // 64 == np.arange(32)[None, :] // DK),
        "pick64": (p % 64 == np.arange(64)[None, :]),
        "half2": ((p % 32) // DK == np.arange(2)[None, :]),
        "group": np.where(p % GI == c % GI, 0.0, -BIG),
        "upper": same & (i > j),
        "dist": np.where(same & (i > j), i - j, 0),
        "low0": same & (p % 2 == 1) & (c == p - 1),
        "first": np.broadcast_to(8.0 - c8, (P, 8)),
        "ones": np.ones((P, P)),
        "earlier": (p < c),
        "column": np.broadcast_to(c, (P, P)),
        "row": p,
        "full": np.broadcast_to(P * np.arange(NT), (P, NT)),
        "before": np.broadcast_to((P * (c8.T > c8)).reshape(1, -1), (P, NEXP * NEXP)),
        "upto": np.broadcast_to((P * (c8.T >= c8)).reshape(1, -1), (P, NEXP * NEXP)),
        "block": np.broadcast_to(P * np.arange(NB), (P, NB)),
        "slot": p + P * np.arange(NB),
    }
    for k in range(LEVELS):
        s = 2 ** k
        parts[f"up{k}"] = (i // (2 * s) == j // (2 * s)) & (i // s % 2 == 1) & (j // s % 2 == 0)
    at, where, cols = 0, {}, []
    for name, a in parts.items():
        a = np.asarray(a, np.float32)
        where[name] = (at, at + a.shape[1])
        at += a.shape[1]
        cols.append(a)
    return where, np.concatenate(cols, 1)


CONST_AT, CONST = const_layout()
NVEC = 8
V_B2, V_G2, V_BE2, V_BOUT, V_BPROJ, V_LNG, V_LNB, V_RBR = range(NVEC)


TILES = [("V", n) for n in range(4)] + [("T", u, g) for u in range(6) for g in range(2)]
TILES += [("K", n) for n in range(4)] + [("T", u, g) for u in (6, 7) for g in range(2)]


def tile_bank(*tile):
    return 4 + TILES.index(tile) % 3


class Chain:

    def __init__(self, eng, sem):
        self.eng, self.sem, self.base, self.n = eng, sem, 0, 0

    def add(self, ins):
        self.n += 1
        return ins.then_inc(self.sem, 1)

    def sync(self):
        self.eng.wait_ge(self.sem, self.base + self.n)

    def step(self, ins):
        self.add(ins)
        self.sync()

    def enter(self, i, per):
        self.before, self.per = self.base + self.n, per
        self.base, self.n = i * per + self.before, 0

    def leave(self, times):
        assert self.n == self.per, self.n
        self.base, self.n = self.before + times * self.per, 0


def perceiver(nc, A, out):
    sems = {}

    def sem(name):
        if name not in sems:
            sems[name] = nc.alloc_semaphore(name)
        return sems[name]

    def sb(name, *shape):
        return nc.alloc_sbuf_tensor(name, [P, *shape], F32)

    consts = sb("consts", CONST.shape[1])
    x_tok = sb("x_tok", NT, D)
    xn_tok = sb("xn_tok", NT, D)
    y_tok = sb("y_tok", NT, D)
    tmp_tok = sb("tmp_tok", NT, D)
    xnT = sb("xnT", KC, TOK)
    aT = sb("aT", KC, TOK)
    vecs = sb("vecs", NVEC, D)
    cols = sb("cols", 12 + 2 * MH)
    small = sb("small", 256)
    hT = sb("hT", FC, TOK)
    xnT_h = nc.alloc_sbuf_tensor("xnT_h", [P, KC, TOK], F32R)
    xnT_l = nc.alloc_sbuf_tensor("xnT_l", [P, KC, TOK], F32R)
    arena_base = nc.sbuf_base
    arena = sb("arena", 36000)
    PS = nc.alloc_psum_tensor("PS", [P, 8, 512], F32)

    def C(name):
        a, b = CONST_AT[name]
        return consts[:, a:b]

    class Carve:
        def __init__(self, at=0):
            self.at = at

        def __call__(self, *shape):
            n = int(np.prod(shape))
            v = arena[:, self.at:self.at + n]
            self.at += n
            assert self.at <= 36000, self.at
            if len(shape) == 1:
                return v
            names = "abcd"[:len(shape)]
            return v.rearrange(f"p ({' '.join(names)}) -> p {' '.join(names)}",
                               **{k: s for k, s in zip(names[1:], shape[1:])})

    def carve_r(carve, name, *shape):
        carve.at += -(arena_base // 4 + carve.at) % 8
        t = nc.alloc_sbuf_tensor_at(name, [P, *shape], F32R, offset=arena_base + 4 * carve.at)
        carve.at += int(np.prod(shape))
        assert carve.at <= 36000, carve.at
        return t

    def wide(ap):
        return ap.bitcast(F32)

    def bank(n, k=1):
        return PS[:, n:n + k, :].rearrange("p a b -> p (a b)")

    def bcast(ap, axis, shape):
        return ap.unsqueeze(axis).to_broadcast([ap.shape[0], *shape])

    def settle(eng):
        eng.sem_inc(sem("waited"), 1)

    stats = small[:, 0:24].rearrange("p (t s) -> p t s", t=NT)
    mv = small[:, 24:32].rearrange("p (t s) -> p t s", t=NT)
    eps, std, rstd = small[:, 32:33], small[:, 36:40], small[:, 40:44]

    zero8 = small[:, 64:64 + P]

    ca = Carve()
    w1_0, w2_0 = ca(KC, FF), ca(FC, D)
    ww, wr = ca(KC, D), ca(KC, D)
    after_w = ca.at
    ca = Carve()
    pT = ca(4, KT, P)
    rsum0, nmax0, rinv0 = ca(8), ca(8), ca(4)
    ca.at = after_w
    ring = ca(8, KEYS)
    ctxT0 = hT[:].rearrange("p a b -> p (a b)")[:, 0:KC * KEYS].rearrange("p (k n) -> p k n", k=KC)
    v0 = hT[:].rearrange("p a b -> p (a b)")[:, KC * KEYS:].rearrange("p (k n) -> p k n", k=KT)
    ctx_h, ctx_l = carve_r(ca, "ctx_h", KC, KEYS), carve_r(ca, "ctx_l", KC, KEYS)
    kT_h, kT_l = carve_r(ca, "kT_h", KC, KEYS), carve_r(ca, "kT_l", KC, KEYS)
    qz_h, qz_l = carve_r(ca, "qz_h", KC, 8, S), carve_r(ca, "qz_l", KC, 8, S)
    q_h, q_l = carve_r(ca, "q_h", KC, TOK), carve_r(ca, "q_l", KC, TOK)
    wk_h, wk_l = carve_r(ca, "wk_h", KC, D), carve_r(ca, "wk_l", KC, D)
    wv_h, wv_l = carve_r(ca, "wv_h", KC, D), carve_r(ca, "wv_l", KC, D)
    qT0 = ca(KC, TOK)
    wq0, wk0, wv0 = ca(KC, D), ca(KC, D), ca(KC, D)
    wo0 = wk0
    rdiag = ca(4, 32)
    osel, osel2 = ca(S), ca(S)
    cb = Carve(after_w)
    decayed = cb(MH, P)
    low0g = cb(MH, P)
    MT, IT, T, TT, CT, X = (cb(MH, NT, P) for _ in range(6))
    vb, vnew = cb(NT, D), cb(NT, D)
    rkT, wkT = cb(KC, TOK), cb(KC, B, S)
    ssq, rinvB = cb(NT * MH), cb(NT * MH)
    cc = Carve(cb.at)
    CW = 6 * P
    stage = [cc(FC, CW) for _ in range(2)]
    cc = Carve(0)
    w_h, w_l = carve_r(cc, "w_h", 4, CW), carve_r(cc, "w_l", 4, CW)
    h_h, h_l = carve_r(cc, "h_h", 4, TOK), carve_r(cc, "h_l", 4, TOK)
    sg, hm = cc(2, TOK), cc(2, TOK)
    assert cc.at <= cb.at
    cd = Carve()
    U = cd(KC, XH, TOK)
    wv1, wo1 = cd(KC, FF), cd(FC, D)
    after_wo1 = cd.at
    wq1, wkT1 = cd(KC, FF), cd(FC, D)
    hT_flat = hT[:].rearrange("p a b -> p (a b)")
    ctxT1 = [cd(KC, KEYS), hT_flat[:, 0:KC * KEYS].rearrange("p (k n) -> p k n", k=KC)]
    ctxG = [cd(GRP, D), hT_flat[:, KC * KEYS:].rearrange("p (g n) -> p g n", g=GRP)]
    Ub = cd(KC, GRP, P)
    after_ub = cd.at
    Ub0 = [Ub[:, 0], tmp_tok[:].rearrange("p a b -> p (a b)").rearrange("p (g n) -> p g n", g=GRP)]
    Z, PTx = cd(2, 4, P), cd(2, 4, P)
    qz1 = cd(2, 2, TOK)
    mx1, rs1, ri1 = cd(2, 4), cd(2, 4), cd(2, 4)
    ce = Carve()
    wqkv, wproj = ce(KC, 3 * D), ce(KC, D)
    qTe = ce(KC, TOK)
    kTz = ce(KC, 8, TOK)
    Ze = ce(NT, H, S)
    PzT = ce(2, H, P)
    mxe, rie = ce(NT, H), ce(NT, H)
    assert ce.at <= after_wo1
    ce = Carve(after_wo1)
    Pz = ce(NT, H, P)
    ve = ce(NT, H, DK + 1)
    assert ce.at <= after_ub
    cf = Carve()
    wblk = cf(3, ROW1)
    wf1 = [wblk[:, j, 0:KC * FF].rearrange("p (k n) -> p k n", k=KC) for j in range(3)]
    wf2 = [wblk[:, j, KC * FF:KC * FF + FC * D].rearrange("p (k n) -> p k n", k=FC) for j in range(3)]
    bf1 = [wblk[:, j, KC * FF + FC * D:] for j in range(3)]
    wrt, b2f = cf(KC, NEXP), cf(D)
    logit, eq8, oh8 = cf(NT, NEXP), cf(NT, NEXP), cf(NT, NEXP)
    top = cf(NT)
    ohT8 = cf(TOK)
    over, blocks8 = cf(NEXP, NT), cf(NEXP)
    ends3, ends, starts3, starts = cf(NEXP, NEXP), cf(NEXP), cf(NEXP, NEXP), cf(NEXP)
    ended, owner, owner_row = cf(NB, NEXP), cf(NB), cf(NB)
    place3, place = cf(NT, NEXP), cf(NT)
    rel_place = cf(NB, NT)
    placed = cf(NT, P)
    placeT = cf(TOK)
    xg = cf(KC, P)
    hb = cf(FC, P)
    xn_h, xn_l = carve_r(cf, "xn_h", NT, D), carve_r(cf, "xn_l", NT, D)
    pick = carve_r(cf, "pick", 3, NT, P)
    pickT = carve_r(cf, "pickT", 3, TOK)
    yb_h, yb_l = carve_r(cf, "yb_h", D), carve_r(cf, "yb_l", D)
    rows = nc.alloc_sbuf_tensor_at("rows", [P, NB], mybir.dt.int32, offset=arena_base + 4 * cf.at)
    cf(NB)

    def ln_stats(dve, ch, src, tiles):
        for t in tiles:
            ch.add(dve.bn_stats(stats[:, t, :], src[:, t, :]))

    def ln_dve(dve, ch, k, src, dst, signal=None):
        ch.sync()
        for t in range(NT):
            dve.bn_aggr(mv[:, t, :], stats[:, t, :]).then_inc(sem("ln_var"), 1)
        dve.wait_ge(sem("ln_std"), k)
        ch.step(dve.reciprocal(rstd, std))
        for t in range(NT):
            last = dve.tensor_scalar(dst[:, t, :], src[:, t, :], mv[:, t, 0:1], rstd[:, t:t + 1],
                                     ALU.subtract, ALU.mult)
            if signal:
                last.then_inc(signal, 1)
            elif t < NT - 1:
                ch.add(last)
        return last

    def ln_act(act, k):
        act.wait_ge(sem("ln_var"), NT * k + 1)
        act.activation(std, mv[:, :, 1], ACT.Sqrt, bias=eps).then_inc(sem("ln_std"), 1)

    def tr_pe(pe, k, src, b0=0):
        for t in range(NT):
            pe.wait_ge(sem("tr_src"), NT * (k - 1) + t + 1)
            for kc in range(KC):
                last = pe.transpose(PS[:, b0 + kc, t * P:(t + 1) * P],
                                    src[:, t, kc * P:(kc + 1) * P], C("ident"))
                if t == NT - 1:
                    last.then_inc(sem("tr_ps"), 1)

    def tr_dve(dve, k, dst, b0=0, affine=None):
        dve.wait_ge(sem("tr_ps"), 2 * k - 1)
        if affine:
            dve.tensor_scalar(dst[:, 0], bank(b0), cols[:, 0:1], cols[:, 2:3], ALU.mult,
                              ALU.add).then_inc(sem("tr_sb"), 1)
        else:
            dve.tensor_copy(dst[:, 0], bank(b0)).then_inc(sem("tr_sb"), 1)

    def tr_act(act, k, dst, b0=0, affine=None):
        act.wait_ge(sem("tr_ps"), 2 * k)
        if affine:
            act.activation(dst[:, 1], bank(b0 + 1), ACT.Identity, scale=cols[:, 1:2],
                           bias=cols[:, 3:4]).then_inc(sem("tr_sb"), 1)
        else:
            act.copy(dst[:, 1], bank(b0 + 1)).then_inc(sem("tr_sb"), 1)

    def split_act(act, k, b0=0):
        act.wait_ge(sem("tr_ps"), 2 * k)
        for kc in range(KC):
            act.copy(xnT_h[:, kc], bank(b0 + kc)).then_inc(sem("tr_h"), 1)

    def split_dve(dve, n, b0=0):
        for kc in range(KC):
            dve.wait_ge(sem("tr_h"), 2 * n + kc - 1)
            dve.tensor_tensor(xnT_l[:, kc], bank(b0 + kc), wide(xnT_h[:, kc]), ALU.subtract)\
               .then_inc(sem("tr_l"), 1)

    def mm3(pe, out, a, b, start=True, stop=True):
        pe.matmul(out, a[0], b[0], start=start, stop=False)
        pe.matmul(out, a[0], b[1], start=False, stop=False)
        return pe.matmul(out, a[1], b[0], start=False, stop=stop)

    def tok_mm(pe, lhsT, rhs, b0, s, n=D):
        kk = lhsT.shape[1]
        for t in range(NT):
            for k in range(kk):
                last = pe.matmul(PS[:, b0 + t // 2, (t % 2) * D:(t % 2) * D + n],
                                 lhsT[:, k, t * P:(t + 1) * P], rhs[:, k, 0:n],
                                 start=k == 0, stop=k == kk - 1)
            if t % 2:
                last.then_inc(s, 1)

    def two(ap, i):
        return ap[:, 2 * i:2 * i + 2, :].rearrange("p a b -> p (a b)")

    def vec(i):
        return bcast(vecs[:, i, :], 1, (2, D))

    def pair(ap, i):
        return ap[:, 2 * i:2 * i + 2, :]

    def bankpair(b):
        return PS[:, b, :].rearrange("p (a b) -> p a b", a=2)

    with nc.Block() as block:

        @block.sync
        def _(sp):
            sp.dma_start(x_tok[:], A["x"].rearrange("(t p) d -> p t d", p=P)).then_inc(sem("in_x"), 16)
            sp.dma_start(consts[:], A["consts"]).then_inc(sem("in_const"), 16)

            def w_in(dst, src, s):
                sp.dma_start(dst, src.rearrange("(k p) n -> p k n", p=P)).then_inc(sem(s), 16)
            w_in(wq0, A["wq0"], "in_wq0")
            w_in(wk0, A["wk0"], "in_wkv0")
            w_in(wv0, A["wv0"], "in_wkv0")
            with sp.Fori(0, B) as b:
                sp.wait_ge(sem("a_cl"), b * 2 + 1)
                settle(sp)
                sp.dma_start(ctxT0, A["ctxT"][bass.ds(b, 1)].rearrange("a (k p) n -> p (a k) n", p=P))\
                  .then_inc(sem("a_ctx_in"), 16)
                for u in range(8):
                    sp.wait_ge(sem("a_tps"), b * 16 + 2 * u + 3)
                    settle(sp)
                    sp.dma_start(ring[:, u, :],
                                 A["bias"][bass.ds(b, 1), 2 * u:2 * u + 2].rearrange("a h q k -> (a h q) k"))\
                      .then_inc(sem(f"a_bias_in{u}"), 16)
            sp.wait_ge(sem("a_wkv"), 1)
            w_in(wo0, A["wo0"], "in_wo0")
            sp.wait_ge(sem("a_ot"), 2 * B + 1)
            w_in(w1_0, A["w1_0"], "in_w12")
            w_in(w2_0, A["w2_0"], "in_w12")
            w_in(ww, A["ww"], "in_wwr")
            w_in(wr, A["wr"], "in_wwr")
            sp.wait_ge(sem("a2_o"), 2)
            with sp.Fori(0, NEXP // 2) as i:
                for e2 in range(2):
                    sp.wait_ge(sem("c_wl"), i * 16 + 8 * e2 + 8)
                    settle(sp)
                    sp.dma_start(stage[e2], A["wall"][bass.ds(i * 2 + e2, 1)].rearrange("a p c n -> p (a c) n"))\
                      .then_inc(sem(f"c_w{e2}"), 16)
            sp.wait_ge(sem("c_done"), 1)
            w_in(wq1, A["wq1"], "in_wq1")
            w_in(wkT1, A["wkT1"], "in_wk1")
            w_in(wv1, A["wv1"], "in_wvo1")
            w_in(wo1, A["wo1"], "in_wvo1")
            with sp.Fori(0, B // 2) as i:
                for j in range(2):
                    b = i * 2 + j
                    sp.wait_ge(sem("d_sim"), b * 2 + 1)
                    settle(sp)
                    sp.dma_start(ctxT1[j], A["ctxT"][bass.ds(b, 1)].rearrange("a (k p) n -> p (a k) n", p=P))\
                      .then_inc(sem(f"d_ctxT{j}"), 16)
                    sp.wait_ge(sem("d_w"), b * 4 + 1)
                    settle(sp)
                    sp.dma_start(ctxG[j], A["ctxG"][bass.ds(b, 1)].rearrange("a p g n -> p (a g) n"))\
                      .then_inc(sem(f"d_ctxG{j}"), 16)
            sp.wait_ge(sem("x_tok"), 4)
            w_in(wqkv, A["wqkv"], "in_wqkv")
            w_in(wproj, A["wproj"], "in_wproj")
            sp.wait_ge(sem("x_tok"), 5)
            w_in(wrt, A["wrt"], "in_wrt")
            sp.dma_start(b2f[0:NEXP], A["b2f"]).then_inc(sem("in_wrt"), 16)
            sp.wait_ge(sem("x_tok"), 6)
            sp.dma_start(out.rearrange("(t p) d -> p t d", p=P), x_tok[:]).then_inc(sem("stored"), 16)
            sp.wait_ge(sem("stored"), 16)

        @block.gpsimd
        def _(pool):
            pool.wait_ge(sem("a_ot"), 3)
            pool.dma_start(cols[:], A["cols"]).then_inc(sem("in_vecs"), 16)
            pool.dma_start(vecs[:], A["vecs"].partition_broadcast(P)).then_inc(sem("in_vecs"), 16)

            pool.wait_ge(sem("x_tok"), 3)
            pool.memset(qz1[:], 0.0).then_inc(sem("d_qz0"), 1)

            pool.wait_ge(sem("d_ue0"), 2 * FC)

            def grouped(i, j):
                b = i * 2 + j
                pool.wait_ge(sem("d_sim"), b * 2 + 1)
                settle(pool)
                pool.tensor_copy(Ub0[j].rearrange("p g (h i) -> p g h i", i=GI),
                                 U[:, 0, :, bass.ds(b * S, S)].rearrange("p h (g i) -> p g h i", i=GI))\
                    .then_inc(sem("d_ub0"), 1)

            pool.wait_ge(sem("d_ub0"), 1)
            grouped(0, 1)
            with pool.Fori(1, B // 2) as i:
                grouped(i, 0)
                grouped(i, 1)

            pool.wait_ge(sem("d_w"), 4 * B + 5)
            pool.memset(Pz, 0.0)
            pool.memset(ve, 1.0).then_inc(sem("e_set"), 1)
            for i in range(2):
                for n, v in enumerate((V_LNG, V_LNB, V_BPROJ)):
                    if n == 0:
                        pool.wait_ge(sem("e_y"), 1)
                    else:
                        pool.wait_ge(sem("e_yown"), 4 * i + n)
                    pool.tensor_tensor(pair(y_tok, i), pair(y_tok, i), vec(v), ALU.mult if n == 0 else ALU.add)\
                        .then_inc(sem("e_yown"), 1)
                pool.wait_ge(sem("e_yown"), 4 * i + 3)
                pool.tensor_tensor(pair(x_tok, i), pair(x_tok, i), pair(y_tok, i), ALU.add)\
                    .then_inc(sem("e_yown"), 1)

            pool.wait_ge(sem("f_rows"), 1)
            for k in range(NB):
                if k >= 3:
                    pool.wait_ge(sem("f_dn"), k - 2)
                pool.indirect_dma_start(wblk[:, k % 3, :], None, A["wf"],
                                        bass.IndirectOffsetOnAxis(ap=rows[:, k:k + 1], axis=0))\
                    .then_inc(sem(f"f_w{k % 3}"), 16)

        @block.tensor
        def _(pe):
            pe.sem_inc(sem("a_tps"), 16)
            pe.sem_inc(sem("d_sim"), 3)
            pe.sem_inc(sem("d_w"), 5)
            pe.sem_inc(sem("d_t"), 2)
            pe.sem_inc(sem("c_dn"), 4)

            pe.wait_ge(sem("in_const"), 16)
            tr_pe(pe, 1, xn_tok)
            pe.wait_ge(sem("in_wq0"), 16)
            pe.wait_ge(sem("tr_sb"), 2)
            for mo in range(KC):
                for ki in range(KC):
                    last = pe.matmul(bank(2 + mo), wq0[:, ki, mo * P:(mo + 1) * P], xnT[:, ki],
                                     start=ki == 0, stop=ki == KC - 1)
                last.then_inc(sem("a_qps"), 1)


            def tile_free(b, *tile, keys=True):
                at = TILES.index(tile)
                back = 3
                while not keys and TILES[at - back][0] == "K":
                    back += 3
                old, ob = TILES[at - back], b if at >= back else b - 1
                if old[0] == "V":
                    pe.wait_ge(sem("a_vev"), ob * 4 + old[1] + 1)
                elif old[0] == "K":
                    pe.wait_ge(sem("a_kl"), (ob + 1) * 4 + old[1] + 1)
                else:
                    pe.wait_ge(sem(f"a_tev{old[2]}"), ob * 8 + old[1] + 3)

            def keys(b, free=lambda n: None):
                pe.wait_ge(sem("a_cl"), b * 2 + 3)
                for n in range(4):
                    free(n)
                    for ki in range(KC):
                        w, c = slice((n // 2) * P, (n // 2 + 1) * P), slice((n % 2) * 512, (n % 2 + 1) * 512)
                        last = mm3(pe, bank(tile_bank("K", n)), (wk_h[:, ki, w], wk_l[:, ki, w]),
                                   (ctx_h[:, ki, c], ctx_l[:, ki, c]), ki == 0, ki == KC - 1)
                    last.then_inc(sem("a_kps"), 1)

            def weighted(b, kc):
                for g in range(2):
                    pe.wait_ge(sem(f"a_tev{g}"), b * 8 + 4 * kc + 6)
                pe.wait_ge(sem("a_ot"), b * 2 + kc + 1)
                for kt in range(KT):
                    for j in range(4):
                        pe.matmul(PS[32 * j:32 * j + 32, 7, 0:P],
                                  v0[:, kt, kc * P + 32 * j:kc * P + 32 * j + 32],
                                  pT[:, j, kt, :], start=kt == 0, stop=kt == KT - 1)
                pe.wait_ge(sem("a_rl"), b * 2 + kc + 1)
                for j in range(4):
                    last = pe.matmul(PS[32 * j:32 * j + 32, 7, P:P + S], rdiag[:, j, :], C("pick64"),
                                     start=True, stop=True)
                last.then_inc(sem("a_pv"), 1)

            def batch(b, first=False, last_batch=False):
                def scores(u):
                    if u % 4 == 0:
                        pe.wait_ge(sem("a_kl"), b * 4 + (2 if u < 4 else 4))
                        pe.wait_ge(sem("a_qz"), b * 4 + (2 if u < 4 else 4))
                    pe.wait_ge(sem("a_z"), b * 8 + u + 1)
                    kc, j = u // 4, u % 4
                    q = [t[:, kc, 2 * j:2 * j + 2, :].rearrange("p a b -> p (a b)") for t in (qz_h, qz_l)]
                    for half in range(2):
                        c = slice(half * 512, (half + 1) * 512)
                        last = mm3(pe, bank(2 * (u % 2) + half), q, (kT_h[:, kc, c], kT_l[:, kc, c]))
                    last.then_inc(sem("a_s"), 1)

                def transposes(u):
                    pe.wait_ge(sem("a_exp"), b * 8 + u + 1)
                    for g in range(2):
                        tile_free(b, "T", u, g, keys=not last_batch)
                        n = tile_bank("T", u, g)
                        for c in range(4):
                            last = pe.transpose(PS[:, n, c * P:(c + 1) * P],
                                                ring[:, u, (4 * g + c) * P:(4 * g + c + 1) * P], C("ident"))
                        last.then_inc(sem("a_tps"), 1)

                scores(0)
                scores(1)
                if not first:
                    weighted(b - 1, 1)
                pe.wait_ge(sem("a_kl"), b * 4 + 4)
                if first:
                    pe.wait_ge(sem("a_wkv"), 2)
                for n in range(4):
                    if not (first and n < 3):
                        tile_free(b, "V", n)
                    for kt in (2 * n, 2 * n + 1):
                        for ki in range(KC):
                            c = slice(kt * P, (kt + 1) * P)
                            last = mm3(pe, PS[:, tile_bank("V", n), (kt % 2) * D:(kt % 2 + 1) * D],
                                       (ctx_h[:, ki, c], ctx_l[:, ki, c]), (wv_h[:, ki], wv_l[:, ki]),
                                       ki == 0, ki == KC - 1)
                    last.then_inc(sem("a_vps"), 1)
                for u in range(2, 8):
                    scores(u)
                    if u == 6:
                        weighted(b, 0)
                    transposes(u - 2)
                if not last_batch:
                    keys(b + 1, lambda n: tile_free(b, "K", n))
                transposes(6)
                transposes(7)

            pe.wait_ge(sem("a_wkv"), 1)
            def first_free(n):
                if n == 3:
                    pe.wait_ge(sem("a_kl"), 1)
            keys(0, first_free)
            batch(0, first=True)
            with pe.Fori(1, B - 1) as b:
                batch(b)
            batch(B - 1, last_batch=True)
            weighted(B - 1, 1)

            pe.wait_ge(sem("in_wo0"), 16)
            pe.wait_ge(sem("a_ot"), 2 * B + 1)
            tok_mm(pe, aT, wo0, 0, sem("a2_o"))
            tr_pe(pe, 2, tmp_tok, 4)
            pe.wait_ge(sem("in_w12"), 32)
            pe.wait_ge(sem("tr_sb"), 4)
            for c in range(FC):
                if c >= 4:
                    pe.wait_ge(sem("a2_g"), c - 3)
                for ki in range(KC):
                    last = pe.matmul(bank(c % 4), w1_0[:, ki, c * P:(c + 1) * P], xnT[:, ki],
                                     start=ki == 0, stop=ki == KC - 1)
                last.then_inc(sem("a2_h"), 1)
            pe.wait_ge(sem("a2_g"), 8)
            tok_mm(pe, hT, w2_0, 4, sem("a2_y"))

            tr_pe(pe, 3, xn_tok)
            pe.wait_ge(sem("in_wwr"), 32)
            pe.wait_ge(sem("tr_sb"), 6)
            tok_mm(pe, xnT, ww, 2, sem("b_v"))
            tr_pe(pe, 4, tmp_tok, 4)
            pe.wait_ge(sem("tr_sb"), 8)
            for h in range(MH):
                r = slice(64 * (h % 2), 64 * (h % 2) + 64)
                for t in range(NT):
                    wk_t = wkT[r, h // 2, 2 * t:2 * t + 2, :].rearrange("p a b -> p (a b)")
                    rk_t = rkT[r, h // 2, t * P:(t + 1) * P]
                    if t == 0 and h == 2:
                        pe.wait_ge(sem("b_copied"), 2)
                    pe.matmul(PS[:, h, t * P:(t + 1) * P], wk_t, wk_t, start=True, stop=True)
                    last = pe.matmul(PS[:, 4 + h, t * P:(t + 1) * P], wk_t, rk_t, start=True, stop=True)
                last.then_inc(sem("b_gram"), 1)
            for k in range(1, LEVELS):
                for h in range(MH):
                    pe.wait_ge(sem("b_ct"), 4 * (k - 1) + h + 1)
                    for t in range(NT):
                        last = pe.matmul(PS[:, h, t * P:(t + 1) * P], CT[:, h, t, :], T[:, h, t, :],
                                         start=True, stop=True)
                    last.then_inc(sem("b_x"), 1)
                for h in range(MH):
                    pe.wait_ge(sem("b_xsb"), 4 * (k - 1) + h + 1)
                    if k == 1:
                        pe.wait_ge(sem("b_copied"), 3 + h)
                    for t in range(NT):
                        last = pe.matmul(PS[:, h, t * P:(t + 1) * P], X[:, h, t, :], TT[:, h, t, :],
                                         start=True, stop=True)
                    if k == LEVELS - 1:
                        last.then_inc(sem("b_tx"), 1)
                        continue
                    for t in range(NT):
                        last = pe.matmul(PS[:, 4 + h, t * P:(t + 1) * P], TT[:, h, t, :], X[:, h, t, :],
                                         start=True, stop=True)
                    last.then_inc(sem("b_tx"), 1)
            pe.wait_ge(sem("b_inv"), 4)
            for t in range(NT):
                for h in range(MH):
                    last = pe.matmul(PS[:, 4 + t // 2, (t % 2) * D + h * MD:(t % 2) * D + (h + 1) * MD],
                                     TT[:, h, t, :], vb[:, t, h * MD:(h + 1) * MD], start=True, stop=True)
                if t % 2:
                    last.then_inc(sem("b_vn"), 1)
            pe.wait_ge(sem("b_vnsb"), 2)
            pe.wait_ge(sem("b_inv"), 2 * MH)
            for t in range(NT):
                for h in range(MH):
                    last = pe.matmul(PS[:, 6 + t // 2, (t % 2) * D + h * MD:(t % 2) * D + (h + 1) * MD],
                                     IT[:, h, t, :], vnew[:, t, h * MD:(h + 1) * MD], start=True, stop=True)
                if t % 2:
                    last.then_inc(sem("b_o"), 1)
            tr_pe(pe, 5, tmp_tok, 0)
            pe.wait_ge(sem("tr_sb"), 10)
            tok_mm(pe, aT, wr, 2, sem("b_out"))

            tr_pe(pe, 6, xn_tok)
            pe.wait_ge(sem("tr_l"), 2)
            pe.wait_ge(sem("c_zero"), 1)
            for t in range(NT):
                pe.matmul(PS[:, 4 + t, 0:D], zero8, y_tok[:, 0, :], start=True, stop=False)

            def down(i, s):
                pe.wait_ge(sem("c_hl"), i * 16 + s + 1)
                for t in range(NT):
                    tk = slice(t * P, (t + 1) * P)
                    last = mm3(pe, PS[:, 4 + t, 0:D], (h_h[:, s % 4, tk], h_l[:, s % 4, tk]),
                               (w_h[:, s % 4, 4 * P:], w_l[:, s % 4, 4 * P:]), False, False)
                last.then_inc(sem("c_dn"), 1)

            def experts(i, first=False):
                for s in range(16):
                    pe.wait_ge(sem("c_wl"), i * 16 + s + 17)
                    pe.wait_ge(sem("c_hd"), i * 16 + s + 1)
                    for at, b0, name in ((0, 0, "c_g"), (2, 2, "c_u")):
                        for ki in range(KC):
                            w = slice((at + ki) * P, (at + ki + 1) * P)
                            last = mm3(pe, bank(b0 + s % 2), (w_h[:, s % 4, w], w_l[:, s % 4, w]),
                                       (xnT_h[:, ki], xnT_l[:, ki]), ki == 0, ki == KC - 1)
                        last.then_inc(sem(name), 1)
                    if s >= 2:
                        down(i, s - 2)
                    elif not first:
                        down(i - 1, s + 14)

            experts(0, first=True)
            with pe.Fori(1, NEXP // 2) as i:
                experts(i)
            down(NEXP // 2 - 1, 14)
            down(NEXP // 2 - 1, 15)
            for t in range(NT):
                last = pe.matmul(PS[:, 4 + t, 0:D], zero8, y_tok[:, 0, :], start=False, stop=True)
            last.then_inc(sem("c_done"), 1)

            tr_pe(pe, 7, xn_tok)
            pe.wait_ge(sem("tr_sb"), 12)
            pe.wait_ge(sem("in_wq1"), 16)

            def q_mm(c):
                if c >= 2:
                    pe.wait_ge(sem("d_qa"), c - 1)
                    pe.wait_ge(sem("d_qd"), c - 1)
                for ki in range(KC):
                    last = pe.matmul(bank(c % 2), wq1[:, ki, c * P:(c + 1) * P], xnT[:, ki],
                                     start=ki == 0, stop=ki == KC - 1)
                last.then_inc(sem("d_q"), 1)

            q_mm(0)
            pe.wait_ge(sem("in_wk1"), 16)
            pe.wait_ge(sem("d_qz0"), 1)
            for c in range(FC):
                if c + 1 < FC:
                    q_mm(c + 1)
                pe.wait_ge(sem("d_qa"), c + 1)
                pe.wait_ge(sem("d_qd"), c + 1)
                for h2 in range(2):
                    for dc in range(KC):
                        if c:
                            pe.wait_ge(sem(f"d_ue{dc}"), 2 * (c - 1) + h2 + 1)
                        pe.matmul(bank(2 + 2 * h2 + dc), wkT1[:, c, dc * P:(dc + 1) * P],
                                  qz1[:, c % 2, h2, :], start=True, stop=True).then_inc(sem(f"d_u{dc}"), 1)

            def sims(i, j):
                b = i * 2 + j
                pe.wait_ge(sem(f"d_ctxT{j}"), i * 16 + 16)
                pe.wait_ge(sem("d_ub0"), b + 1)
                pe.wait_ge(sem("d_ub1"), b + 1)
                for hf in range(2):
                    pe.wait_ge(sem("d_z"), b * 2 + hf + 1)
                    for g in range(4 * hf, 4 * hf + 4):
                        for dc in range(KC):
                            last = pe.matmul(PS[:, hf, (g % 4) * P:(g % 4 + 1) * P],
                                             (Ub0[j] if dc == 0 else Ub[:, 1])[:, g, :],
                                             ctxT1[j][:, dc, :].rearrange("p (m i) -> p m i", i=S)[:, :, g * GI:(g + 1) * GI],
                                             start=dc == 0, stop=dc == KC - 1)
                    last.then_inc(sem("d_sim"), 1)

            def sums(i, j):
                b = i * 2 + j
                for hf in range(2):
                    pe.wait_ge(sem("d_p"), b * 2 + hf + 1)
                    for g in range(4):
                        last = pe.transpose(PS[:, 2 + hf, g * P:(g + 1) * P], Z[:, hf, g, :], C("ident"))
                    last.then_inc(sem("d_t"), 1)
                pe.wait_ge(sem(f"d_ctxG{j}"), i * 16 + 16)
                for hf in range(2):
                    pe.wait_ge(sem("d_te"), b * 2 + hf + 1)
                    for dc in range(KC):
                        pe.wait_ge(sem(f"d_we{dc}"), b * 2 + hf + 1)
                        for g in range(4):
                            last = pe.matmul(PS[:, 4 + 2 * hf + dc, g * P:(g + 1) * P],
                                             ctxG[j][:, 4 * hf + g, dc * P:(dc + 1) * P], PTx[:, hf, g, :],
                                             start=True, stop=True)
                        last.then_inc(sem("d_w"), 1)

            sims(0, 0)
            with pe.Fori(0, B // 2 - 1) as i:
                sims(i, 1)
                sums(i, 0)
                sims(i + 1, 0)
                sums(i, 1)
            sims(B // 2 - 1, 1)
            sums(B // 2 - 1, 0)
            sums(B // 2 - 1, 1)
            pe.wait_ge(sem("in_wvo1"), 32)
            pe.wait_ge(sem("d_we0"), 2 * B + 2)
            pe.wait_ge(sem("d_we1"), 2 * B + 2)
            for c in range(FC):
                if c >= 2:
                    pe.wait_ge(sem("d_oe"), c - 1)
                for ki in range(KC):
                    for h2 in range(2):
                        last = pe.matmul(PS[64 * h2:64 * h2 + 64, c % 2, :],
                                         wv1[:, ki, (2 * c + h2) * XD:(2 * c + h2 + 1) * XD],
                                         U[:, ki, 2 * c + h2, :], start=ki == 0, stop=ki == KC - 1)
                last.then_inc(sem("d_o"), 1)
            pe.wait_ge(sem("d_oe"), FC)
            tok_mm(pe, hT, wo1, 2, sem("d_out"))

            tr_pe(pe, 8, xn_tok)
            pe.wait_ge(sem("tr_sb"), 14)
            pe.wait_ge(sem("in_wqkv"), 16)
            for mo in range(4):
                for ki in range(KC):
                    last = pe.matmul(bank(2 + mo), wqkv[:, ki, mo * P:(mo + 1) * P], xnT[:, ki],
                                     start=ki == 0, stop=ki == KC - 1)
                last.then_inc(sem("e_qk"), 1)
            tok_mm(pe, xnT, wqkv[:, :, 2 * D:3 * D], 6, sem("e_v"))
            pe.wait_ge(sem("e_qsb"), 4)
            pe.wait_ge(sem("e_ksb"), 2)
            for t in range(NT):
                for kc in range(KC):
                    for b2 in range(2):
                        tk = slice((2 * t + b2) * S, (2 * t + b2 + 1) * S)
                        last = pe.matmul(PS[64 * b2:64 * b2 + 64, 2 * t + kc, :], qTe[:, kc, tk],
                                         kTz[:, kc, :, tk], start=True, stop=True)
                    last.then_inc(sem("e_s"), 1)

            def turned(t):
                pe.wait_ge(sem("e_e"), 2 * t + 2)
                for g in range(4):
                    if t == 0:
                        pe.wait_ge(sem("e_z"), g + 1)
                    else:
                        pe.wait_ge(sem(f"e_te{g % 2}"), 2 * t + g // 2 - 1)
                    for hh in range(4):
                        last = pe.transpose(PS[:, g, hh * P:(hh + 1) * P], Pz[:, t, 4 * g + hh, :], C("ident"))
                    last.then_inc(sem("e_t"), 1)

            turned(0)
            for t in range(NT):
                if t + 1 < NT:
                    turned(t + 1)
                pe.wait_ge(sem("e_te0"), 2 * t + 2)
                pe.wait_ge(sem("e_te1"), 2 * t + 2)
                pe.wait_ge(sem("e_z"), 5 + t)
                for h in range(H):
                    last = pe.matmul(PS[:, 4 + t, h * (DK + 1):(h + 1) * (DK + 1)],
                                     PzT[:, t % 2, h, :], ve[:, t, h, :], start=True, stop=True)
                last.then_inc(sem("e_o"), 1)
            tr_pe(pe, 9, tmp_tok, 0)
            pe.wait_ge(sem("tr_sb"), 16)
            pe.wait_ge(sem("in_wproj"), 16)
            tok_mm(pe, aT, wproj, 2, sem("e_out"))

            tr_pe(pe, 10, xn_tok)
            pe.wait_ge(sem("tr_sb"), 18)
            pe.wait_ge(sem("in_wrt"), 32)
            for t in range(NT):
                for ki in range(KC):
                    last = pe.matmul(PS[:, 2, t * NEXP:(t + 1) * NEXP], xnT[:, ki, t * P:(t + 1) * P],
                                     wrt[:, ki, :], start=ki == 0, stop=ki == KC - 1)
            last.then_inc(sem("f_log"), 1)
            pe.wait_ge(sem("f_oh8"), 1)
            counts = lambda a, b: PS[:, 4, a * NEXP:b * NEXP]
            chose = lambda a, b: oh8[:, a:b, :].rearrange("p t e -> p (t e)")
            pe.matmul(counts(0, NT + 1), zero8, C("column")[:, 0:(NT + 1) * NEXP], start=True, stop=False)
            pe.matmul(counts(0, NT), C("earlier"), chose(0, NT), start=False, stop=False)
            for back in range(1, NT + 1):
                last = pe.matmul(counts(back, NT + 1), C("ones"), chose(0, NT + 1 - back), start=False,
                                 stop=back == NT)
            last.then_inc(sem("f_count"), 1)
            for t in range(NT):
                last = pe.transpose(PS[0:NEXP, 3, t * P:(t + 1) * P], oh8[:, t, :], C("ident"))
            last.then_inc(sem("f_oht"), 1)

            def gather(k, j):
                pe.wait_ge(sem("f_pick"), k + 1)
                for kc in range(KC):
                    for t in range(NT):
                        for part in (xn_h, xn_l):
                            last = pe.matmul(PS[:, 0, kc * P:(kc + 1) * P], part[:, t, kc * P:(kc + 1) * P],
                                             pick[:, j, t, :], start=t == 0 and part is xn_h,
                                             stop=t == NT - 1 and part is xn_l)
                last.then_inc(sem("f_x"), 1)

            def scatter(k, j):
                pe.wait_ge(sem("f_yl"), k + 1)
                pe.wait_ge(sem("f_pickT"), k + 1)
                for t in range(NT):
                    for part in (yb_h, yb_l):
                        pe.matmul(PS[:, 6 + t // 2, (t % 2) * D:(t % 2 + 1) * D],
                                  pickT[:, j, t * P:(t + 1) * P], part[:], start=False, stop=False)

            def step(i, j, first=False, last_step=False):
                k = i * 3 + j
                pe.wait_ge(sem(f"f_w{j}"), i * 16 + 16)
                pe.wait_ge(sem("f_xg"), k + 1)
                for c in range(FC):
                    for ki in range(KC):
                        last = pe.matmul(PS[:, 1 + c // 4, (c % 4) * P:(c % 4 + 1) * P],
                                         wf1[j][:, ki, c * P:(c + 1) * P], xg[:, ki, :],
                                         start=ki == 0, stop=ki == KC - 1)
                    if c % 4 == 3:
                        last.then_inc(sem("f_upd" if c // 4 else "f_upa"), 1)
                if not first:
                    scatter(k - 1, (j + 2) % 3)
                if not last_step:
                    gather(k + 1, (j + 1) % 3)
                for c in range(FC):
                    pe.wait_ge(sem("f_hd" if c // 4 else "f_ha"), k * 4 + c % 4 + 1)
                    last = pe.matmul(PS[:, 5, 0:D], hb[:, c, :], wf2[j][:, c, :], start=c == 0, stop=c == FC - 1)
                last.then_inc(sem("f_dn"), 1)

            pe.wait_ge(sem("f_ohs"), 1)
            for t in range(NT):
                if t % 2 == 0:
                    pe.matmul(bank(6 + t // 2), zero8, two(xn_tok, 0), start=True, stop=False)
                pe.matmul(PS[:, 6 + t // 2, (t % 2) * D:(t % 2 + 1) * D], ohT8[0:NEXP, t * P:(t + 1) * P],
                          b2f[0:NEXP], start=False, stop=False)
            pe.wait_ge(sem("f_xnl"), 1)
            gather(0, 0)
            pe.wait_ge(sem("f_placed"), 1)
            pe.matmul(bank(4), C("ones"), placed.rearrange("p a b -> p (a b)"), start=True, stop=True)\
              .then_inc(sem("f_place"), 1)
            step(0, 0, first=True)
            step(0, 1)
            step(0, 2)
            with pe.Fori(1, NB // 3) as i:
                for j in range(3):
                    step(i, j)
            step(NB // 3, 0)
            step(NB // 3, 1, last_step=True)
            scatter(NB - 1, 1)
            for i in range(2):
                last = pe.matmul(bank(6 + i), zero8, two(xn_tok, 0), start=False, stop=True)
            last.then_inc(sem("f_done"), 1)

        @block.scalar
        def _(act):
            act.sem_inc(sem("a_tev1"), 2)
            act.sem_inc(sem("d_we1"), 2)

            ln_act(act, 1)
            def context(b, ki):
                act.wait_ge(sem("a_ctx_in"), b * 16 + 16)
                act.copy(ctx_h[:, ki], ctxT0[:, ki]).then_inc(sem("a_ch"), 1)

            tr_act(act, 1, xnT)
            act.wait_ge(sem("in_wkv0"), 32)
            act.copy(wk_h[:], wk0).then_inc(sem("a_wkvh"), 1)
            act.copy(wv_h[:], wv0).then_inc(sem("a_wkvh"), 1)
            context(0, 0)
            context(0, 1)
            for mo in range(KC):
                act.wait_ge(sem("a_qps"), mo + 1)
                act.mul(qT0[:, mo], bank(2 + mo), DK ** -0.5).then_inc(sem("a_qsb"), 1)
            for mo in range(KC):
                act.wait_ge(sem("a_qsb"), mo + 1)
                act.copy(q_h[:, mo], qT0[:, mo]).then_inc(sem("a_qh"), 1)
            def keys(b):
                for n in range(4):
                    act.wait_ge(sem("a_kps"), b * 4 + n + 1)
                    act.copy(kT_h[:, n // 2, (n % 2) * 512:(n % 2 + 1) * 512], bank(tile_bank("K", n)))\
                       .then_inc(sem("a_kh"), 1)

            def batch(b, last_batch=False):
                def exps(u):
                    act.wait_ge(sem("a_z"), b * 8 + u + 3)
                    act.activation(ring[:, u, :], ring[:, u, :], ACT.Exp, bias=nmax0[:, u:u + 1], scale=-1.0,
                                   accum_out=rsum0[:, u:u + 1]).then_inc(sem("a_exp"), 1)

                def evac(u):
                    act.wait_ge(sem("a_tps"), b * 16 + 2 * u + 18)
                    act.copy(pT[:, u % 4, 4:8, :].rearrange("p a b -> p (a b)"), bank(tile_bank("T", u, 1)))\
                       .then_inc(sem("a_tev1"), 1)

                exps(0)
                exps(1)
                for n in range(4):
                    act.wait_ge(sem("a_vps"), b * 4 + n + 1)
                    act.copy(v0[:, 2 * n:2 * n + 2, :].rearrange("p a b -> p (a b)"), bank(tile_bank("V", n)))\
                       .then_inc(sem("a_vev"), 1)
                for u in range(2, 8):
                    evac(u - 2)
                    exps(u)
                    if not last_batch and u in (4, 5):
                        context(b + 1, u - 4)
                if not last_batch:
                    keys(b + 1)
                evac(6)
                evac(7)

            keys(0)
            batch(0)
            with act.Fori(1, B - 1) as b:
                batch(b)
            batch(B - 1, last_batch=True)
            act.wait_ge(sem("in_vecs"), 32)
            dec, lal = cols[:, 12:12 + MH], cols[:, 12 + MH:12 + 2 * MH]
            ed, lg, alpha = small[:, 44:48], small[:, 48:52], small[:, 52:56]
            act.activation(ed, dec, ACT.Exp, scale=-1.0).then_inc(sem("b_functions"), 1)
            act.wait_ge(sem("b_arguments"), 1)
            act.activation(lg, small[:, 56:60], ACT.Ln).then_inc(sem("b_functions"), 1)
            act.activation(alpha, lal, ACT.Exp).then_inc(sem("b_functions"), 1)
            act.wait_ge(sem("b_arguments"), 2)
            for h in range(MH):
                act.activation(decayed[:, h, :], C("dist"), ACT.Exp, scale=small[:, 60 + h:61 + h])\
                   .then_inc(sem("b_functions"), 1)
            ln_act(act, 2)
            tr_act(act, 2, xnT, 4, affine=True)
            for c in range(FC):
                act.wait_ge(sem("a2_h"), c + 1)
                act.activation(hT[:, c, :], bank(c % 4), ACT.Gelu, bias=cols[:, 4 + c:5 + c])\
                   .then_inc(sem("a2_g"), 1)
            ln_act(act, 3)

            ln_act(act, 4)
            tr_act(act, 3, xnT)
            act.wait_ge(sem("b_arguments"), 3)
            act.activation(rinvB, ssq, ACT.Sqrt).then_inc(sem("b_functions"), 1)
            for i in range(2):
                act.wait_ge(sem("b_v"), i + 1)
                act.copy(two(vb, i), bank(2 + i)).then_inc(sem("b_copied"), 1)
            act.wait_ge(sem("tr_ps"), 8)
            act.copy(rkT[:, 1], bank(5))
            act.copy(wkT[:, 1, :, 1:S], bank(5).rearrange("p (b s) -> p b s", b=B)[:, :, 0:S - 1])\
               .then_inc(sem("tr_sb"), 1)
            for h in range(MH):
                act.wait_ge(sem("b_gram"), h + 1)
                act.copy(IT[:, h].rearrange("p a b -> p (a b)"), bank(4 + h)).then_inc(sem("b_copied"), 1)
            for k in range(1, LEVELS):
                for h in range(MH):
                    act.wait_ge(sem("b_x"), 4 * (k - 1) + h + 1)
                    act.copy(X[:, h].rearrange("p a b -> p (a b)"), bank(h)).then_inc(sem("b_xsb"), 1)
            for i in range(2):
                act.wait_ge(sem("b_vn"), i + 1)
                act.copy(two(vnew, i), bank(4 + i)).then_inc(sem("b_vnsb"), 1)
            tr_act(act, 5, aT)

            ln_act(act, 5)
            def weights(i, s):
                if s % 8 == 0:
                    act.wait_ge(sem(f"c_w{s // 8 % 2}"), (i + s // 16) * 16 + 16)
                act.wait_ge(sem("c_dn"), i * 16 + s + 1)
                act.copy(w_h[:, s % 4, :], stage[s // 8 % 2][:, s % 8, :]).then_inc(sem("c_wh"), 1)

            def experts(i, last_two=False):
                for s in range(16):
                    act.wait_ge(sem("c_g"), i * 16 + s + 1)
                    act.activation(sg[:, s % 2, :], bank(s % 2), ACT.Silu).then_inc(sem("c_sg"), 1)
                    if not (last_two and s >= 14):
                        weights(i, s + 2)
                    act.wait_ge(sem("c_hd"), i * 16 + s + 3)
                    act.wait_ge(sem("c_dn"), i * 16 + s + 1)
                    act.copy(h_h[:, s % 4, :], hm[:, s % 2, :]).then_inc(sem("c_hh"), 1)

            weights(0, 0)
            weights(0, 1)
            split_act(act, 6)
            with act.Fori(0, NEXP // 2 - 1) as i:
                experts(i)
            experts(NEXP // 2 - 1, last_two=True)

            ln_act(act, 6)
            tr_act(act, 7, xnT)
            def queries(c):
                act.wait_ge(sem("d_q"), c + 1)
                if c == 0:
                    act.wait_ge(sem("d_qz0"), 1)
                if c >= 2:
                    act.wait_ge(sem("d_u0"), 2 * (c - 1))
                    act.wait_ge(sem("d_u1"), 2 * (c - 1))
                act.mul(qz1[0:64, c % 2, 0, :], PS[0:64, c % 2, :], XD ** -0.5).then_inc(sem("d_qa"), 1)

            queries(0)
            for c in range(FC):
                if c + 1 < FC:
                    queries(c + 1)
                for h2 in range(2):
                    act.wait_ge(sem("d_u1"), 2 * c + h2 + 1)
                    act.copy(U[:, 1, 2 * c + h2, :], bank(3 + 2 * h2)).then_inc(sem("d_ue1"), 1)
            act.wait_ge(sem("d_ue0"), 2 * FC)
            act.copy(Ub0[0].rearrange("p g (h i) -> p g h i", i=GI),
                     U[:, 0, :, 0:S].rearrange("p h (g i) -> p g h i", i=GI)).then_inc(sem("d_ub0"), 1)

            def exps(b):
                for hf in range(2):
                    act.wait_ge(sem("d_z"), b * 2 + hf + 3)
                    for g in range(4):
                        last = act.activation(Z[:, hf, g, :], Z[:, hf, g, :], ACT.Exp, bias=mx1[:, hf, g:g + 1],
                                              scale=-1.0, accum_out=rs1[:, hf, g:g + 1])
                    last.then_inc(sem("d_e"), 1)

            def transposed(b):
                for hf in range(2):
                    act.wait_ge(sem("d_t"), b * 2 + hf + 3)
                    act.copy(PTx[:, hf].rearrange("p a b -> p (a b)"), bank(2 + hf)).then_inc(sem("d_te"), 1)

            def summed(b):
                for hf in range(2):
                    act.wait_ge(sem("d_w"), b * 4 + hf * 2 + 7)
                    act.copy(U[:, 1, :, bass.ds(b * S + hf * 32, 32)].rearrange("p h (g i) -> p g h i", g=4),
                             PS[:, 5 + 2 * hf, :].rearrange("p (g h i) -> p g h i", g=4, h=XH))\
                       .then_inc(sem("d_we1"), 1)

            exps(0)
            with act.Fori(1, B) as b:
                transposed(b - 1)
                exps(b)
                summed(b - 1)
            transposed(B - 1)
            summed(B - 1)
            for c in range(FC):
                act.wait_ge(sem("d_o"), c + 1)
                act.copy(hT[:, c, :], bank(c % 2)).then_inc(sem("d_oe"), 1)

            ln_act(act, 7)
            tr_act(act, 8, xnT)
            ln_act(act, 8)
            for mo in range(KC):
                act.wait_ge(sem("e_qk"), mo + 1)
                act.mul(qTe[:, mo, :], bank(2 + mo), DK ** -0.5).then_inc(sem("e_qsb"), 1)
            act.wait_ge(sem("e_qk"), 4)
            for h in range(8):
                last = act.activation(kTz[:, 1, h, :], bank(5), ACT.Copy, scale=C("head8")[:, h:h + 1])
            last.then_inc(sem("e_ksb"), 1)
            def exps(n):
                act.wait_ge(sem("e_z"), n + 1)
                hs = slice(8 * (n % 2), 8 * (n % 2) + 8)
                for b2 in range(2):
                    r = slice(64 * b2, 64 * b2 + 64)
                    last = act.activation(Pz[r, n // 2, hs, 64 * b2:64 * b2 + 64], Ze[r, n // 2, hs, :], ACT.Exp)
                last.then_inc(sem("e_e"), 1)

            def turned(t):
                for g in (0, 2):
                    act.wait_ge(sem("e_t"), 4 * t + g + 1)
                    act.copy(PzT[:, t % 2, 4 * g:4 * g + 4, :].rearrange("p a b -> p (a b)"), bank(g))\
                       .then_inc(sem("e_te0"), 1)

            for n in range(4):
                exps(n)
            turned(0)
            for n in range(4, 6):
                exps(n)
            turned(1)
            for n in range(6, 8):
                exps(n)
            turned(2)
            turned(3)
            tr_act(act, 9, aT)
            ln_act(act, 9)
            tr_act(act, 10, xnT)
            act.copy(xn_h[:].rearrange("p a b -> p (a b)"), xn_tok[:].rearrange("p a b -> p (a b)"))\
               .then_inc(sem("f_xnh"), 1)
            act.wait_ge(sem("f_oht"), 1)
            act.copy(ohT8[0:NEXP], PS[0:NEXP, 3, :]).then_inc(sem("f_ohs"), 1)

            def tokens(k):
                act.wait_ge(sem("f_x"), k + 1)
                act.copy(xg.rearrange("p a b -> p (a b)"), PS[:, 0, 0:KC * P]).then_inc(sem("f_xg"), 1)

            def result(k):
                act.wait_ge(sem("f_dn"), k + 1)
                act.copy(yb_h[:], PS[:, 5, 0:D]).then_inc(sem("f_yh"), 1)

            def step(i, j, first=False, last_step=False):
                k = i * 3 + j
                if not first:
                    result(k - 1)
                act.wait_ge(sem(f"f_w{j}"), i * 16 + 16)
                act.wait_ge(sem("f_upa"), k + 1)
                for c in range(4):
                    act.activation(hb[:, c, :], PS[:, 1, c * P:(c + 1) * P], ACT.Relu, bias=bf1[j][:, c:c + 1])\
                       .then_inc(sem("f_ha"), 1)
                if not last_step:
                    tokens(k + 1)

            tokens(0)
            act.wait_ge(sem("f_place"), 1)
            act.copy(placeT, bank(4)).then_inc(sem("f_placeT"), 1)
            step(0, 0, first=True)
            step(0, 1)
            step(0, 2)
            with act.Fori(1, NB // 3) as i:
                for j in range(3):
                    step(i, j)
            step(NB // 3, 0)
            step(NB // 3, 1, last_step=True)
            result(NB - 1)

        @block.vector
        def _(dve):
            ch = Chain(dve, sem("dve_own"))
            dve.sem_inc(sem("a_z"), 2)
            dve.sem_inc(sem("a_tev0"), 2)
            dve.sem_inc(sem("a_ot"), 1)
            dve.sem_inc(sem("d_z"), 2)
            dve.sem_inc(sem("d_we0"), 2)
            dve.sem_inc(sem("c_hd"), 2)
            dve.sem_inc(sem("a_cl"), 1)
            dve.sem_inc(sem("c_wl"), 16)
            dve.memset(zero8, 0.0).then_inc(sem("c_zero"), 1)
            dve.memset(eps, EPS).then_inc(sem("ln_var"), 1)

            dve.wait_ge(sem("in_x"), 16)
            ln_stats(dve, ch, x_tok, range(NT))
            ln_dve(dve, ch, 1, x_tok, xn_tok, sem("tr_src"))
            tr_dve(dve, 1, xnT)

            def context(b, ki):
                dve.wait_ge(sem("a_ch"), b * 2 + ki + 1)
                dve.tensor_tensor(ctx_l[:, ki], ctxT0[:, ki], wide(ctx_h[:, ki]), ALU.subtract)\
                   .then_inc(sem("a_cl"), 1)

            def keys(b):
                for n in range(4):
                    c = slice((n % 2) * 512, (n % 2 + 1) * 512)
                    dve.wait_ge(sem("a_kh"), b * 4 + n + 1)
                    dve.tensor_tensor(kT_l[:, n // 2, c], bank(tile_bank("K", n)), wide(kT_h[:, n // 2, c]),
                                      ALU.subtract).then_inc(sem("a_kl"), 1)

            def queries(b, n):
                part, z = ((q_h, qz_h), (q_l, qz_l))[n % 2]
                dve.tensor_tensor(z[:, n // 2], bcast(wide(part[:, n // 2, bass.ds(b * S, S)]), 1, (8, S)),
                                  bcast(C("head8"), 2, (8, S)), ALU.mult).then_inc(sem("a_qz"), 1)

            def inverse(b, kc):
                dve.wait_ge(sem("a_exp"), b * 8 + 4 * kc + 4)
                ch.step(dve.reciprocal(rinv0, rsum0[:, 4 * kc:4 * kc + 4]))
                dve.tensor_tensor(rdiag, bcast(rinv0, 2, (4, 32)), bcast(C("pair32"), 1, (4, 32)),
                                  ALU.mult).then_inc(sem("a_rl"), 1)

            def outputs(b, kc):
                dve.wait_ge(sem("a_pv"), b * 2 + kc + 1)
                ch.step(dve.tensor_scalar(osel, PS[:, 7, 0:S], C("half2")[:, 0:1], None, ALU.mult))
                ch.step(dve.scalar_tensor_tensor(osel2, PS[:, 7, S:2 * S], C("half2")[:, 1:2], osel,
                                                 ALU.mult, ALU.add))
                dve.tensor_tensor(aT[:, kc, bass.ds(b * S, S)], osel2, PS[:, 7, P:P + S], ALU.mult)\
                   .then_inc(sem("a_ot"), 1)

            def batch(b, first=False, last_batch=False):
                def scores(u):
                    dve.wait_ge(sem("a_s"), b * 8 + u + 1)
                    dve.wait_ge(sem(f"a_bias_in{u}"), b * 16 + 16)
                    if not last_batch:
                        settle(dve)
                    dve.tensor_tensor_reduce(out=ring[:, u, :], in0=bank(2 * (u % 2), 2), in1=ring[:, u, :],
                                             scale=-1.0, scalar=3e38, op0=ALU.add, op1=ALU.min,
                                             accum_out=nmax0[:, u:u + 1]).then_inc(sem("a_z"), 1)

                def evac(u):
                    dve.wait_ge(sem("a_tps"), b * 16 + 2 * u + 17)
                    dve.tensor_copy(pT[:, u % 4, 0:4, :].rearrange("p a b -> p (a b)"), bank(tile_bank("T", u, 0)))\
                       .then_inc(sem("a_tev0"), 1)

                scores(0)
                scores(1)
                if not first:
                    inverse(b - 1, 1)
                    outputs(b - 1, 1)
                for u in range(2, 8):
                    scores(u)
                    if not last_batch and u == 6:
                        context(b + 1, 1)
                    evac(u - 2)
                    if u == 5:
                        inverse(b, 0)
                        if not last_batch:
                            context(b + 1, 0)
                outputs(b, 0)
                if not last_batch:
                    queries(b + 1, 0)
                    queries(b + 1, 1)
                if not last_batch:
                    keys(b + 1)
                evac(6)
                evac(7)
                if not last_batch:
                    queries(b + 1, 2)
                    queries(b + 1, 3)

            dve.wait_ge(sem("a_wkvh"), 2)
            dve.tensor_tensor(wk_l[:], wk0, wide(wk_h[:]), ALU.subtract).then_inc(sem("a_wkv"), 1)
            dve.tensor_tensor(wv_l[:], wv0, wide(wv_h[:]), ALU.subtract).then_inc(sem("a_wkv"), 1)
            context(0, 0)
            context(0, 1)
            for mo in range(KC):
                dve.wait_ge(sem("a_qh"), mo + 1)
                ch.add(dve.tensor_tensor(q_l[:, mo], qT0[:, mo], wide(q_h[:, mo]), ALU.subtract))
            ch.sync()
            dve.wait_ge(sem("in_const"), 16)
            keys(0)
            for n in range(4):
                queries(0, n)
            batch(0, first=True)
            with dve.Fori(1, B - 1) as b:
                ch.enter(b - 1, 6)
                batch(b)
                ch.leave(B - 2)
            batch(B - 1, last_batch=True)
            inverse(B - 1, 1)
            outputs(B - 1, 1)

            dve.wait_ge(sem("b_functions"), 1)
            dve.tensor_scalar_add(small[:, 56:60], small[:, 44:48], 1.0).then_inc(sem("b_arguments"), 1)
            dve.wait_ge(sem("b_functions"), 2)
            dve.tensor_scalar_mul(small[:, 60:64], small[:, 48:52], -1.0).then_inc(sem("b_arguments"), 1)
            for i in range(2):
                dve.wait_ge(sem("a2_o"), i + 1)
                ch.step(dve.tensor_tensor(two(y_tok, i), bank(i), two(xn_tok, i), ALU.add))
                ln_stats(dve, ch, y_tok, (2 * i, 2 * i + 1))
            ln_dve(dve, ch, 2, y_tok, tmp_tok, sem("tr_src"))
            dve.wait_ge(sem("in_vecs"), 32)
            tr_dve(dve, 2, xnT, 4, affine=True)
            ch.add(dve.memset(wkT[:, :, :, 0:1], 0.0))
            for i in range(2):
                ch.add(dve.tensor_tensor(pair(y_tok, i), pair(y_tok, i), vec(V_B2), ALU.add))
                ch.add(dve.tensor_tensor(pair(x_tok, i), pair(x_tok, i), vec(V_BE2), ALU.add))
            ch.step(dve.reciprocal(small[:, 192:196], small[:, 56:60]))
            ch.step(dve.tensor_tensor(low0g, bcast(C("low0"), 1, (MH, P)), bcast(small[:, 192:196], 2, (MH, P)),
                                      ALU.mult))
            dve.wait_ge(sem("b_functions"), 3 + MH)
            ch.step(dve.tensor_tensor(decayed, decayed, bcast(C("upper"), 1, (MH, P)), ALU.mult))
            for i in range(2):
                dve.wait_ge(sem("a2_y"), i + 1)
                ch.step(dve.tensor_tensor(two(tmp_tok, i), bank(4 + i), two(y_tok, i), ALU.add))
                ln_stats(dve, ch, tmp_tok, (2 * i, 2 * i + 1))
            ch.sync()
            for t in range(NT):
                dve.bn_aggr(mv[:, t, :], stats[:, t, :]).then_inc(sem("ln_var"), 1)
            dve.wait_ge(sem("ln_var"), 3 * NT + 1)
            for t in range(NT):
                ch.add(dve.scalar_tensor_tensor(y_tok[:, t, :], tmp_tok[:, t, :], mv[:, t, 0:1], vecs[:, V_G2, :],
                                                ALU.subtract, ALU.mult))
            dve.wait_ge(sem("ln_std"), 3)
            ch.step(dve.reciprocal(rstd, std))
            for t in range(NT):
                ch.add(dve.scalar_tensor_tensor(x_tok[:, t, :], y_tok[:, t, :], rstd[:, t:t + 1], x_tok[:, t, :],
                                                ALU.mult, ALU.add))
            ch.sync()
            dve.sem_inc(sem("x_tok"), 1)

            ln_stats(dve, ch, x_tok, range(NT))
            ln_dve(dve, ch, 4, x_tok, xn_tok, sem("tr_src"))
            tr_dve(dve, 3, xnT)
            heads = lambda ap: ap[:].rearrange("p t (h d) -> p (t h) d", h=MH)
            dve.wait_ge(sem("tr_src"), 3 * NT)
            ch.step(dve.tensor_tensor(tmp_tok[:], xn_tok[:], xn_tok[:], ALU.mult))
            dve.reduce_sum(ssq, heads(tmp_tok), axis=AX.X).then_inc(sem("b_arguments"), 1)
            dve.wait_ge(sem("b_functions"), 4 + MH)
            ch.step(dve.tensor_scalar_max(rinvB, rinvB, 1e-12))
            ch.step(dve.reciprocal(rinvB, rinvB))
            dve.tensor_tensor(heads(tmp_tok), heads(xn_tok), bcast(rinvB, 2, (NT * MH, MD)), ALU.mult)\
               .then_inc(sem("tr_src"), NT)
            dve.wait_ge(sem("tr_ps"), 7)
            ch.add(dve.tensor_copy(rkT[:, 0], bank(4)))
            dve.tensor_copy(wkT[:, 0, :, 1:S], bank(4).rearrange("p (b s) -> p b s", b=B)[:, :, 0:S - 1])\
               .then_inc(sem("tr_sb"), 1)
            tiles = lambda ap: bcast(ap, 1, (NT, P))
            for h in range(MH):
                dve.wait_ge(sem("b_gram"), h + 1)
                gram = PS[:, h, :].rearrange("p (t c) -> p t c", t=NT)
                ch.add(dve.tensor_tensor(MT[:, h], gram, tiles(decayed[:, h, :]), ALU.mult))
                ch.step(dve.tensor_tensor(T[:, h], gram, tiles(low0g[:, h, :]), ALU.mult))
                ch.add(dve.tensor_tensor(T[:, h], tiles(C("ident")), T[:, h], ALU.subtract))
                ch.step(dve.tensor_tensor(TT[:, h], MT[:, h], tiles(C("up0")), ALU.mult))
                ch.add(dve.tensor_tensor(TT[:, h], tiles(C("ident")), TT[:, h], ALU.subtract))
                dve.tensor_tensor(CT[:, h], MT[:, h], tiles(C("up1")), ALU.mult).then_inc(sem("b_ct"), 1)
            for k in range(1, LEVELS):
                for h in range(MH):
                    dve.wait_ge(sem("b_tx"), 4 * (k - 1) + h + 1)
                    new_tt = PS[:, h, :].rearrange("p (t c) -> p t c", t=NT)
                    new_t = PS[:, 4 + h, :].rearrange("p (t c) -> p t c", t=NT)
                    if k == LEVELS - 1:
                        dve.tensor_tensor(TT[:, h], TT[:, h], new_tt, ALU.subtract).then_inc(sem("b_inv"), 1)
                        continue
                    ch.add(dve.tensor_tensor(TT[:, h], TT[:, h], new_tt, ALU.subtract))
                    ch.add(dve.tensor_tensor(T[:, h], T[:, h], new_t, ALU.subtract))
                    dve.tensor_tensor(CT[:, h], MT[:, h], tiles(C(f"up{k + 1}")), ALU.mult)\
                       .then_inc(sem("b_ct"), 1)
            for h in range(MH):
                dve.wait_ge(sem("b_copied"), 3 + h)
                dve.tensor_tensor(IT[:, h], IT[:, h], tiles(decayed[:, h, :]), ALU.mult).then_inc(sem("b_inv"), 1)
            dve.wait_ge(sem("b_functions"), 3)
            for i in range(2):
                dve.wait_ge(sem("b_o"), i + 1)
                dve.tensor_tensor(pair(tmp_tok, i).rearrange("p t (h d) -> p t h d", h=MH),
                                  PS[:, 6 + i, :].rearrange("p (t h d) -> p t h d", t=2, h=MH),
                                  bcast(bcast(small[:, 52:56], 1, (2, MH)), 3, (2, MH, MD)), ALU.mult)\
                   .then_inc(sem("tr_src"), 2)
            tr_dve(dve, 5, aT)
            ch.step(dve.tensor_tensor(x_tok[:], x_tok[:], xn_tok[:], ALU.add))
            for i in range(2):
                dve.wait_ge(sem("b_out"), i + 1)
                ch.step(dve.tensor_tensor(two(x_tok, i), bank(2 + i), two(x_tok, i), ALU.add))
                ln_stats(dve, ch, x_tok, (2 * i, 2 * i + 1))
            ch.sync()
            dve.sem_inc(sem("x_tok"), 1)

            ln_dve(dve, ch, 5, x_tok, xn_tok, sem("tr_src"))
            def weights(i, s):
                dve.wait_ge(sem("c_wh"), i * 16 + s + 1)
                dve.tensor_tensor(w_l[:, s % 4, :], stage[s // 8 % 2][:, s % 8, :], wide(w_h[:, s % 4, :]),
                                  ALU.subtract).then_inc(sem("c_wl"), 1)

            def experts(i, last_two=False):
                for s in range(16):
                    dve.wait_ge(sem("c_sg"), i * 16 + s + 1)
                    dve.wait_ge(sem("c_u"), i * 16 + s + 1)
                    dve.tensor_tensor(hm[:, s % 2, :], bank(2 + s % 2), sg[:, s % 2, :], ALU.mult)\
                       .then_inc(sem("c_hd"), 1)
                    if not (last_two and s >= 14):
                        weights(i, s + 2)
                    dve.wait_ge(sem("c_hh"), i * 16 + s + 1)
                    dve.tensor_tensor(h_l[:, s % 4, :], hm[:, s % 2, :], wide(h_h[:, s % 4, :]), ALU.subtract)\
                       .then_inc(sem("c_hl"), 1)

            weights(0, 0)
            weights(0, 1)
            split_dve(dve, 1)
            with dve.Fori(0, NEXP // 2 - 1) as i:
                experts(i)
            experts(NEXP // 2 - 1, last_two=True)
            dve.wait_ge(sem("c_done"), 1)
            for t in range(NT):
                ch.add(dve.tensor_tensor(x_tok[:, t, :], PS[:, 4 + t, 0:D], x_tok[:, t, :], ALU.add))
            ch.sync()
            dve.sem_inc(sem("x_tok"), 1)

            ln_stats(dve, ch, x_tok, range(NT))
            ln_dve(dve, ch, 6, x_tok, xn_tok, sem("tr_src"))
            tr_dve(dve, 7, xnT)
            dve.wait_ge(sem("d_qz0"), 1)
            def queries(c):
                dve.wait_ge(sem("d_q"), c + 1)
                dve.wait_ge(sem("d_qa"), c + 1)
                dve.tensor_scalar_mul(qz1[64:128, c % 2, 1, :], PS[64:128, c % 2, :], XD ** -0.5)\
                   .then_inc(sem("d_qd"), 1)

            queries(0)
            for c in range(FC):
                if c + 1 < FC:
                    queries(c + 1)
                for h2 in range(2):
                    dve.wait_ge(sem("d_u0"), 2 * c + h2 + 1)
                    dve.tensor_copy(U[:, 0, 2 * c + h2, :], bank(2 + 2 * h2)).then_inc(sem("d_ue0"), 1)

            def grouped(b):
                settle(dve)
                dve.tensor_copy(Ub[:, 1].rearrange("p g (h i) -> p g h i", i=GI),
                                U[:, 1, :, bass.ds(b * S, S)].rearrange("p h (g i) -> p g h i", i=GI))\
                   .then_inc(sem("d_ub1"), 1)

            def scores(b):
                for hf in range(2):
                    dve.wait_ge(sem("d_sim"), b * 2 + hf + 4)
                    dve.wait_ge(sem("d_t"), b * 2 + hf + 1)
                    settle(dve)
                    for g in range(4):
                        last = dve.tensor_tensor_reduce(out=Z[:, hf, g, :], in0=PS[:, hf, g * P:(g + 1) * P],
                                                        in1=C("group"), scale=-1.0, scalar=3e38, op0=ALU.add,
                                                        op1=ALU.min, accum_out=mx1[:, hf, g:g + 1])
                    last.then_inc(sem("d_z"), 1)

            def probabilities(b):
                for hf in range(2):
                    dve.wait_ge(sem("d_e"), b * 2 + hf + 1)
                    ch.step(dve.reciprocal(ri1[:, hf, :], rs1[:, hf, :]))
                    dve.tensor_tensor(Z[:, hf], Z[:, hf], bcast(ri1[:, hf, :], 2, (4, P)), ALU.mult)\
                       .then_inc(sem("d_p"), 1)

            def summed(b):
                for hf in range(2):
                    dve.wait_ge(sem("d_w"), b * 4 + hf * 2 + 6)
                    settle(dve)
                    dve.tensor_copy(U[:, 0, :, bass.ds(b * S + hf * 32, 32)].rearrange("p h (g i) -> p g h i", g=4),
                                    PS[:, 4 + 2 * hf, :].rearrange("p (g h i) -> p g h i", g=4, h=XH))\
                       .then_inc(sem("d_we0"), 1)

            dve.wait_ge(sem("d_ue1"), 2 * FC)
            grouped(0)
            scores(0)
            grouped(1)
            probabilities(0)
            with dve.Fori(1, B - 1) as b:
                ch.enter(b - 1, 2)
                scores(b)
                grouped(b + 1)
                probabilities(b)
                summed(b - 1)
                ch.leave(B - 2)
            scores(B - 1)
            probabilities(B - 1)
            summed(B - 2)
            summed(B - 1)
            ch.step(dve.tensor_tensor(pair(x_tok, 0), pair(x_tok, 0), vec(V_BOUT), ALU.add))
            ch.step(dve.tensor_tensor(pair(x_tok, 1), pair(x_tok, 1), vec(V_BOUT), ALU.add))
            for i in range(2):
                dve.wait_ge(sem("d_out"), i + 1)
                ch.step(dve.tensor_tensor(two(x_tok, i), bank(2 + i), two(x_tok, i), ALU.add))
                ln_stats(dve, ch, x_tok, (2 * i, 2 * i + 1))
            ch.sync()
            dve.sem_inc(sem("x_tok"), 1)

            ln_dve(dve, ch, 7, x_tok, xn_tok, sem("tr_src"))
            tr_dve(dve, 8, xnT)
            ln_stats(dve, ch, xn_tok, range(NT))
            ln_dve(dve, ch, 8, xn_tok, y_tok).then_inc(sem("e_y"), 1)
            dve.wait_ge(sem("e_qk"), 3)
            dve.tensor_tensor(kTz[:, 0], bcast(bank(4), 1, (8, TOK)), bcast(C("head8"), 2, (8, TOK)),
                              ALU.mult).then_inc(sem("e_ksb"), 1)
            dve.wait_ge(sem("e_set"), 1)
            for i in range(2):
                dve.wait_ge(sem("e_v"), i + 1)
                dve.tensor_copy(ve[:, 2 * i:2 * i + 2, :, 0:DK],
                                bank(6 + i).rearrange("p (t h d) -> p t h d", t=2, h=H)).then_inc(sem("e_qsb"), 1)

            def scores(n):
                t, hs = n // 2, slice(8 * (n % 2), 8 * (n % 2) + 8)
                s3 = PS[:, n, :].rearrange("p (h k) -> p h k", h=8)
                dve.wait_ge(sem("e_s"), n + 1)
                ch.step(dve.reduce_max(mxe[:, t, hs], s3, axis=AX.X))
                dve.tensor_tensor(Ze[:, t, hs, :], s3, bcast(mxe[:, t, hs], 2, (8, S)), ALU.subtract)\
                   .then_inc(sem("e_z"), 1)

            def turned(t):
                for g in (1, 3):
                    dve.wait_ge(sem("e_t"), 4 * t + g + 1)
                    dve.tensor_copy(PzT[:, t % 2, 4 * g:4 * g + 4, :].rearrange("p a b -> p (a b)"), bank(g))\
                       .then_inc(sem("e_te1"), 1)

            def output(t):
                dve.wait_ge(sem("e_o"), t + 1)
                o = PS[:, 4 + t, 0:H * (DK + 1)].rearrange("p (h d) -> p h d", h=H)
                ch.step(dve.reciprocal(rie[:, t, :], o[:, :, DK]))
                dve.tensor_tensor(tmp_tok[:, t, :].rearrange("p (h d) -> p h d", h=H), o[:, :, 0:DK],
                                  bcast(rie[:, t, :], 2, (H, DK)), ALU.mult).then_inc(sem("tr_src"), 1)

            for n in range(6):
                scores(n)
            turned(0)
            scores(6)
            scores(7)
            turned(1)
            turned(2)
            output(0)
            turned(3)
            output(1)
            output(2)
            output(3)
            tr_dve(dve, 9, aT)
            dve.wait_ge(sem("e_yown"), 8)
            for i in range(2):
                dve.wait_ge(sem("e_out"), i + 1)
                ch.step(dve.tensor_tensor(two(x_tok, i), bank(2 + i), two(x_tok, i), ALU.add))
                ln_stats(dve, ch, x_tok, (2 * i, 2 * i + 1))
            ch.sync()
            dve.sem_inc(sem("x_tok"), 1)

            ln_dve(dve, ch, 9, x_tok, xn_tok, sem("tr_src"))
            tr_dve(dve, 10, xnT)
            dve.wait_ge(sem("f_log"), 1)
            router_b = bcast(vecs[:, V_RBR, 0:NEXP], 1, (NT, NEXP))
            ch.step(dve.tensor_tensor(logit, PS[:, 2, 0:NT * NEXP].rearrange("p (t e) -> p t e", t=NT), router_b,
                                      ALU.add))
            ch.step(dve.reduce_max(top, logit, axis=AX.X))
            ch.step(dve.tensor_tensor(eq8, logit, bcast(top, 2, (NT, NEXP)), ALU.is_equal))
            ch.step(dve.tensor_tensor(eq8, eq8, bcast(C("first"), 1, (NT, NEXP)), ALU.mult))
            ch.step(dve.reduce_max(top, eq8, axis=AX.X))
            dve.tensor_tensor(oh8, eq8, bcast(top, 2, (NT, NEXP)), ALU.is_equal).then_inc(sem("f_oh8"), 1)
            dve.wait_ge(sem("f_xnh"), 1)
            dve.tensor_tensor(xn_l[:], xn_tok[:], wide(xn_h[:]), ALU.subtract).then_inc(sem("f_xnl"), 1)
            dve.wait_ge(sem("f_count"), 1)
            ch.step(dve.tensor_tensor(over, bcast(PS[:, 4, NT * NEXP:(NT + 1) * NEXP], 2, (NEXP, NT)),
                                      bcast(C("full"), 1, (NEXP, NT)), ALU.is_gt))
            ch.step(dve.reduce_sum(blocks8, over, axis=AX.X))
            square = lambda ap: ap.rearrange("p (a b) -> p a b", a=NEXP)
            ch.add(dve.tensor_tensor(ends3, bcast(blocks8, 1, (NEXP, NEXP)), square(C("upto")), ALU.mult))
            ch.step(dve.tensor_tensor(starts3, bcast(blocks8, 1, (NEXP, NEXP)), square(C("before")), ALU.mult))
            ch.add(dve.reduce_sum(ends, ends3, axis=AX.X))
            ch.step(dve.reduce_sum(starts, starts3, axis=AX.X))
            ch.step(dve.tensor_tensor(ended, bcast(ends, 1, (NB, NEXP)), bcast(C("block"), 2, (NB, NEXP)), ALU.is_le))
            ch.step(dve.reduce_sum(owner, ended, axis=AX.X))
            ch.step(dve.tensor_scalar(owner, owner, float(NEXP - 1), float(P), ALU.min, ALU.mult))
            ch.step(dve.tensor_scalar(owner_row, owner, C("row")[:, 0:1], None, ALU.add))
            dve.tensor_copy(rows[:], owner_row).then_inc(sem("f_rows"), 1)
            ch.step(dve.tensor_tensor(place3, PS[:, 4, 0:NT * NEXP].rearrange("p (t e) -> p t e", t=NT),
                                      bcast(starts, 1, (NT, NEXP)), ALU.add))
            ch.step(dve.tensor_tensor(place3, place3, oh8, ALU.mult))
            ch.step(dve.reduce_sum(place, place3, axis=AX.X))
            ch.step(dve.tensor_tensor(rel_place, bcast(place, 1, (NB, NT)), bcast(C("block"), 2, (NB, NT)),
                                      ALU.subtract))

            def picks(k, j):
                dve.tensor_tensor(pick[:, j], bcast(C("column"), 1, (NT, P)),
                                  bcast(rel_place[:, bass.ds(k, 1), :].rearrange("p a t -> p (a t)"), 2, (NT, P)),
                                  ALU.is_equal).then_inc(sem("f_pick"), 1)

            def picksT(k, j):
                dve.tensor_tensor(pickT[:, j, :], placeT, C("slot")[:, bass.ds(k, 1)].to_broadcast([P, TOK]),
                                  ALU.is_equal).then_inc(sem("f_pickT"), 1)

            def result(k):
                dve.wait_ge(sem("f_yh"), k + 1)
                dve.tensor_tensor(yb_l[:], PS[:, 5, 0:D], wide(yb_h[:]), ALU.subtract).then_inc(sem("f_yl"), 1)

            def step(i, j, first=False, last_steps=False):
                k = i * 3 + j
                if not first:
                    result(k - 1)
                dve.wait_ge(sem(f"f_w{j}"), i * 16 + 16)
                dve.wait_ge(sem("f_upd"), k + 1)
                for c in range(4):
                    dve.tensor_scalar(hb[:, 4 + c, :], PS[:, 2, c * P:(c + 1) * P], bf1[j][:, 4 + c:5 + c], 0.0,
                                      ALU.add, ALU.max).then_inc(sem("f_hd"), 1)
                if not last_steps:
                    picks(k + 2, (j + 2) % 3)
                picksT(k, j)

            picks(0, 0)
            dve.tensor_tensor(placed, bcast(C("ident"), 1, (NT, P)), bcast(place, 2, (NT, P)), ALU.mult)\
               .then_inc(sem("f_placed"), 1)
            picks(1, 1)
            dve.wait_ge(sem("f_placeT"), 1)
            step(0, 0, first=True)
            step(0, 1)
            step(0, 2)
            with dve.Fori(1, NB // 3) as i:
                for j in range(3):
                    step(i, j)
            step(NB // 3, 0, last_steps=True)
            step(NB // 3, 1, last_steps=True)
            result(NB - 1)
            dve.wait_ge(sem("f_done"), 1)
            for i in range(2):
                ch.add(dve.tensor_tensor(two(x_tok, i), bank(6 + i), two(x_tok, i), ALU.add))
            ch.sync()
            dve.sem_inc(sem("x_tok"), 1)


def kernel(**inputs):
    import concourse.bacc as bacc
    from concourse.bass_utils import run_bass_kernel_spmd as run

    a = {k: np.asarray(v) for k, v in inputs.items()}
    t = lambda k: np.ascontiguousarray(a[k].T)
    ctx = a["ctx_1024"]
    cols = np.concatenate([
        a["L0_xattn_g1"].reshape(KC, P).T, a["L0_xattn_be1"].reshape(KC, P).T,
        a["L0_xattn_b1"].reshape(FC, P).T,
        np.broadcast_to(a["L0_attn_decay"], (P, MH)), np.broadcast_to(a["L0_attn_log_alpha"], (P, MH))], 1)
    vecs = np.zeros((NVEC, D), np.float32)
    for i, k in enumerate(["L0_xattn_b2", "L0_xattn_g2", "L0_xattn_be2", "L1_xattn_bout", "L1_attn_b_proj",
                           "L1_attn_ln_gamma", "L1_attn_ln_beta"]):
        vecs[i] = a[k]
    vecs[V_RBR, :NEXP] = a["L1_ffn_br"]
    arrays = {
        "x": a["x"].reshape(TOK, D), "bias": a["fside_Bx16xSxS2_0"], "consts": CONST,
        "ctxT": ctx.transpose(0, 2, 1),
        "ctxG": ctx.reshape(B, GM, GRP, GI, D).transpose(0, 1, 3, 2, 4).reshape(B, P, GRP, D),
        "wq0": t("L0_xattn_Wq"), "wk0": t("L0_xattn_Wk"), "wv0": t("L0_xattn_Wv"), "wo0": t("L0_xattn_Wo"),
        "w1_0": t("L0_xattn_W1"), "w2_0": t("L0_xattn_W2"), "ww": t("L0_attn_Ww"), "wr": t("L0_attn_Wr"),
        "wall": np.concatenate(
            [a[k].reshape(NEXP, KC, P, FC, P).transpose(0, 2, 3, 1, 4).reshape(NEXP, P, FC, KC * P)
             for k in ("L0_ffn_Wg", "L0_ffn_Wu")]
            + [a["L0_ffn_Wd"].reshape(NEXP, FC, P, D).transpose(0, 2, 1, 3)], 3),
        "wq1": a["L1_xattn_Wq"], "wkT1": a["L1_xattn_Wkv"][:, :XH * XD].T, "wv1": a["L1_xattn_Wkv"][:, XH * XD:],
        "wo1": a["L1_xattn_Wout"], "wqkv": t("L1_attn_W_qkv"), "wproj": t("L1_attn_W_proj"),
        "wrt": t("L1_ffn_Wr"), "b2f": a["L1_ffn_b2"],
        "wf": np.concatenate(
            [a["L1_ffn_W1"].reshape(NEXP, FF, KC, P).transpose(0, 3, 2, 1).reshape(NEXP * P, KC * FF),
             a["L1_ffn_W2"].reshape(NEXP, D, FC, P).transpose(0, 3, 2, 1).reshape(NEXP * P, FC * D),
             a["L1_ffn_b1"].reshape(NEXP, FC, P).transpose(0, 2, 1).reshape(NEXP * P, FC)], 1),
        "cols": cols, "vecs": vecs,
    }
    nc = bacc.Bacc("TRN2", target_bir_lowering=False, num_devices=1)
    A, sent = {}, {}
    for k, v in arrays.items():
        v = np.ascontiguousarray(v)
        sent[f"in_{k}"] = v
        A[k] = nc.dram_tensor(f"in_{k}", v.shape, mybir.dt.from_np(v.dtype), kind="ExternalInput").ap()
    out = nc.dram_tensor("out", (TOK, D), F32, kind="ExternalOutput").ap()
    perceiver(nc, A, out)
    r = run(nc, [sent], core_ids=[0])
    return r.results[0]["out"].reshape(B, S, D)
```
